# Optimizing a Trainium2 kernel written in Bass

```python
import numpy as np
import jax
import jax.numpy as jnp

def _softmax(x, axis=-1):
    return jax.nn.softmax(x, axis=axis)

def _gelu(x):
    return jax.nn.gelu(x, approximate=True)

def _silu(x):
    return jax.nn.silu(x)

def _sigmoid(x):
    return jax.nn.sigmoid(x)

def _layernorm(x, axis=-1, eps=1e-05):
    m = jnp.mean(x, axis=axis, keepdims=True)
    v = jnp.var(x, axis=axis, keepdims=True)
    return (x - m) / jnp.sqrt(v + eps)

def _scatter_add(tgt, idx, src, axis=0):
    return tgt.at[idx].add(src)

def _segment_sum(src, seg, n):
    return jax.ops.segment_sum(src, seg, n)
kernel_name = 'mk_decoder_preln_d4_seqx_r8_cc23e3'

def setup_inputs(seed: int=0):
    np.random.seed(seed)
    _w = jnp.asarray

    def _rec_inputs():
        import jax
        import jax.numpy as jnp
        _rk = jax.random.key(seed)
        x = -0.000125 + 0.9999 * jax.random.normal(jax.random.fold_in(_rk, 1), (16, 100, 128), jnp.float32)
        _lenS = 100 - jax.random.randint(jax.random.fold_in(_rk, 7), (16,), 0, max(1, 100 // 4) + 1, jnp.int32)
        _lenS2 = 1444 - jax.random.randint(jax.random.fold_in(_rk, 8), (16,), 0, max(1, 1444 // 4) + 1, jnp.int32)
        _ctx_768P = jax.random.normal(jax.random.fold_in(_rk, 11), (16, 16, 96), jnp.float32)
        _ctx_768c = jax.random.dirichlet(jax.random.fold_in(_rk, 511), 0.3 * jnp.ones((16,), jnp.float32), (16, 1444))
        _ctx_768t = jnp.einsum('bsk,bkd->bsd', _ctx_768c, _ctx_768P)
        _ctx_768t = _ctx_768t * jax.lax.rsqrt(jnp.mean(jnp.square(_ctx_768t)) + 1e-12) * 0.953939
        ctx_768 = 0.00272024 + 0.999456 * (_ctx_768t + 0.3 * jax.random.normal(jax.random.fold_in(_rk, 611), (16, 1444, 96), jnp.float32))
        _validS = jnp.arange(100)[None, :] < _lenS[:, None]
        _validS2 = jnp.arange(1444)[None, :] < _lenS2[:, None]
        _causal = jnp.tril(jnp.ones((100, 100), dtype=bool))
        mask_BxS_bf1 = jnp.ones((16, 100), dtype=bool)
        mask_BxS2_bf1 = jnp.ones((16, 1444), dtype=bool)
        return (x, ctx_768, mask_BxS_bf1, mask_BxS2_bf1)
    x, ctx_768, mask_BxS_bf1, mask_BxS2_bf1 = _rec_inputs()

    def _L0_attn_setup():
        import jax, jax.numpy as jnp
        import numpy as np
        H = 128
        NH = 16
        HD = H // NH
        B, S = (2, 256)
        key = jax.random.key(seed)
        ks = jax.random.split(key, 6)
        std = 0.02
        x = jax.random.normal(ks[0], (B, S, H), dtype=jnp.float32)
        w_qkv = jax.random.normal(ks[1], (3 * H, H), dtype=jnp.float32) * std
        b_qkv = jnp.zeros((3 * H,), dtype=jnp.float32)
        ln_g = jnp.ones((H,), dtype=jnp.float32)
        ln_b = jnp.zeros((H,), dtype=jnp.float32)
        w_ent = jax.random.normal(ks[2], (1, H), dtype=jnp.float32) * std
        b_ent = jnp.zeros((1,), dtype=jnp.float32)
        w_out = jax.random.normal(ks[3], (H, H), dtype=jnp.float32) * std
        b_out = jnp.zeros((H,), dtype=jnp.float32)
        return {'x': x, 'ln_g': ln_g, 'ln_b': ln_b, 'w_qkv': w_qkv, 'b_qkv': b_qkv, 'w_ent': w_ent, 'b_ent': b_ent, 'w_out': w_out, 'b_out': b_out}
    _L0_attn_all = _L0_attn_setup()
    _L0_attn_in = {k: v for k, v in _L0_attn_all.items() if k in ('ln_g', 'ln_b', 'w_qkv', 'b_qkv', 'w_ent', 'b_ent', 'w_out', 'b_out')}
    del _L0_attn_all

    def _L0_xattn_setup():
        import jax, jax.numpy as jnp
        import numpy as np
        HEADS = 16
        DIM_HEAD = 64
        SCALE = DIM_HEAD ** (-0.5)
        QUERY_DIM = 128
        CONTEXT_DIM = 96
        INNER_DIM = HEADS * DIM_HEAD
        key = jax.random.key(seed)
        ks = jax.random.split(key, 7)
        B, Nq, Nk = (8, 512, 77)
        x = jax.random.normal(ks[0], (B, Nq, QUERY_DIM), dtype=jnp.float32)
        context = jax.random.normal(ks[1], (B, Nk, CONTEXT_DIM), dtype=jnp.float32)
        Wq = jax.random.normal(ks[2], (QUERY_DIM, INNER_DIM), dtype=jnp.float32) * QUERY_DIM ** (-0.5)
        Wk = jax.random.normal(ks[3], (CONTEXT_DIM, INNER_DIM), dtype=jnp.float32) * CONTEXT_DIM ** (-0.5)
        Wv = jax.random.normal(ks[4], (CONTEXT_DIM, INNER_DIM), dtype=jnp.float32) * CONTEXT_DIM ** (-0.5)
        Wo = jax.random.normal(ks[5], (INNER_DIM, QUERY_DIM), dtype=jnp.float32) * INNER_DIM ** (-0.5)
        bo = jnp.zeros((QUERY_DIM,), dtype=jnp.float32)
        return {'x': x, 'context': context, 'Wq': Wq, 'Wk': Wk, 'Wv': Wv, 'Wo': Wo, 'bo': bo}
    _L0_xattn_all = _L0_xattn_setup()
    _L0_xattn_in = {k: v for k, v in _L0_xattn_all.items() if k in ('Wq', 'Wk', 'Wv', 'Wo', 'bo')}
    del _L0_xattn_all

    def _L0_ffn_setup():
        import jax, jax.numpy as jnp
        import numpy as np
        HIDDEN = 128
        FFN = 512
        NUM_EXPERTS = 8
        TOP_K = 2
        BATCH, SEQ = (2, 256)
        key = jax.random.key(seed)
        ks = jax.random.split(key, 6)
        s_h = 1.0 / np.sqrt(HIDDEN)
        s_f = 1.0 / np.sqrt(FFN)
        return {'hidden_states': jax.random.normal(ks[0], (BATCH, SEQ, HIDDEN), jnp.float32), 'gate_w': jax.random.uniform(ks[1], (HIDDEN, NUM_EXPERTS), jnp.float32, -s_h, s_h), 'gate_b': jax.random.uniform(ks[2], (NUM_EXPERTS,), jnp.float32, -s_h, s_h), 'w1': jax.random.uniform(ks[3], (NUM_EXPERTS, HIDDEN, FFN), jnp.float32, -s_h, s_h), 'w3': jax.random.uniform(ks[4], (NUM_EXPERTS, HIDDEN, FFN), jnp.float32, -s_h, s_h), 'w2': jax.random.uniform(ks[5], (NUM_EXPERTS, FFN, HIDDEN), jnp.float32, -s_f, s_f)}
    _L0_ffn_all = _L0_ffn_setup()
    _L0_ffn_in = {k: v for k, v in _L0_ffn_all.items() if k in ('gate_w', 'gate_b', 'w1', 'w3', 'w2')}
    del _L0_ffn_all

    def _L1_attn_setup():
        import math
        import jax, jax.numpy as jnp
        import numpy as np
        N_HEAD = 16

        def quant_weight(w):
            scale = jnp.maximum(jnp.mean(jnp.abs(w)), 1e-08)
            w_quant = jnp.clip(jnp.round(w / scale), -2.0, 2.0)
            return jax.lax.stop_gradient(w_quant * scale - w) + w
        key = jax.random.key(seed)
        k1, k2, k3 = jax.random.split(key, 3)
        C = 128
        x = jax.random.normal(k1, (2, 256, C), dtype=jnp.float32)
        w_attn = jax.random.normal(k2, (3 * C, C), dtype=jnp.float32) * (1.0 / math.sqrt(C))
        w_proj = jax.random.normal(k3, (C, C), dtype=jnp.float32) * (1.0 / math.sqrt(C))
        return {'x': x, 'w_attn': w_attn, 'w_proj': w_proj}
    _L1_attn_all = _L1_attn_setup()
    _L1_attn_in = {k: v for k, v in _L1_attn_all.items() if k in ('w_attn', 'w_proj')}
    del _L1_attn_all

    def _L1_xattn_setup():
        import jax, jax.numpy as jnp
        import numpy as np
        Q_DIM, K_DIM, V_DIM, OUT_DIM = (128, 96, 96, 128)
        key = jax.random.key(seed)
        ks = jax.random.split(key, 9)
        s = lambda d: 1.0 / np.sqrt(d)
        return {'query': jax.random.normal(ks[0], (16, 256, Q_DIM), jnp.float32), 'key': jax.random.normal(ks[1], (16, 256, K_DIM), jnp.float32), 'value': jax.random.normal(ks[2], (16, 256, V_DIM), jnp.float32), 'Wq': jax.random.uniform(ks[3], (OUT_DIM, Q_DIM), jnp.float32, -s(Q_DIM), s(Q_DIM)), 'bq': jax.random.uniform(ks[4], (OUT_DIM,), jnp.float32, -s(Q_DIM), s(Q_DIM)), 'Wk': jax.random.uniform(ks[5], (OUT_DIM, K_DIM), jnp.float32, -s(K_DIM), s(K_DIM)), 'bk': jax.random.uniform(ks[6], (OUT_DIM,), jnp.float32, -s(K_DIM), s(K_DIM)), 'Wv': jax.random.uniform(ks[7], (OUT_DIM, V_DIM), jnp.float32, -s(V_DIM), s(V_DIM)), 'bv': jax.random.uniform(ks[8], (OUT_DIM,), jnp.float32, -s(V_DIM), s(V_DIM))}
    _L1_xattn_all = _L1_xattn_setup()
    _L1_xattn_in = {k: v for k, v in _L1_xattn_all.items() if k in ('Wq', 'bq', 'Wk', 'bk', 'Wv', 'bv')}
    del _L1_xattn_all

    def _L1_ffn_setup():
        import jax, jax.numpy as jnp
        import numpy as np
        B, S, D = (4, 256, 128)
        DFF = 64
        E = 16
        TOP_K = 2
        N_SHARED = 2
        FUSED_DFF = DFF * N_SHARED
        key = jax.random.key(seed)
        ks = jax.random.split(key, 16)
        sc_d = 1.0 / np.sqrt(D)
        sc_f = 1.0 / np.sqrt(DFF)
        sc_sf = 1.0 / np.sqrt(FUSED_DFF)
        inp = {'x': jax.random.normal(ks[0], (B, S, D), dtype=jnp.float32), 'gate_w': jax.random.uniform(ks[1], (E, D), dtype=jnp.float32, minval=-sc_d, maxval=sc_d), 'expert_bias': jnp.zeros((E,), dtype=jnp.float32), 'w1': jax.random.uniform(ks[2], (E, DFF, D), dtype=jnp.float32, minval=-sc_d, maxval=sc_d), 'b1': jax.random.uniform(ks[3], (E, DFF), dtype=jnp.float32, minval=-sc_d, maxval=sc_d), 'w3': jax.random.uniform(ks[4], (E, DFF, D), dtype=jnp.float32, minval=-sc_d, maxval=sc_d), 'b3': jax.random.uniform(ks[5], (E, DFF), dtype=jnp.float32, minval=-sc_d, maxval=sc_d), 'w2': jax.random.uniform(ks[6], (E, D, DFF), dtype=jnp.float32, minval=-sc_f, maxval=sc_f), 'b2': jax.random.uniform(ks[7], (E, D), dtype=jnp.float32, minval=-sc_f, maxval=sc_f), 'sw1': jax.random.uniform(ks[8], (FUSED_DFF, D), dtype=jnp.float32, minval=-sc_d, maxval=sc_d), 'sb1': jax.random.uniform(ks[9], (FUSED_DFF,), dtype=jnp.float32, minval=-sc_d, maxval=sc_d), 'sw3': jax.random.uniform(ks[10], (FUSED_DFF, D), dtype=jnp.float32, minval=-sc_d, maxval=sc_d), 'sb3': jax.random.uniform(ks[11], (FUSED_DFF,), dtype=jnp.float32, minval=-sc_d, maxval=sc_d), 'sw2': jax.random.uniform(ks[12], (D, FUSED_DFF), dtype=jnp.float32, minval=-sc_sf, maxval=sc_sf), 'sb2': jax.random.uniform(ks[13], (D,), dtype=jnp.float32, minval=-sc_sf, maxval=sc_sf)}
        return inp
    _L1_ffn_all = _L1_ffn_setup()
    _L1_ffn_in = {k: v for k, v in _L1_ffn_all.items() if k in ('gate_w', 'expert_bias', 'w1', 'b1', 'w2', 'b2', 'w3', 'b3', 'sw1', 'sb1', 'sw2', 'sb2', 'sw3', 'sb3')}
    del _L1_ffn_all

    def _L2_attn_setup():
        import jax, jax.numpy as jnp
        import numpy as np
        import math
        N_EMBD = 128
        N_HEAD = 16
        HEAD = N_EMBD // N_HEAD
        LAYER_IDX = 2
        LAMBDA_INIT = 0.8 - 0.6 * math.exp(-0.3 * (LAYER_IDX - 1))
        BN_EPS = 1e-05
        RMS_EPS = 1e-05

        def _heads(y, B, T, d):
            return y.reshape(B, T, N_HEAD, d).transpose(0, 2, 1, 3)
        key = jax.random.key(seed)
        ks = jax.random.split(key, 16)
        B, T = (4, 128)
        s = 1.0 / math.sqrt(N_EMBD)
        return {'x': jax.random.normal(ks[0], (B, T, N_EMBD), jnp.float32), 'q1_w': jax.random.normal(ks[1], (N_EMBD, N_EMBD), jnp.float32) * s, 'q2_w': jax.random.normal(ks[2], (N_EMBD, N_EMBD), jnp.float32) * s, 'k1_w': jax.random.normal(ks[3], (N_EMBD, N_EMBD), jnp.float32) * s, 'k2_w': jax.random.normal(ks[4], (N_EMBD, N_EMBD), jnp.float32) * s, 'v_w': jax.random.normal(ks[5], (2 * N_EMBD, N_EMBD), jnp.float32) * s, 'c_w': jax.random.normal(ks[6], (N_EMBD, 2 * N_EMBD), jnp.float32) * s, 'subln_w': jnp.ones((2 * HEAD,), jnp.float32), 'lq1': jax.random.normal(ks[7], (HEAD,), jnp.float32) * 0.1, 'lk1': jax.random.normal(ks[8], (HEAD,), jnp.float32) * 0.1, 'lq2': jax.random.normal(ks[9], (HEAD,), jnp.float32) * 0.1, 'lk2': jax.random.normal(ks[10], (HEAD,), jnp.float32) * 0.1, 'bn_gamma': jnp.ones((N_EMBD,), jnp.float32), 'bn_beta': jnp.zeros((N_EMBD,), jnp.float32)}
    _L2_attn_all = _L2_attn_setup()
    _L2_attn_in = {k: v for k, v in _L2_attn_all.items() if k in ('q1_w', 'q2_w', 'k1_w', 'k2_w', 'v_w', 'c_w', 'subln_w', 'lq1', 'lk1', 'lq2', 'lk2', 'bn_gamma', 'bn_beta')}
    del _L2_attn_all

    def _L2_xattn_setup():
        import jax, jax.numpy as jnp
        import numpy as np
        N_HEADS = 16
        DIM_EMBED = 128
        DIM_CROSS = 96
        DIM_HEAD = DIM_EMBED // N_HEADS
        key = jax.random.key(seed)
        ks = jax.random.split(key, 10)
        B, Sq, Sk = (8, 512, 77)
        s_e = 1.0 / np.sqrt(DIM_EMBED)
        s_c = 1.0 / np.sqrt(DIM_CROSS)
        return {'x': jax.random.normal(ks[0], (B, Sq, DIM_EMBED), jnp.float32), 'y': jax.random.normal(ks[1], (B, Sk, DIM_CROSS), jnp.float32), 'wq': jax.random.normal(ks[2], (DIM_EMBED, DIM_EMBED), jnp.float32) * s_e, 'bq': jax.random.normal(ks[3], (DIM_EMBED,), jnp.float32) * 0.01, 'wk': jax.random.normal(ks[4], (DIM_CROSS, DIM_EMBED), jnp.float32) * s_c, 'bk': jax.random.normal(ks[5], (DIM_EMBED,), jnp.float32) * 0.01, 'wv': jax.random.normal(ks[6], (DIM_CROSS, DIM_EMBED), jnp.float32) * s_c, 'bv': jax.random.normal(ks[7], (DIM_EMBED,), jnp.float32) * 0.01, 'wo': jax.random.normal(ks[8], (DIM_EMBED, DIM_EMBED), jnp.float32) * s_e, 'bo': jax.random.normal(ks[9], (DIM_EMBED,), jnp.float32) * 0.01}
    _L2_xattn_all = _L2_xattn_setup()
    _L2_xattn_in = {k: v for k, v in _L2_xattn_all.items() if k in ('wq', 'bq', 'wk', 'bk', 'wv', 'bv', 'wo', 'bo')}
    del _L2_xattn_all

    def _L2_ffn_setup():
        import jax, jax.numpy as jnp
        import numpy as np
        B, S, D, F, E = (2, 256, 128, 512, 8)
        LN_EPS = 1e-05

        def _xavier(key, shape, fan_in, fan_out):
            a = np.sqrt(6.0 / (fan_in + fan_out))
            return jax.random.uniform(key, shape, jnp.float32, -a, a)
        key = jax.random.key(seed)
        ks = jax.random.split(key, 8)
        tgt = jax.random.normal(ks[0], (B, S, D), jnp.float32)
        router_w = _xavier(ks[1], (E, D), D, E)
        router_b = jnp.zeros((E,), jnp.float32)
        w1 = _xavier(ks[2], (E, D, F), D, F)
        b1 = jnp.zeros((E, F), jnp.float32)
        w2 = _xavier(ks[3], (E, F, D), F, D)
        b2 = jnp.zeros((E, D), jnp.float32)
        gamma = jnp.ones((D,), jnp.float32)
        beta = jnp.zeros((D,), jnp.float32)
        return {'tgt': tgt, 'router_w': router_w, 'router_b': router_b, 'w1': w1, 'b1': b1, 'w2': w2, 'b2': b2, 'gamma': gamma, 'beta': beta}
    _L2_ffn_all = _L2_ffn_setup()
    _L2_ffn_in = {k: v for k, v in _L2_ffn_all.items() if k in ('router_w', 'router_b', 'w1', 'b1', 'w2', 'b2', 'gamma', 'beta')}
    del _L2_ffn_all

    def _L3_attn_setup():
        import jax, jax.numpy as jnp
        import numpy as np
        D_MODEL = 128
        NHEAD = 16
        D_K = D_MODEL // NHEAD
        SCALE = 1.0 / np.sqrt(D_K * 2.0)
        TEMP = 1.5
        EPS = 1e-08

        def _l2norm(t):
            n = jnp.sqrt(jnp.sum(t * t, axis=-1, keepdims=True))
            return t / jnp.maximum(n, EPS)
        key = jax.random.key(seed)
        ks = jax.random.split(key, 9)
        B, T = (2, 256)
        x = jax.random.normal(ks[0], (B, T, D_MODEL), dtype=jnp.float32)

        def w(k):
            return 0.02 * jax.random.normal(k, (D_MODEL, D_MODEL), dtype=jnp.float32)
        return {'x': x, 'Wq': w(ks[1]), 'bq': jnp.zeros((D_MODEL,), jnp.float32), 'Wk': w(ks[2]), 'bk': jnp.zeros((D_MODEL,), jnp.float32), 'Wv': w(ks[3]), 'bv': jnp.zeros((D_MODEL,), jnp.float32), 'Wo': w(ks[4]), 'bo': jnp.zeros((D_MODEL,), jnp.float32)}
    _L3_attn_all = _L3_attn_setup()
    _L3_attn_in = {k: v for k, v in _L3_attn_all.items() if k in ('Wq', 'bq', 'Wk', 'bk', 'Wv', 'bv', 'Wo', 'bo')}
    del _L3_attn_all

    def _L3_xattn_setup():
        import jax, jax.numpy as jnp
        import numpy as np
        B, T, DT, G, DV = (16, 64, 128, 72, 96)
        H, DH = (4, 32)
        INNER = H * DH
        HID = 4 * DT
        N_STATE = 64
        K_TOP = 32

        def layernorm(x, g, b, eps=1e-05):
            m = x.mean(-1, keepdims=True)
            v = x.var(-1, keepdims=True)
            return (x - m) * jax.lax.rsqrt(v + eps) * g + b

        def s4d(x, log_dt, A_re, A_im, C_re, C_im, D_skip):
            Bb, L, D = x.shape
            dt = jnp.exp(log_dt)
            A = A_re + 1j * A_im
            C = C_re + 1j * C_im
            dtA = dt[:, None] * A
            dC = C * (jnp.exp(dtA) - 1.0) / A
            powers = jnp.exp(dtA[:, :, None] * jnp.arange(L))
            K = 2.0 * jnp.einsum('dn,dnl->dl', dC, powers).real
            n = 2 * L
            Kf = jnp.fft.rfft(K, n=n, axis=-1)
            xf = jnp.fft.rfft(x, n=n, axis=1)
            y = jnp.fft.irfft(xf * Kf.T[None], n=n, axis=1)[:, :L]
            return y + x * D_skip
        key = jax.random.key(seed)
        ks = jax.random.split(key, 16)
        s = 0.02
        inp = {'x_text': jax.random.normal(ks[0], (B, T, DT), jnp.float32), 'x_vision': jax.random.normal(ks[1], (B, G, DV), jnp.float32), 'text_mask': jnp.ones((B, T), bool), 'vision_mask': jnp.ones((B, G), bool), 'Wq': jax.random.normal(ks[2], (DT, INNER), jnp.float32) * s, 'Wk': jax.random.normal(ks[3], (DV, INNER), jnp.float32) * s, 'Wv': jax.random.normal(ks[4], (DV, DT), jnp.float32) * s, 'W_film_in': jax.random.normal(ks[5], (DT, 2 * DT), jnp.float32) * s, 'b_film_in': jnp.zeros((2 * DT,), jnp.float32), 'W_film_out': jax.random.normal(ks[6], (DT, 2 * DT), jnp.float32) * s, 'b_film_out': jnp.zeros((2 * DT,), jnp.float32), 'g_norm_in': jnp.ones((DT,), jnp.float32), 'b_norm_in': jnp.zeros((DT,), jnp.float32), 'g_norm_out': jnp.ones((DT,), jnp.float32), 'b_norm_out': jnp.zeros((DT,), jnp.float32), 'g_ffn': jnp.ones((DT,), jnp.float32), 'b_ffn': jnp.zeros((DT,), jnp.float32), 'W1': jax.random.normal(ks[7], (DT, HID), jnp.float32) * s, 'b1': jnp.zeros((HID,), jnp.float32), 'W2': jax.random.normal(ks[8], (HID, DT), jnp.float32) * s, 'b2': jnp.zeros((DT,), jnp.float32), 'log_dt': jnp.log(0.001) + jax.random.uniform(ks[9], (DT,), jnp.float32) * (jnp.log(0.1) - jnp.log(0.001)), 'A_re': -0.5 * jnp.ones((DT, N_STATE), jnp.float32), 'A_im': jnp.tile(jnp.pi * jnp.arange(N_STATE, dtype=jnp.float32), (DT, 1)), 'C_re': jax.random.normal(ks[10], (DT, N_STATE), jnp.float32) * 0.5 ** 0.5, 'C_im': jax.random.normal(ks[11], (DT, N_STATE), jnp.float32) * 0.5 ** 0.5, 'D_skip': jax.random.normal(ks[12], (DT,), jnp.float32), 'mod_gate': jnp.array(0.5, jnp.float32)}
        return inp
    _L3_xattn_all = _L3_xattn_setup()
    _L3_xattn_in = {k: v for k, v in _L3_xattn_all.items() if k in ('Wq', 'Wk', 'Wv', 'W_film_in', 'b_film_in', 'W_film_out', 'b_film_out', 'g_norm_in', 'b_norm_in', 'g_norm_out', 'b_norm_out', 'g_ffn', 'b_ffn', 'W1', 'b1', 'W2', 'b2', 'log_dt', 'A_re', 'A_im', 'C_re', 'C_im', 'D_skip', 'mod_gate')}
    del _L3_xattn_all

    def _L3_ffn_setup():
        import jax, jax.numpy as jnp
        import numpy as np
        NUM_EXPERTS = 8
        TOP_K = 2
        DIM = 128
        HIDDEN = 512
        B, S = (4, 256)
        key = jax.random.key(seed)
        ks = jax.random.split(key, 6)
        scale = 0.02
        x = jax.random.normal(ks[0], (B, S, DIM), dtype=jnp.float32)
        wg = jax.random.normal(ks[1], (NUM_EXPERTS, DIM), dtype=jnp.float32) * scale
        bg = jnp.zeros((NUM_EXPERTS,), dtype=jnp.float32)
        Wgate = jax.random.normal(ks[2], (NUM_EXPERTS, HIDDEN, DIM), dtype=jnp.float32) * scale
        Wup = jax.random.normal(ks[3], (NUM_EXPERTS, HIDDEN, DIM), dtype=jnp.float32) * scale
        Wdown = jax.random.normal(ks[4], (NUM_EXPERTS, DIM, HIDDEN), dtype=jnp.float32) * scale
        return {'x': x, 'wg': wg, 'bg': bg, 'Wgate': Wgate, 'Wup': Wup, 'Wdown': Wdown}
    _L3_ffn_all = _L3_ffn_setup()
    _L3_ffn_in = {k: v for k, v in _L3_ffn_all.items() if k in ('wg', 'bg', 'Wgate', 'Wup', 'Wdown')}
    del _L3_ffn_all
    return {'x': x, 'ctx_768': ctx_768, 'mask_BxS_bf1': mask_BxS_bf1, 'mask_BxS2_bf1': mask_BxS2_bf1, 'L0_attn_ln_g': _L0_attn_in['ln_g'], 'L0_attn_ln_b': _L0_attn_in['ln_b'], 'L0_attn_w_qkv': _L0_attn_in['w_qkv'], 'L0_attn_b_qkv': _L0_attn_in['b_qkv'], 'L0_attn_w_ent': _L0_attn_in['w_ent'], 'L0_attn_b_ent': _L0_attn_in['b_ent'], 'L0_attn_w_out': _L0_attn_in['w_out'], 'L0_attn_b_out': _L0_attn_in['b_out'], 'L0_xattn_Wq': _L0_xattn_in['Wq'], 'L0_xattn_Wk': _L0_xattn_in['Wk'], 'L0_xattn_Wv': _L0_xattn_in['Wv'], 'L0_xattn_Wo': _L0_xattn_in['Wo'], 'L0_xattn_bo': _L0_xattn_in['bo'], 'L0_ffn_gate_w': _L0_ffn_in['gate_w'], 'L0_ffn_gate_b': _L0_ffn_in['gate_b'], 'L0_ffn_w1': _L0_ffn_in['w1'], 'L0_ffn_w3': _L0_ffn_in['w3'], 'L0_ffn_w2': _L0_ffn_in['w2'], 'L1_attn_w_attn': _L1_attn_in['w_attn'], 'L1_attn_w_proj': _L1_attn_in['w_proj'], 'L1_xattn_Wq': _L1_xattn_in['Wq'], 'L1_xattn_bq': _L1_xattn_in['bq'], 'L1_xattn_Wk': _L1_xattn_in['Wk'], 'L1_xattn_bk': _L1_xattn_in['bk'], 'L1_xattn_Wv': _L1_xattn_in['Wv'], 'L1_xattn_bv': _L1_xattn_in['bv'], 'L1_ffn_gate_w': _L1_ffn_in['gate_w'], 'L1_ffn_expert_bias': _L1_ffn_in['expert_bias'], 'L1_ffn_w1': _L1_ffn_in['w1'], 'L1_ffn_b1': _L1_ffn_in['b1'], 'L1_ffn_w2': _L1_ffn_in['w2'], 'L1_ffn_b2': _L1_ffn_in['b2'], 'L1_ffn_w3': _L1_ffn_in['w3'], 'L1_ffn_b3': _L1_ffn_in['b3'], 'L1_ffn_sw1': _L1_ffn_in['sw1'], 'L1_ffn_sb1': _L1_ffn_in['sb1'], 'L1_ffn_sw2': _L1_ffn_in['sw2'], 'L1_ffn_sb2': _L1_ffn_in['sb2'], 'L1_ffn_sw3': _L1_ffn_in['sw3'], 'L1_ffn_sb3': _L1_ffn_in['sb3'], 'L2_attn_q1_w': _L2_attn_in['q1_w'], 'L2_attn_q2_w': _L2_attn_in['q2_w'], 'L2_attn_k1_w': _L2_attn_in['k1_w'], 'L2_attn_k2_w': _L2_attn_in['k2_w'], 'L2_attn_v_w': _L2_attn_in['v_w'], 'L2_attn_c_w': _L2_attn_in['c_w'], 'L2_attn_subln_w': _L2_attn_in['subln_w'], 'L2_attn_lq1': _L2_attn_in['lq1'], 'L2_attn_lk1': _L2_attn_in['lk1'], 'L2_attn_lq2': _L2_attn_in['lq2'], 'L2_attn_lk2': _L2_attn_in['lk2'], 'L2_attn_bn_gamma': _L2_attn_in['bn_gamma'], 'L2_attn_bn_beta': _L2_attn_in['bn_beta'], 'L2_xattn_wq': _L2_xattn_in['wq'], 'L2_xattn_bq': _L2_xattn_in['bq'], 'L2_xattn_wk': _L2_xattn_in['wk'], 'L2_xattn_bk': _L2_xattn_in['bk'], 'L2_xattn_wv': _L2_xattn_in['wv'], 'L2_xattn_bv': _L2_xattn_in['bv'], 'L2_xattn_wo': _L2_xattn_in['wo'], 'L2_xattn_bo': _L2_xattn_in['bo'], 'L2_ffn_router_w': _L2_ffn_in['router_w'], 'L2_ffn_router_b': _L2_ffn_in['router_b'], 'L2_ffn_w1': _L2_ffn_in['w1'], 'L2_ffn_b1': _L2_ffn_in['b1'], 'L2_ffn_w2': _L2_ffn_in['w2'], 'L2_ffn_b2': _L2_ffn_in['b2'], 'L2_ffn_gamma': _L2_ffn_in['gamma'], 'L2_ffn_beta': _L2_ffn_in['beta'], 'L3_attn_Wq': _L3_attn_in['Wq'], 'L3_attn_bq': _L3_attn_in['bq'], 'L3_attn_Wk': _L3_attn_in['Wk'], 'L3_attn_bk': _L3_attn_in['bk'], 'L3_attn_Wv': _L3_attn_in['Wv'], 'L3_attn_bv': _L3_attn_in['bv'], 'L3_attn_Wo': _L3_attn_in['Wo'], 'L3_attn_bo': _L3_attn_in['bo'], 'L3_xattn_Wq': _L3_xattn_in['Wq'], 'L3_xattn_Wk': _L3_xattn_in['Wk'], 'L3_xattn_Wv': _L3_xattn_in['Wv'], 'L3_xattn_W_film_in': _L3_xattn_in['W_film_in'], 'L3_xattn_b_film_in': _L3_xattn_in['b_film_in'], 'L3_xattn_W_film_out': _L3_xattn_in['W_film_out'], 'L3_xattn_b_film_out': _L3_xattn_in['b_film_out'], 'L3_xattn_g_norm_in': _L3_xattn_in['g_norm_in'], 'L3_xattn_b_norm_in': _L3_xattn_in['b_norm_in'], 'L3_xattn_g_norm_out': _L3_xattn_in['g_norm_out'], 'L3_xattn_b_norm_out': _L3_xattn_in['b_norm_out'], 'L3_xattn_g_ffn': _L3_xattn_in['g_ffn'], 'L3_xattn_b_ffn': _L3_xattn_in['b_ffn'], 'L3_xattn_W1': _L3_xattn_in['W1'], 'L3_xattn_b1': _L3_xattn_in['b1'], 'L3_xattn_W2': _L3_xattn_in['W2'], 'L3_xattn_b2': _L3_xattn_in['b2'], 'L3_xattn_log_dt': _L3_xattn_in['log_dt'], 'L3_xattn_A_re': _L3_xattn_in['A_re'], 'L3_xattn_A_im': _L3_xattn_in['A_im'], 'L3_xattn_C_re': _L3_xattn_in['C_re'], 'L3_xattn_C_im': _L3_xattn_in['C_im'], 'L3_xattn_D_skip': _L3_xattn_in['D_skip'], 'L3_xattn_mod_gate': _L3_xattn_in['mod_gate'], 'L3_ffn_wg': _L3_ffn_in['wg'], 'L3_ffn_bg': _L3_ffn_in['bg'], 'L3_ffn_Wgate': _L3_ffn_in['Wgate'], 'L3_ffn_Wup': _L3_ffn_in['Wup'], 'L3_ffn_Wdown': _L3_ffn_in['Wdown']}

def reference(x, ctx_768, mask_BxS_bf1, mask_BxS2_bf1, L0_attn_ln_g, L0_attn_ln_b, L0_attn_w_qkv, L0_attn_b_qkv, L0_attn_w_ent, L0_attn_b_ent, L0_attn_w_out, L0_attn_b_out, L0_xattn_Wq, L0_xattn_Wk, L0_xattn_Wv, L0_xattn_Wo, L0_xattn_bo, L0_ffn_gate_w, L0_ffn_gate_b, L0_ffn_w1, L0_ffn_w3, L0_ffn_w2, L1_attn_w_attn, L1_attn_w_proj, L1_xattn_Wq, L1_xattn_bq, L1_xattn_Wk, L1_xattn_bk, L1_xattn_Wv, L1_xattn_bv, L1_ffn_gate_w, L1_ffn_expert_bias, L1_ffn_w1, L1_ffn_b1, L1_ffn_w2, L1_ffn_b2, L1_ffn_w3, L1_ffn_b3, L1_ffn_sw1, L1_ffn_sb1, L1_ffn_sw2, L1_ffn_sb2, L1_ffn_sw3, L1_ffn_sb3, L2_attn_q1_w, L2_attn_q2_w, L2_attn_k1_w, L2_attn_k2_w, L2_attn_v_w, L2_attn_c_w, L2_attn_subln_w, L2_attn_lq1, L2_attn_lk1, L2_attn_lq2, L2_attn_lk2, L2_attn_bn_gamma, L2_attn_bn_beta, L2_xattn_wq, L2_xattn_bq, L2_xattn_wk, L2_xattn_bk, L2_xattn_wv, L2_xattn_bv, L2_xattn_wo, L2_xattn_bo, L2_ffn_router_w, L2_ffn_router_b, L2_ffn_w1, L2_ffn_b1, L2_ffn_w2, L2_ffn_b2, L2_ffn_gamma, L2_ffn_beta, L3_attn_Wq, L3_attn_bq, L3_attn_Wk, L3_attn_bk, L3_attn_Wv, L3_attn_bv, L3_attn_Wo, L3_attn_bo, L3_xattn_Wq, L3_xattn_Wk, L3_xattn_Wv, L3_xattn_W_film_in, L3_xattn_b_film_in, L3_xattn_W_film_out, L3_xattn_b_film_out, L3_xattn_g_norm_in, L3_xattn_b_norm_in, L3_xattn_g_norm_out, L3_xattn_b_norm_out, L3_xattn_g_ffn, L3_xattn_b_ffn, L3_xattn_W1, L3_xattn_b1, L3_xattn_W2, L3_xattn_b2, L3_xattn_log_dt, L3_xattn_A_re, L3_xattn_A_im, L3_xattn_C_re, L3_xattn_C_im, L3_xattn_D_skip, L3_xattn_mod_gate, L3_ffn_wg, L3_ffn_bg, L3_ffn_Wgate, L3_ffn_Wup, L3_ffn_Wdown):
    import jax
    import jax.numpy as jnp

    def _L0_attn_ref(x, ln_g, ln_b, w_qkv, b_qkv, w_ent, b_ent, w_out, b_out):
        import jax, jax.numpy as jnp
        import numpy as np
        H = 128
        NH = 16
        HD = H // NH
        B, S = (2, 256)
        b, s, h = x.shape
        scale = 1.0 / jnp.sqrt(jnp.float32(HD))
        TEMP = 0.1
        mu = jnp.mean(x, axis=-1, keepdims=True)
        var = jnp.mean(jnp.square(x - mu), axis=-1, keepdims=True)
        xn = (x - mu) / jnp.sqrt(var + 1e-06) * ln_g + ln_b
        qkv = xn @ w_qkv.T + b_qkv
        qkv = qkv.reshape(b, s, 3, NH, HD).transpose(2, 0, 3, 1, 4)
        q, k, v = (qkv[0], qkv[1], qkv[2])
        scores = jnp.einsum('bhqd,bhkd->bhqk', q, k) * scale
        causal = jnp.tril(jnp.ones((s, s), dtype=bool))
        scores = jnp.where(causal[None, None], scores, -jnp.inf)
        probs = jax.nn.softmax(scores / TEMP, axis=-1)
        gate = jax.nn.sigmoid(xn @ w_ent.T + b_ent)
        gate = jnp.clip(gate, 0.1, 2.0)[:, None, None, :, 0]
        probs = probs * gate
        out = jnp.einsum('bhqk,bhkd->bhqd', probs, v)
        out = out.transpose(0, 2, 1, 3).reshape(b, s, h)
        return (out @ w_out.T + b_out) * 0.1

    def _L0_xattn_ref(x, context, Wq, Wk, Wv, Wo, bo):
        import jax, jax.numpy as jnp
        import numpy as np
        HEADS = 16
        DIM_HEAD = 64
        SCALE = DIM_HEAD ** (-0.5)
        QUERY_DIM = 128
        CONTEXT_DIM = 96
        INNER_DIM = HEADS * DIM_HEAD
        B, Nq, _ = x.shape
        Nk = context.shape[1]
        q = x @ Wq
        k = context @ Wk
        v = context @ Wv
        q = q.reshape(B, Nq, HEADS, DIM_HEAD).transpose(0, 2, 1, 3)
        k = k.reshape(B, Nk, HEADS, DIM_HEAD).transpose(0, 2, 1, 3)
        v = v.reshape(B, Nk, HEADS, DIM_HEAD).transpose(0, 2, 1, 3)
        sim = jnp.einsum('bhid,bhjd->bhij', q, k) * SCALE
        attn = jax.nn.softmax(sim, axis=-1)
        out = jnp.einsum('bhij,bhjd->bhid', attn, v)
        out = out.transpose(0, 2, 1, 3).reshape(B, Nq, INNER_DIM)
        return out @ Wo + bo

    def _L0_ffn_ref(hidden_states, gate_w, gate_b, w1, w3, w2):
        import jax, jax.numpy as jnp
        import numpy as np
        HIDDEN = 128
        FFN = 512
        NUM_EXPERTS = 8
        TOP_K = 2
        BATCH, SEQ = (2, 256)
        B, S, D = hidden_states.shape
        T = B * S
        x = hidden_states.reshape(T, D)
        logits = x @ gate_w + gate_b
        probs = jax.nn.softmax(logits.astype(jnp.float32), axis=-1)
        top_w, top_idx = jax.lax.top_k(probs, TOP_K)
        top_w = top_w / jnp.sum(top_w, axis=-1, keepdims=True)
        combine = jnp.zeros((T, NUM_EXPERTS), jnp.float32)
        combine = combine.at[jnp.arange(T)[:, None], top_idx].set(top_w)
        combine = combine.astype(x.dtype)
        h = jax.nn.silu(jnp.einsum('td,edf->tef', x, w1)) * jnp.einsum('td,edf->tef', x, w3)
        out_e = jnp.einsum('tef,efd->ted', h, w2)
        out = jnp.einsum('ted,te->td', out_e, combine)
        return out.reshape(B, S, D)

    def _L1_attn_ref(x, w_attn, w_proj):
        import math
        import jax, jax.numpy as jnp
        import numpy as np
        N_HEAD = 16

        def quant_weight(w):
            scale = jnp.maximum(jnp.mean(jnp.abs(w)), 1e-08)
            w_quant = jnp.clip(jnp.round(w / scale), -2.0, 2.0)
            return jax.lax.stop_gradient(w_quant * scale - w) + w
        B, T, C = x.shape
        H = N_HEAD
        D = C // H
        qkv = jnp.einsum('btc,oc->bto', x, quant_weight(w_attn))
        q, k, v = jnp.split(qkv, 3, axis=-1)
        q = q.reshape(B, T, H, D).transpose(0, 2, 1, 3)
        k = k.reshape(B, T, H, D).transpose(0, 2, 1, 3)
        v = v.reshape(B, T, H, D).transpose(0, 2, 1, 3)
        att = jnp.einsum('bhqd,bhkd->bhqk', q, k) * (1.0 / math.sqrt(D))
        causal = jnp.tril(jnp.ones((T, T), dtype=bool))
        att = jnp.where(causal, att, jnp.finfo(att.dtype).min)
        att = jax.nn.softmax(att, axis=-1)
        y = jnp.einsum('bhqk,bhkd->bhqd', att, v)
        y = y.transpose(0, 2, 1, 3).reshape(B, T, C)
        return jnp.einsum('btc,oc->bto', y, quant_weight(w_proj))

    def _L1_xattn_ref(query, key, value, Wq, bq, Wk, bk, Wv, bv):
        import jax, jax.numpy as jnp
        import numpy as np
        Q_DIM, K_DIM, V_DIM, OUT_DIM = (128, 96, 96, 128)
        scale = OUT_DIM ** (-0.5)
        q = jnp.einsum('bsd,od->bso', query, Wq) + bq
        k = jnp.einsum('bsd,od->bso', key, Wk) + bk
        v = jnp.einsum('bsd,od->bso', value, Wv) + bv
        scores = jnp.einsum('bqo,bko->bqk', q, k) * scale
        probs = jax.nn.softmax(scores, axis=-1)
        return jnp.einsum('bqk,bko->bqo', probs, v)

    def _L1_ffn_ref(x, gate_w, expert_bias, w1, b1, w2, b2, w3, b3, sw1, sb1, sw2, sb2, sw3, sb3):
        import jax, jax.numpy as jnp
        import numpy as np
        B, S, D = (4, 256, 128)
        DFF = 64
        E = 16
        TOP_K = 2
        N_SHARED = 2
        FUSED_DFF = DFF * N_SHARED
        Bv, Sv, Dv = x.shape
        xf = x.reshape(-1, Dv)
        logits = xf @ gate_w.T
        scores = jax.nn.sigmoid(logits)
        biased = logits + expert_bias.astype(logits.dtype)[None, :]
        _, topk_idx = jax.lax.top_k(biased, TOP_K)
        topk_w = jnp.take_along_axis(scores, topk_idx, axis=-1)
        topk_w = topk_w / (topk_w.sum(-1, keepdims=True) + 1e-10)
        gatew = (jax.nn.one_hot(topk_idx, E, dtype=xf.dtype) * topk_w[..., None]).sum(1)
        y = jnp.zeros_like(xf)
        for e in range(E):
            h = jax.nn.silu(xf @ w1[e].T + b1[e]) * (xf @ w3[e].T + b3[e])
            y = y + gatew[:, e:e + 1] * (h @ w2[e].T + b2[e])
        hs = jax.nn.silu(xf @ sw1.T + sb1) * (xf @ sw3.T + sb3)
        y = y + hs @ sw2.T + sb2
        return y.reshape(Bv, Sv, Dv)

    def _L2_attn_ref(x, q1_w, q2_w, k1_w, k2_w, v_w, c_w, subln_w, lq1, lk1, lq2, lk2, bn_gamma, bn_beta):
        import jax, jax.numpy as jnp
        import numpy as np
        import math
        N_EMBD = 128
        N_HEAD = 16
        HEAD = N_EMBD // N_HEAD
        LAYER_IDX = 2
        LAMBDA_INIT = 0.8 - 0.6 * math.exp(-0.3 * (LAYER_IDX - 1))
        BN_EPS = 1e-05
        RMS_EPS = 1e-05

        def _heads(y, B, T, d):
            return y.reshape(B, T, N_HEAD, d).transpose(0, 2, 1, 3)
        B, T, C = x.shape
        mean = jnp.mean(x, axis=(0, 1))
        var = jnp.var(x, axis=(0, 1))
        xn = (x - mean) * jax.lax.rsqrt(var + BN_EPS) * bn_gamma + bn_beta
        q1 = _heads(xn @ q1_w.T, B, T, HEAD)
        q2 = _heads(xn @ q2_w.T, B, T, HEAD)
        k1 = _heads(xn @ k1_w.T, B, T, HEAD)
        k2 = _heads(xn @ k2_w.T, B, T, HEAD)
        v = _heads(xn @ v_w.T, B, T, 2 * HEAD)
        scale = 1.0 / math.sqrt(HEAD)
        att1 = jax.nn.softmax(jnp.einsum('bhtd,bhsd->bhts', q1, k1) * scale, axis=-1)
        att2 = jax.nn.softmax(jnp.einsum('bhtd,bhsd->bhts', q2, k2) * scale, axis=-1)
        lam = jnp.exp(jnp.sum(lq1 * lk1)) - jnp.exp(jnp.sum(lq2 * lk2)) + LAMBDA_INIT
        att = att1 - lam * att2
        y = jnp.einsum('bhts,bhse->bhte', att, v)
        y = y * jax.lax.rsqrt(jnp.mean(y * y, axis=-1, keepdims=True) + RMS_EPS) * subln_w
        y = y * (1.0 - LAMBDA_INIT)
        y = y.transpose(0, 2, 1, 3).reshape(B, T, 2 * C)
        return y @ c_w.T

    def _L2_xattn_ref(x, y, wq, bq, wk, bk, wv, bv, wo, bo):
        import jax, jax.numpy as jnp
        import numpy as np
        N_HEADS = 16
        DIM_EMBED = 128
        DIM_CROSS = 96
        DIM_HEAD = DIM_EMBED // N_HEADS
        B, Sq, E = x.shape
        H, D = (N_HEADS, DIM_HEAD)
        q = (x @ wq + bq).reshape(B, Sq, H, D).transpose(0, 2, 1, 3)
        k = (y @ wk + bk).reshape(B, -1, H, D).transpose(0, 2, 1, 3)
        v = (y @ wv + bv).reshape(B, -1, H, D).transpose(0, 2, 1, 3)
        scores = jnp.einsum('bhqd,bhkd->bhqk', q, k) / jnp.sqrt(jnp.asarray(D, x.dtype))
        attn = jax.nn.softmax(scores, axis=-1)
        out = jnp.einsum('bhqk,bhkd->bhqd', attn, v)
        out = out.transpose(0, 2, 1, 3).reshape(B, Sq, E)
        return out @ wo + bo

    def _L2_ffn_ref(tgt, router_w, router_b, w1, b1, w2, b2, gamma, beta):
        import jax, jax.numpy as jnp
        import numpy as np
        B, S, D, F, E = (2, 256, 128, 512, 8)
        LN_EPS = 1e-05

        def _xavier(key, shape, fan_in, fan_out):
            a = np.sqrt(6.0 / (fan_in + fan_out))
            return jax.random.uniform(key, shape, jnp.float32, -a, a)
        logits = jnp.einsum('bsd,ed->bse', tgt, router_w) + router_b
        rw = jax.nn.softmax(logits, axis=-1)
        rw = jnp.zeros_like(rw).at[..., 0].set(1.0)
        h = jax.nn.relu(jnp.einsum('bsd,edf->besf', tgt, w1) + b1[None, :, None, :])
        eo = jnp.einsum('besf,efd->besd', h, w2) + b2[None, :, None, :]
        tgt2 = jnp.einsum('besd,bse->bsd', eo, rw)
        x = tgt + tgt2
        mean = jnp.mean(x, axis=-1, keepdims=True)
        var = jnp.mean(jnp.square(x - mean), axis=-1, keepdims=True)
        return (x - mean) * jax.lax.rsqrt(var + LN_EPS) * gamma + beta

    def _L3_attn_ref(x, Wq, bq, Wk, bk, Wv, bv, Wo, bo):
        import jax, jax.numpy as jnp
        import numpy as np
        D_MODEL = 128
        NHEAD = 16
        D_K = D_MODEL // NHEAD
        SCALE = 1.0 / np.sqrt(D_K * 2.0)
        TEMP = 1.5
        EPS = 1e-08

        def _l2norm(t):
            n = jnp.sqrt(jnp.sum(t * t, axis=-1, keepdims=True))
            return t / jnp.maximum(n, EPS)
        B, T, D = x.shape

        def heads(W, b):
            y = x @ W.T + b
            return y.reshape(B, T, NHEAD, D_K).transpose(0, 2, 1, 3)
        q = _l2norm(heads(Wq, bq))
        k = _l2norm(heads(Wk, bk))
        v = heads(Wv, bv)
        scores = jnp.einsum('bhqd,bhkd->bhqk', q, k) * SCALE
        scores = jnp.clip(scores, -5.0, 5.0)
        causal = jnp.triu(jnp.ones((T, T), dtype=bool), k=1)
        scores = jnp.where(causal[None, None], -10000.0, scores)
        attn = jax.nn.softmax(scores / TEMP, axis=-1)
        out = jnp.einsum('bhqk,bhkd->bhqd', attn, v)
        out = out.transpose(0, 2, 1, 3).reshape(B, T, D)
        return (out @ Wo.T + bo) * 0.5

    def _L3_xattn_ref(x_text, x_vision, text_mask, vision_mask, Wq, Wk, Wv, W_film_in, b_film_in, W_film_out, b_film_out, g_norm_in, b_norm_in, g_norm_out, b_norm_out, g_ffn, b_ffn, W1, b1, W2, b2, log_dt, A_re, A_im, C_re, C_im, D_skip, mod_gate):
        import jax, jax.numpy as jnp
        import numpy as np
        B, T, DT, G, DV = (16, 64, 128, 72, 96)
        H, DH = (4, 32)
        INNER = H * DH
        HID = 4 * DT
        N_STATE = 64
        K_TOP = 32

        def layernorm(x, g, b, eps=1e-05):
            m = x.mean(-1, keepdims=True)
            v = x.var(-1, keepdims=True)
            return (x - m) * jax.lax.rsqrt(v + eps) * g + b

        def s4d(x, log_dt, A_re, A_im, C_re, C_im, D_skip):
            Bb, L, D = x.shape
            dt = jnp.exp(log_dt)
            A = A_re + 1j * A_im
            C = C_re + 1j * C_im
            dtA = dt[:, None] * A
            dC = C * (jnp.exp(dtA) - 1.0) / A
            powers = jnp.exp(dtA[:, :, None] * jnp.arange(L))
            K = 2.0 * jnp.einsum('dn,dnl->dl', dC, powers).real
            n = 2 * L
            Kf = jnp.fft.rfft(K, n=n, axis=-1)
            xf = jnp.fft.rfft(x, n=n, axis=1)
            y = jnp.fft.irfft(xf * Kf.T[None], n=n, axis=1)[:, :L]
            return y + x * D_skip
        Bb, Tt, D = x_text.shape
        Gg = x_vision.shape[1]
        Q = (x_text @ Wq).reshape(Bb, Tt, H, DH)
        K = (x_vision @ Wk).reshape(Bb, Gg, H, DH)
        scores = jnp.einsum('bthd,bghd->bhtg', Q, K) / np.sqrt(DH).astype(np.float32)
        scores = jnp.where(vision_mask[:, None, None, :], scores, -jnp.inf)
        topv, topi = jax.lax.top_k(scores, K_TOP)
        probs = jax.nn.softmax(topv, axis=-1)
        bi = jnp.arange(Bb)[:, None, None, None]
        hi = jnp.arange(H)[None, :, None, None]
        ti = jnp.arange(Tt)[None, None, :, None]
        attn = jnp.zeros_like(scores).at[bi, hi, ti, topi].set(probs)
        attn_mean = attn.mean(axis=1)
        V = x_vision @ Wv
        c_t = jnp.einsum('btg,bgd->btd', attn_mean, V)
        c_t = c_t * text_mask[..., None]
        x = layernorm(x_text, g_norm_in, b_norm_in)
        scale_in, shift_in = jnp.split(c_t @ W_film_in + b_film_in, 2, axis=-1)
        x = x * (1.0 + mod_gate * scale_in) + mod_gate * shift_in
        y = s4d(x, log_dt, A_re, A_im, C_re, C_im, D_skip)
        scale_out, shift_out = jnp.split(c_t @ W_film_out + b_film_out, 2, axis=-1)
        y = y * (1.0 + mod_gate * scale_out) + mod_gate * shift_out
        xt = x_text + y
        h = layernorm(xt, g_ffn, b_ffn)
        h = jax.nn.gelu(h @ W1 + b1, approximate=False) @ W2 + b2
        xt = xt + h
        return layernorm(xt, g_norm_out, b_norm_out)

    def _L3_ffn_ref(x, wg, bg, Wgate, Wup, Wdown):
        import jax, jax.numpy as jnp
        import numpy as np
        NUM_EXPERTS = 8
        TOP_K = 2
        DIM = 128
        HIDDEN = 512
        B, S = (4, 256)
        b, s, d = x.shape
        xf = x.reshape(-1, d)
        T = xf.shape[0]
        logits = xf @ wg.T + bg
        vals, idx = jax.lax.top_k(logits, TOP_K)
        masked = jnp.full_like(logits, -jnp.inf)
        rows = jnp.arange(T)[:, None]
        masked = masked.at[rows, idx].set(vals)
        weights = jax.nn.softmax(masked, axis=-1)
        out = jnp.zeros_like(xf)
        for e in range(NUM_EXPERTS):
            g = xf @ Wgate[e].T
            u = xf @ Wup[e].T
            h = g * jax.nn.sigmoid(g) * u
            out = out + h @ Wdown[e].T * weights[:, e:e + 1]
        return out.reshape(b, s, d)
    x = x + _L0_attn_ref(_layernorm(x, axis=-1), L0_attn_ln_g, L0_attn_ln_b, L0_attn_w_qkv, L0_attn_b_qkv, L0_attn_w_ent, L0_attn_b_ent, L0_attn_w_out, L0_attn_b_out)
    x = x + _L0_xattn_ref(_layernorm(x, axis=-1), ctx_768, L0_xattn_Wq, L0_xattn_Wk, L0_xattn_Wv, L0_xattn_Wo, L0_xattn_bo)
    x = x + _L0_ffn_ref(_layernorm(x, axis=-1), L0_ffn_gate_w, L0_ffn_gate_b, L0_ffn_w1, L0_ffn_w3, L0_ffn_w2)
    x = x + _L1_attn_ref(_layernorm(x, axis=-1), L1_attn_w_attn, L1_attn_w_proj)
    x = x + _L1_xattn_ref(_layernorm(x, axis=-1), ctx_768, ctx_768, L1_xattn_Wq, L1_xattn_bq, L1_xattn_Wk, L1_xattn_bk, L1_xattn_Wv, L1_xattn_bv)
    x = x + _L1_ffn_ref(_layernorm(x, axis=-1), L1_ffn_gate_w, L1_ffn_expert_bias, L1_ffn_w1, L1_ffn_b1, L1_ffn_w2, L1_ffn_b2, L1_ffn_w3, L1_ffn_b3, L1_ffn_sw1, L1_ffn_sb1, L1_ffn_sw2, L1_ffn_sb2, L1_ffn_sw3, L1_ffn_sb3)
    x = x + _L2_attn_ref(_layernorm(x, axis=-1), L2_attn_q1_w, L2_attn_q2_w, L2_attn_k1_w, L2_attn_k2_w, L2_attn_v_w, L2_attn_c_w, L2_attn_subln_w, L2_attn_lq1, L2_attn_lk1, L2_attn_lq2, L2_attn_lk2, L2_attn_bn_gamma, L2_attn_bn_beta)
    x = x + _L2_xattn_ref(_layernorm(x, axis=-1), ctx_768, L2_xattn_wq, L2_xattn_bq, L2_xattn_wk, L2_xattn_bk, L2_xattn_wv, L2_xattn_bv, L2_xattn_wo, L2_xattn_bo)
    x = x + _L2_ffn_ref(_layernorm(x, axis=-1), L2_ffn_router_w, L2_ffn_router_b, L2_ffn_w1, L2_ffn_b1, L2_ffn_w2, L2_ffn_b2, L2_ffn_gamma, L2_ffn_beta)
    x = x + _L3_attn_ref(_layernorm(x, axis=-1), L3_attn_Wq, L3_attn_bq, L3_attn_Wk, L3_attn_bk, L3_attn_Wv, L3_attn_bv, L3_attn_Wo, L3_attn_bo)
    x = x + _L3_xattn_ref(_layernorm(x, axis=-1), ctx_768, mask_BxS_bf1, mask_BxS2_bf1, L3_xattn_Wq, L3_xattn_Wk, L3_xattn_Wv, L3_xattn_W_film_in, L3_xattn_b_film_in, L3_xattn_W_film_out, L3_xattn_b_film_out, L3_xattn_g_norm_in, L3_xattn_b_norm_in, L3_xattn_g_norm_out, L3_xattn_b_norm_out, L3_xattn_g_ffn, L3_xattn_b_ffn, L3_xattn_W1, L3_xattn_b1, L3_xattn_W2, L3_xattn_b2, L3_xattn_log_dt, L3_xattn_A_re, L3_xattn_A_im, L3_xattn_C_re, L3_xattn_C_im, L3_xattn_D_skip, L3_xattn_mod_gate)
    x = x + _L3_ffn_ref(_layernorm(x, axis=-1), L3_ffn_wg, L3_ffn_bg, L3_ffn_Wgate, L3_ffn_Wup, L3_ffn_Wdown)
    return x

_drawn_inputs = setup_inputs


def setup_inputs(seed=0):
    import zlib

    import numpy as np

    out = dict(_drawn_inputs(seed))
    spreads = {'L0_attn_ln_g': (1.0, 0.6),
     'L0_attn_ln_b': (0.0, 0.8),
     'L0_attn_b_qkv': (0.0, 0.8),
     'L0_attn_b_out': (0.0, 0.62),
     'L0_xattn_bo': (0.0, 0.1),
     'L1_ffn_expert_bias': (0.0, 0.273),
     'L2_attn_subln_w': (1.0, 0.2),
     'L2_attn_bn_gamma': (1.0, 0.2),
     'L2_attn_bn_beta': (0.0, 0.1),
     'L2_ffn_router_b': (0.0, 0.1),
     'L2_ffn_b1': (0.0, 0.1),
     'L2_ffn_b2': (0.0, 0.1),
     'L2_ffn_gamma': (1.0, 0.2),
     'L2_ffn_beta': (0.0, 0.1),
     'L3_attn_bq': (0.0, 0.8),
     'L3_attn_bk': (0.0, 0.8),
     'L3_attn_bv': (0.0, 0.8),
     'L3_attn_bo': (0.0, 0.454),
     'L3_xattn_b_film_in': (0.0, 0.449),
     'L3_xattn_b_film_out': (0.0, 0.581),
     'L3_xattn_g_norm_in': (1.0, 0.2),
     'L3_xattn_b_norm_in': (0.0, 0.294),
     'L3_xattn_g_norm_out': (1.0, 0.2),
     'L3_xattn_b_norm_out': (0.0, 0.275),
     'L3_xattn_g_ffn': (1.0, 0.6),
     'L3_xattn_b_ffn': (0.0, 0.8),
     'L3_xattn_b1': (0.0, 0.8),
     'L3_xattn_b2': (0.0, 0.507),
     'L3_xattn_A_re': (-0.5, 0.6),
     'L3_ffn_bg': (0.0, 0.8)}
    factors = {'L0_attn_w_qkv': 8.0,
     'L0_attn_w_ent': 8.0,
     'L0_attn_w_out': 8.0,
     'L0_ffn_gate_b': 4.06,
     'L1_xattn_bq': 8.0,
     'L1_xattn_bk': 8.0,
     'L1_ffn_b1': 8.0,
     'L1_ffn_b3': 8.0,
     'L1_ffn_sb1': 7.189,
     'L1_ffn_sb3': 7.256,
     'L2_attn_lq1': 3.231,
     'L2_attn_lk1': 2.897,
     'L2_attn_lq2': 8.0,
     'L2_attn_lk2': 8.0,
     'L2_xattn_bq': 8.0,
     'L2_xattn_bk': 8.0,
     'L2_xattn_bv': 8.0,
     'L2_xattn_bo': 7.965,
     'L3_attn_Wq': 8.0,
     'L3_attn_Wk': 8.0,
     'L3_attn_Wv': 7.531,
     'L3_attn_Wo': 6.479,
     'L3_xattn_Wq': 8.0,
     'L3_xattn_Wk': 8.0,
     'L3_xattn_Wv': 8.0,
     'L3_xattn_W_film_in': 8.0,
     'L3_xattn_W_film_out': 8.0,
     'L3_xattn_W1': 6.262,
     'L3_xattn_W2': 5.601,
     'L3_ffn_wg': 8.0,
     'L3_ffn_Wgate': 8.0,
     'L3_ffn_Wup': 8.0,
     'L3_ffn_Wdown': 8.0}
    for name, (base, spread) in spreads.items():
        noise = np.random.default_rng([zlib.crc32(name.encode()), seed]).standard_normal(out[name].shape)
        drawn = base * np.exp(spread * noise) if base else spread * noise
        out[name] = jnp.asarray(drawn.astype(out[name].dtype))
    for name, factor in factors.items():
        out[name] = (out[name] * factor).astype(out[name].dtype)
    return out
```

```python
import math
from contextlib import ExitStack

import numpy as np

import concourse.bass as bass
from concourse import mybir

F32 = mybir.dt.float32
BF16 = mybir.dt.bfloat16
U8 = mybir.dt.uint8
ACT = mybir.ActivationFunctionType
ALU = mybir.AluOpType
AX = mybir.AxisListType

B, S, D = 16, 100, 128
K, C = 1444, 96
GB = 4
NG = B // GB
GT = GB * S
T = B * S
KT = -(-K // 128)
KTAIL = K - 128 * (KT - 1)
HEADS = 16
ARENA = 22200
ROUND = 1.5 * 2 ** 23


class Semaphores:
    def __init__(self, made):
        self.x_loaded = made("x_loaded")
        self.x_final = made("x_final")
        self.stored = made("stored")
        self.start_act = made("start_act")
        self.stage_pe = made("stage_pe")
        self.stage_act = made("stage_act")
        self.act_done = made("act_done")
        self.dve_done = made("dve_done")
        self.mean = made("mean")
        self.centred = made("centred")
        self.squared = made("squared")
        self.variance = made("variance")
        self.deviated = made("deviated")
        self.magnitudes = made("magnitudes")
        self.totals = made("totals")
        self.bn_var = made("bn_var")
        self.bn_dev = made("bn_dev")
        self.lam_sum = made("lam_sum")
        self.lam_exp = made("lam_exp")
        self.xg_ready = made("xg_ready")
        self.proj_full = made("proj_full")
        self.proj_free = made("proj_free")
        self.head_sq = made("head_sq")
        self.head_norm = made("head_norm")
        self.head_dev = made("head_dev")
        self.unit_done = made("unit_done")
        self.qk_ready = made("qk_ready")
        self.v_ready = made("v_ready")
        self.gate_ready = made("gate_ready")
        self.scores = made("scores")
        self.shifted = made("shifted")
        self.probs_ready = made("probs_ready")
        self.turned = made("turned")
        self.probsT_ready = made("probsT_ready")
        self.o_full = made("o_full")
        self.o_free = made("o_free")
        self.rms_sum = made("rms_sum")
        self.rms_root = made("rms_root")
        self.y_ready = made("y_ready")
        self.y_turned = made("y_turned")
        self.y_feat_ready = made("y_feat_ready")
        self.out_full = made("out_full")
        self.ctx_bf = made("ctx_bf")
        self.q_ready = made("q_ready")
        self.q_bf = made("q_bf")
        self.side_full = made("side_full")
        self.side_free = made("side_free")
        self.scoresT = made("scoresT")
        self.pexp_ready = made("pexp_ready")
        self.u_full = made("u_full")
        self.u_raw_ready = made("u_raw_ready")
        self.u_ready = made("u_ready")
        self.maxima_ready = made("maxima_ready")
        self.qa_ready = made("qa_ready")
        self.w_cross_free = made("w_cross_free")
        self.ctx_bf_free = made("ctx_bf_free")
        self.masks_asked = made("masks_asked")
        self.text_mask_loaded = made("text_mask_loaded")
        self.mask_ready = made("mask_ready")
        self.angles = made("angles")
        self.decays = made("decays")
        self.rotation = made("rotation")
        self.qv_ready = made("qv_ready")
        self.row_scores = made("row_scores")
        self.row_scores_free = made("row_scores_free")
        self.scores_sb_free = made("scores_sb_free")
        self.scores_there = made("scores_there")
        self.low_ready = made("low_ready")
        self.expd_ready = made("expd_ready")
        self.mean_ready = made("mean_ready")
        self.kept_free = made("kept_free")
        self.kept_ready = made("kept_ready")
        self.uv_ready = made("uv_ready")
        self.ct_ready = made("ct_ready")
        self.film_full = made("film_full")
        self.film_free = made("film_free")
        self.logits_ready = made("logits_ready")
        self.weights_asked = made("weights_asked")
        self.weights_exp = made("weights_exp")
        self.weights_ready = made("weights_ready")
        self.gates_turned = made("gates_turned")
        self.gates_ready = made("gates_ready")
        self.gates_there = made("gates_there")
        self.gates_stored = made("gates_stored")
        self.up_done = made("up_done")
        self.h_act_ready = made("h_act_ready")
        self.h_ready = made("h_ready")
        self.down_done = made("down_done")
        self.keys_ready = made("keys_ready")
        self.km_act = made("km_act")
        self.km_pool = made("km_pool")


SELF = {
    "sa0": dict(nsm=1, vw=8, causal=True, scale=1 / math.sqrt(8) / 0.1, bias=True, gate=True, out_scale=0.1),
    "sa1": dict(nsm=1, vw=8, causal=True, scale=1 / math.sqrt(8), bias=False, quant=True, out_scale=1.0),
    "sa2": dict(nsm=2, vw=16, causal=False, scale=1 / math.sqrt(8), bias=False, diff=True, out_scale=1.0),
    "sa3": dict(nsm=1, vw=8, causal=True, scale=1 / math.sqrt(16) / 1.5, bias=True, unit=True, out_scale=0.5),
}
LAMBDA_INIT = 0.8 - 0.6 * math.exp(-0.3 * (2 - 1))
CROSS = {
    "ca0": dict(H=16, hd=64, scale=64 ** -0.5),
    "ca1": dict(H=1, hd=128, scale=128 ** -0.5),
    "ca2": dict(H=16, hd=8, scale=8 ** -0.5),
}
FEED = {
    "ff0": dict(E=8, loop=7, last=4, func=ACT.Silu, up2=True, gate="block"),
    "ff1": dict(E=16, loop=2, last=1, func=ACT.Silu, up2=True, gate="chunk", hidden_bias=True, sigmoid=True),
    "ff2": dict(loop=0, last=4, func=ACT.Relu, up2=False, gate=None, hidden_bias=True),
    "ffg": dict(loop=0, last=4, func=ACT.Gelu, up2=False, gate=None, hidden_bias=True),
    "ff3": dict(E=8, loop=7, last=4, func=ACT.Silu, up2=True, gate="block"),
}
TH, TOP = 4, 32
TAKEN = -3e38
STATES = 64
LAGS = 10
CW = 3 * 128 + 2
QR = C + HEADS + 1
RMAX, RBIAS = C, C + HEADS


def column(v):
    return v.reshape(-1, 1)


def self_parts(n, p):
    if n == 0:
        w, b = p["L0_attn_w_qkv"], p["L0_attn_b_qkv"]
        return dict(wqk=w[:256].T, bqk=b[:256].reshape(2, 128).T,
                    wv=np.concatenate([w[256:].T, p["L0_attn_w_ent"].T], 1),
                    bv=np.concatenate([b[256:], p["L0_attn_b_ent"]])[None],
                    wo=p["L0_attn_w_out"].T, bo=column(p["L0_attn_b_out"]),
                    ln_g=column(p["L0_attn_ln_g"]), ln_b=column(p["L0_attn_ln_b"]))
    if n == 1:
        w = p["L1_attn_w_attn"]
        return dict(wqk=w[:256].T, wv=w[256:].T, wo=p["L1_attn_w_proj"].T)
    if n == 2:
        c = p["L2_attn_c_w"].T
        return dict(wqk=np.concatenate([p["L2_attn_" + k].T for k in ("q1_w", "k1_w", "q2_w", "k2_w")], 1),
                    wv=p["L2_attn_v_w"].T, wo=np.concatenate([c[:128], c[128:]], 1),
                    subln=np.tile(p["L2_attn_subln_w"], (128, 1)),
                    lam=np.tile(np.concatenate([p["L2_attn_" + k] for k in ("lq1", "lk1", "lq2", "lk2")]), (128, 1)),
                    bn_g=column(p["L2_attn_bn_gamma"]), bn_b=column(p["L2_attn_bn_beta"]))
    return dict(wqk=np.concatenate([p["L3_attn_Wq"].T, p["L3_attn_Wk"].T], 1),
                bqk=np.stack([p["L3_attn_bq"], p["L3_attn_bk"]], 1),
                wv=p["L3_attn_Wv"].T, bv=p["L3_attn_bv"][None],
                wo=p["L3_attn_Wo"].T, bo=column(p["L3_attn_bo"]))


def by_head(w, H):
    return np.transpose(w.reshape(w.shape[0], H, -1), (2, 1, 0))


def key_rows(wk, bk, H):
    k = by_head(wk, H)
    out = np.zeros((k.shape[0], H, QR), wk.dtype)
    out[:, :, :C] = k
    if bk is not None:
        out[:, :, RBIAS] = bk.reshape(H, -1).T
    return out.reshape(k.shape[0], -1)


def cross_parts(n, p):
    if n == 0:
        wv = np.concatenate([p["L0_xattn_Wv"], np.zeros((1, 1024), np.float32)], 0)
        return dict(wq=by_head(p["L0_xattn_Wq"], 16).reshape(64, -1), wk=key_rows(p["L0_xattn_Wk"], None, 16),
                    wv=by_head(wv, 16).reshape(64, -1),
                    wo=p["L0_xattn_Wo"].reshape(16, 64, 128).transpose(1, 0, 2).reshape(64, -1),
                    bo=column(p["L0_xattn_bo"]))
    if n == 1:
        return dict(wq=p["L1_xattn_Wq"], wk=key_rows(p["L1_xattn_Wk"].T, p["L1_xattn_bk"], 1),
                    bq=column(p["L1_xattn_bq"]),
                    wvo=np.concatenate([p["L1_xattn_Wv"].T, p["L1_xattn_bv"][None]], 0))
    wv = np.concatenate([p["L2_xattn_wv"], p["L2_xattn_bv"][None]], 0)
    return dict(wq=by_head(p["L2_xattn_wq"], 16).reshape(8, -1), wk=key_rows(p["L2_xattn_wk"], p["L2_xattn_bk"], 16),
                bq=p["L2_xattn_bq"].reshape(16, 8).T, wv=by_head(wv, 16).reshape(8, -1),
                wo=p["L2_xattn_wo"].reshape(16, 8, 128).transpose(1, 0, 2).reshape(8, -1),
                bo=column(p["L2_xattn_bo"]))


def chunks_of(up, up2, down, b1=None, b2=None):
    n = up.shape[1] // 128
    out = np.zeros((n, 128, CW), np.float32)
    out[:, :, 0:128] = up.reshape(128, n, 128).transpose(1, 0, 2)
    if up2 is not None:
        out[:, :, 128:256] = up2.reshape(128, n, 128).transpose(1, 0, 2)
    out[:, :, 256:384] = down.reshape(n, 128, 128)
    if b1 is not None:
        out[:, :, 384] = b1.reshape(n, 128)
    if b2 is not None:
        out[:, :, 385] = b2.reshape(n, 128)
    return out


def feed_parts(n, p):
    def wide(w):
        return w.transpose(1, 0, 2).reshape(w.shape[1], -1)

    if n == 0:
        return (chunks_of(wide(p["L0_ffn_w1"]), wide(p["L0_ffn_w3"]), p["L0_ffn_w2"].reshape(-1, 128)),
                dict(gate=p["L0_ffn_gate_w"], gate_b=p["L0_ffn_gate_b"][None]))
    if n == 1:
        up = [np.concatenate([wide(p[f"L1_ffn_w{k}"].transpose(0, 2, 1)), p[f"L1_ffn_sw{k}"].T], 1) for k in (1, 3)]
        down = np.concatenate([p["L1_ffn_w2"].transpose(0, 2, 1).reshape(-1, 128), p["L1_ffn_sw2"].T], 0)
        bias = [np.concatenate([p[f"L1_ffn_b{k}"].reshape(-1), p[f"L1_ffn_sb{k}"]]) for k in (1, 3)]
        return (chunks_of(up[0], up[1], down, *bias),
                dict(gate=p["L1_ffn_gate_w"].T, expert_b=np.tile(p["L1_ffn_expert_bias"], (128, 1)),
                     b2=p["L1_ffn_b2"], sb2=p["L1_ffn_sb2"][None]))
    if n == 2:
        return (chunks_of(p["L2_ffn_w1"][0], None, p["L2_ffn_w2"][0], p["L2_ffn_b1"][0]),
                dict(b2=p["L2_ffn_b2"][0][None], ln_g=column(p["L2_ffn_gamma"]), ln_b=column(p["L2_ffn_beta"])))
    if n == "g":
        return (chunks_of(p["L3_xattn_W1"], None, p["L3_xattn_W2"], p["L3_xattn_b1"]), dict(b2=p["L3_xattn_b2"][None]))
    return (chunks_of(wide(p["L3_ffn_Wgate"].transpose(0, 2, 1)), wide(p["L3_ffn_Wup"].transpose(0, 2, 1)),
                      p["L3_ffn_Wdown"].transpose(0, 2, 1).reshape(-1, 128)),
            dict(gate=p["L3_ffn_wg"].T, gate_b=p["L3_ffn_bg"][None]))


def film_parts(p):
    q = {k[len("L3_xattn_"):]: v for k, v in p.items() if k.startswith("L3_xattn_")}
    return dict(wq=by_head(q["Wq"], TH).reshape(32, -1), wk=by_head(q["Wk"], TH).reshape(32, -1), wv=q["Wv"],
                film_in=q["W_film_in"], film_out=q["W_film_out"],
                b_film_in=q["b_film_in"].reshape(2, 128).T, b_film_out=q["b_film_out"].reshape(2, 128).T,
                g_in=column(q["g_norm_in"]), b_in=column(q["b_norm_in"]), g_out=column(q["g_norm_out"]),
                b_out=column(q["b_norm_out"]), g_ffn=column(q["g_ffn"]), b_ffn=column(q["b_ffn"]),
                log_dt=column(q["log_dt"]), A_re=q["A_re"], A_im=q["A_im"], C_re=q["C_re"], C_im=q["C_im"],
                skip=column(q["D_skip"]), mod=np.tile(q["mod_gate"].reshape(1, 1), (128, 1)))


def pack(parts):
    where, n = {}, 0
    for name, a in parts.items():
        where[name] = (a.shape[0], n, a.shape[1])
        n += a.shape[1]
    out = np.zeros((128, n), np.float32)
    for name, a in parts.items():
        rows, at, cols = where[name]
        out[:rows, at:at + cols] = a
    return out, where


def constants():
    i = np.arange(128)
    ident = np.eye(128, dtype=np.float32)
    mean = np.full((128, 128), 1 / 128, np.float32)
    ones = np.ones((128, 128), np.float32)
    causal = np.where(np.arange(S)[None, :] <= np.arange(S)[:, None], 0.0, -1e30).astype(np.float32)
    row96 = np.zeros((C + 1, C + 1), np.float32)
    row96[C] = 1
    own_head = np.zeros((C + HEADS, HEADS), np.float32)
    for h in range(HEADS):
        own_head[C + h, h] = -1
    head_rows = (i[:, None] // 8 == i[None, :] // 8).astype(np.float32)
    head_of = (i[:, None] // 8 == np.arange(HEADS)[None, :]).astype(np.float32)
    return dict(ident=ident, mean=mean, ones=ones, causal=np.tile(causal, (1, 4)), row96=row96,
                own_head=own_head, head_rows=head_rows, head_of=head_of,
                zeros=np.zeros((HEADS, 128), np.float32),
                ones_row=np.ones((1, GT), np.float32),
                before=np.tile((np.arange(16)[None, :] < np.arange(16)[:, None]).astype(np.float32).reshape(1, -1), (128, 1)))


def build(nc, dram, where, out):
    ctx = ExitStack()

    def sb(name, shape, dt=F32):
        return ctx.enter_context(nc.sbuf_tensor(name, shape, dt))

    cross_cols = max(dram[k].shape[1] for k in CROSS)
    w_cross = sb("w_cross", [128, cross_cols])
    packed = {k: w_cross if k in CROSS else sb("w_" + k, [128, dram[k].shape[1]]) for k in where}

    def W(stage, name):
        rows, at, cols = where[stage][name]
        return packed[stage][0:rows, at:at + cols]

    s = Semaphores(lambda name: ctx.enter_context(nc.semaphore(name)))
    loaded = {k: ctx.enter_context(nc.semaphore("loaded_" + k)) for k in where}
    ctx_loaded = [ctx.enter_context(nc.semaphore(f"ctx_loaded_{i}")) for i in range(2)]
    chunk_loaded = [ctx.enter_context(nc.semaphore(f"chunk_loaded_{i}")) for i in range(4)]
    chunk_free = [ctx.enter_context(nc.semaphore(f"chunk_free_{i}")) for i in range(4)]
    gate_loaded = [ctx.enter_context(nc.semaphore(f"gate_loaded_{i}")) for i in range(NG)]
    gate_free = [ctx.enter_context(nc.semaphore(f"gate_free_{i}")) for i in range(NG)]
    ctx_free = [ctx.enter_context(nc.semaphore(f"ctx_free_{i}")) for i in range(2)]
    ps = ctx.enter_context(nc.psum_tensor("ps", [128, 8, 512], F32))

    x = sb("x", [128, B, S])
    xn = sb("xn", [128, B, S])
    mid = sb("mid", [128, B, S])
    squares = sb("squares", [128, B, S])
    deviation = sb("deviation", [128, B, S])
    eps = sb("eps", [128, 2])
    ident_bf = sb("ident_bf", [128, 128], BF16)
    causal_bf = sb("causal_bf", [S, GT], BF16)
    bn = sb("bn", [128, 4, 6])
    col = sb("col", [128, 16])

    arena = sb("arena", [128, ARENA])
    filled = [0]

    def shared(shape, dt=F32):
        n = math.prod(shape[1:])
        words = {F32: n, BF16: -(-n // 2), U8: -(-n // 4)}[dt]
        v = arena[0:shape[0], filled[0]:filled[0] + words]
        filled[0] += words
        assert filled[0] <= ARENA, filled
        if dt != F32:
            v = v.bitcast(dt)[:, 0:n]
        if len(shape) == 3:
            v = v.rearrange("p (a b) -> p a b", b=shape[2])
        return v

    xg = shared([128, GT])
    qk = shared([128, 4, GT])
    km = shared([128, 2 * HEADS, GT])
    vaug = shared([S, GB, 16 * 17])
    gate = shared([S, GB])
    probs = shared([S, 2, 8 * S])
    probsT = shared([S, 2, 8 * S])
    smax = shared([S, 2, 8])
    rden = shared([S, 16])
    y_tok = shared([S, GB, 256])
    y_sq = shared([S, GB, 256])
    y_rms = shared([S, GB * 16])
    y_feat = shared([128, 2, GT])

    filled[0] = 0
    ctxT = [sb(f"ctxT{i}", [QR, K]) for i in range(2)]
    ctxk = [sb(f"ctxk{i}", [128, KT, C + 1]) for i in range(2)]
    ctxT_bf = shared([QR, K], BF16)
    wfold = shared([128, 16 * QR])
    bfold = shared([QR, 16])
    vfold = shared([C + 1, 16 * 128])
    qa = [shared([QR, HEADS, S]) for i in range(2)]
    qa_bf = shared([QR, HEADS, S], BF16)
    mparts = shared([S, HEADS, 3])
    mrows = shared([S, C + HEADS])
    pexp = [shared([128, GT]) for i in range(3)]
    u_raw = shared([C + 1, HEADS, S])
    u_rec = shared([C + 1, HEADS, S])

    filled[0] = 0
    text_mask = shared([128, T // 4])
    ct = shared([128, B, S])
    scores_sb = [shared([S, K]) for i in range(2)]
    left = shared([S, K])
    expd = [shared([S, K]) for i in range(2)]
    kept = shared([S, TH, K])
    turn_scale = shared([S, TH, S])
    meanT = shared([128, KT, S])
    uv = shared([C, S])
    qv = shared([C, TH, S])
    top8 = shared([S, 4, 8])
    low = shared([S, 2])
    den = shared([S, TH])
    wf4 = shared([128, TH * C])
    mask_u8 = [shared([1, K], U8) for i in range(2)]
    mask_bf = [shared([1, K], BF16) for i in range(2)]
    ones_bf = sb("ones_bf", [1, 128], BF16)
    kernel_l = sb("kernel_l", [128, S])
    filled[0] = 0
    ssm = shared([128, 12, STATES])
    powers = [[shared([128, LAGS + 1, STATES]) for part in range(2)] for base in range(2)]
    prods = [shared([128, S, STATES]) for i in range(2)]
    scratch = [shared([128, LAGS * STATES]) for i in range(3)]
    filled[0] = 0
    logits = shared([S, B, 16])
    biased = shared([S, B, 16])
    rank = shared([S, B, 16])
    weight = shared([S, B, 16])
    best = shared([S, B])
    pairs = shared([S, B * 256])
    pairs2 = shared([S, B * 256])
    gateT = shared([16, T])
    gate_rows = [shared([128, GT]) for g in range(NG)]
    h_act = [shared([128, GT]) for i in range(2)]
    h_all = [shared([128, GT]) for i in range(2)]
    chunk = [sb(f"chunk{c}", [128, CW]) for c in range(4)]
    gate_dram = nc.dram_tensor("gate_dram", (16, T), F32).ap()

    block = ctx.enter_context(nc.Block())
    FF = list(FEED)
    SA, CA = list(SELF), list(CROSS)

    def bank(n, cols=GT, rows=128, at=0):
        return ps[0:rows, n, at:at + cols]

    def group(t, g):
        return t[:, GB * g:GB * g + GB, :]

    def eps_col(i):
        return eps[:, i:i + 1]

    def bs(v):
        return v.rearrange("p (b t) -> p b t", t=S)

    def stages(layernorm, self_attention, cross_attention, feed_forward, film_block):
        layernorm(x)
        layernorm(xn, eps=1, affine=(W("sa0", "ln_g"), W("sa0", "ln_b")))
        self_attention(0)
        layernorm(x)
        cross_attention(0)
        layernorm(x)
        feed_forward(0)
        layernorm(x)
        self_attention(1)
        layernorm(x)
        cross_attention(1)
        layernorm(x)
        feed_forward(1)
        layernorm(x)
        self_attention(2)
        layernorm(x)
        cross_attention(2)
        layernorm(x)
        feed_forward(2)
        layernorm(xn, affine=(W("ff2", "ln_g"), W("ff2", "ln_b")), add=True)
        layernorm(x)
        self_attention(3)
        film_block(layernorm, feed_forward)
        layernorm(x)
        feed_forward(4)

    CHUNKS = [(0, 482), (482, 962), (962, K)]

    def key_rows_of(t):
        return 128 if t < KT - 1 else KTAIL

    def units(H):
        if H == 1:
            return [[(4 * u + j, j * S, 0, 1, 0) for j in range(4)] for u in range(KT // 4)]
        return [[(t, 0, 4 * g, 4, g)] for t in range(KT) for g in range(H // 4)]

    def side_items(H, prep, tail):
        items = []
        if tail:
            items += [("spread", g) for g in range(-(-H // 4))] + [("project", 0)]
        if prep:
            items += [("query", g) for g in range(-(-H // 4))]
            items += [("chunk", (h, c)) for h in range(H) for c in range(3)] + [("maxima", 0)]
        return items

    @block.sync
    def _(sp):
        sp.dma_start(x[:, :, :], dram["x"]).then_inc(s.x_loaded, 16)
        for k in where:
            if k not in CROSS:
                sp.dma_start(packed[k][:, :], dram[k]).then_inc(loaded[k], 16)

        def layernorm(src, eps=0, affine=None, add=False):
            pass

        def self_attention(n):
            pass

        def cross_attention(n):
            def load(b, par):
                sp.wait_ge(ctx_free[par], 1)
                sp.sem_inc(ctx_free[par], -1)
                sp.dma_start(ctxT[par][0:C, :], dram["ctxT"][b, :, :]).then_inc(ctx_loaded[par], 16)
                sp.dma_start(ctxk[par][:, 0:KT - 1, 0:C],
                             dram["ctx"][b, 0:128 * (KT - 1), :].rearrange("(t p) c -> p t c", p=128)).then_inc(ctx_loaded[par], 16)
                sp.dma_start(ctxk[par][0:KTAIL, KT - 1, 0:C],
                             dram["ctx"][b, 128 * (KT - 1):K, :]).then_inc(ctx_loaded[par], 16)
            k = CA[n]
            sp.wait_ge(s.w_cross_free, 1)
            sp.sem_inc(s.w_cross_free, -1)
            sp.dma_start(w_cross[:, 0:dram[k].shape[1]], dram[k]).then_inc(loaded[k], 16)
            load(0, 0)
            with sp.Fori(0, B // 2 - 1) as i:
                load(2 * i + 1, 1)
                load(2 * i + 2, 0)
            load(B - 1, 1)

        def film_block(layernorm, feed_forward):
            def load(b, par):
                sp.wait_ge(ctx_free[par], 1)
                sp.sem_inc(ctx_free[par], -1)
                sp.dma_start(ctxT[par][0:C, :], dram["ctxT"][bass.ds(b, 1), :, :].rearrange("o c k -> (o c) k")).then_inc(ctx_loaded[par], 16)
                sp.dma_start(ctxk[par][:, 0:KT - 1, 0:C],
                             dram["ctx"][bass.ds(b, 1), 0:128 * (KT - 1), :].rearrange("o (t p) c -> p (o t) c", p=128)).then_inc(ctx_loaded[par], 16)
                sp.dma_start(ctxk[par][0:KTAIL, KT - 1, 0:C],
                             dram["ctx"][bass.ds(b, 1), 128 * (KT - 1):K, :].rearrange("o k c -> (o k) c")).then_inc(ctx_loaded[par], 16)
                sp.dma_start(mask_u8[par][:, :], dram["ctx_mask"][bass.ds(b, 1), :]).then_inc(ctx_loaded[par], 16)
            sp.wait_ge(s.masks_asked, 1)
            sp.sem_inc(s.masks_asked, -1)
            sp.dma_start(text_mask.bitcast(U8), dram["text_mask"].to_broadcast([128, T])).then_inc(s.text_mask_loaded, 16)
            load(0, 0)
            with sp.Fori(0, B // 2 - 1) as i:
                load(2 * i + 1, 1)
                load(2 * i + 2, 0)
            load(B - 1, 1)
            feed_forward(3)

        def feed_forward(n):
            cfg = FEED[FF[n]]
            blobs = dram[FF[n] + "_chunks"]

            def weights(i, c):
                sp.wait_ge(chunk_free[c], 1)
                sp.sem_inc(chunk_free[c], -1)
                sp.dma_start(chunk[c][:, :], blobs[bass.ds(4 * i + c, 1), :, :].rearrange("o p c -> (o p) c")).then_inc(chunk_loaded[c], 16)

            def gates(i, c):
                per = 1 if cfg["gate"] == "block" else 2
                for g in range(NG):
                    sp.wait_ge(gate_free[g], 1)
                    sp.sem_inc(gate_free[g], -1)
                    for e in range(per):
                        row = i if per == 1 else 8 * i + 2 * c + e
                        rows = 128 // per
                        sp.dma_start(gate_rows[g][rows * e:rows * e + rows, :],
                                     gate_dram[bass.ds(row, 1), g * GT:g * GT + GT].to_broadcast([rows, GT])).then_inc(gate_loaded[g], 16)

            def block(i, chunks):
                for c in chunks:
                    if cfg["gate"] == "chunk" and not (len(chunks) == 1):
                        weights(i, c)
                        gates(i, c)
                    elif cfg["gate"] == "block" and c == 3:
                        gates(i, c)
                        weights(i, c)
                    else:
                        weights(i, c)

            if cfg["gate"]:
                sp.wait_ge(s.gates_ready, 1)
                sp.sem_inc(s.gates_ready, -1)
                sp.dma_start(gate_dram[0:cfg["E"], :], gateT[0:cfg["E"], :]).then_inc(s.gates_stored, 16)
                sp.wait_ge(s.gates_stored, 16)
                sp.sem_inc(s.gates_stored, -16)
            if cfg["loop"]:
                with sp.Fori(0, cfg["loop"]) as i:
                    block(i, range(4))
            block(cfg["loop"], range(cfg["last"]))
            if cfg["gate"]:
                for g in range(NG):
                    sp.wait_ge(gate_free[g], 1)
                    sp.sem_inc(gate_free[g], -1)

        stages(layernorm, self_attention, cross_attention, feed_forward, film_block)
        sp.wait_ge(s.x_final, 1)
        sp.sem_inc(s.x_final, -1)
        sp.dma_start(out, x[:, :, :]).then_inc(s.stored, 16)
        sp.wait_ge(s.stored, 16)

    @block.gpsimd
    def _(pool):
        def layernorm(src, eps=0, affine=None, add=False):
            pass

        def self_attention(n):
            nsm = SELF[SA[n]]["nsm"]
            pool.wait_ge(loaded["const"], 16)
            with pool.Fori(0, NG) as g:
                for sm in range(nsm):
                    pool.wait_ge(s.keys_ready, 1)
                    pool.sem_inc(s.keys_ready, -1)
                    for h in range(HEADS // 2, HEADS):
                        ins = nc.gpsimd.tensor_scalar(km[:, HEADS * sm + h, :], qk[:, 2 * sm + 1, :],
                                                      W("const", "head_of")[:, h:h + 1], None, ALU.mult)
                    ins.then_inc(s.km_pool, 1)

        def cross_attention(n):
            H = CROSS[CA[n]]["H"]

            def prep(par):
                pool.wait_ge(ctx_loaded[par], 48)
                pool.sem_inc(ctx_loaded[par], -48)
                pool.wait_ge(s.ctx_bf_free, 1)
                pool.sem_inc(s.ctx_bf_free, -1)
                nc.gpsimd.tensor_copy(ctxT_bf[:, :], ctxT[par][:, :]).then_inc(s.ctx_bf)
                for g in range(-(-H // 4)):
                    pool.wait_ge(s.q_ready, 1)
                    pool.sem_inc(s.q_ready, -1)
                    hs = slice(4 * g, min(4 * g + 4, H))
                    nc.gpsimd.tensor_copy(qa_bf[:, hs, :], qa[par][:, hs, :]).then_inc(s.q_bf)
            prep(0)
            with pool.Fori(0, B // 2 - 1) as i:
                prep(1)
                prep(0)
            prep(1)
            pool.wait_ge(s.ctx_bf_free, 1)
            pool.sem_inc(s.ctx_bf_free, -1)

        def feed_forward(n):
            pass

        def film_block(layernorm, feed_forward):
            def mask(par):
                pool.wait_ge(ctx_loaded[par], 64)
                pool.sem_inc(ctx_loaded[par], -64)
                nc.gpsimd.tensor_scalar(mask_bf[par][:, :], mask_u8[par][:, :], 1.0, 1e30, ALU.subtract, ALU.mult).then_inc(s.mask_ready, 1)
            mask(0)
            with pool.Fori(0, B // 2 - 1) as i:
                mask(1)
                mask(0)
            mask(1)

        stages(layernorm, self_attention, cross_attention, feed_forward, film_block)

    @block.scalar
    def _(act):
        def layernorm(src, eps=0, affine=None, add=False):
            for g in range(NG):
                act.wait_ge(s.centred, 1)
                act.sem_inc(s.centred, -1)
                nc.scalar.activation(group(squares, g), group(xn, g), ACT.Square).then_inc(s.squared, 1)
            for g in range(NG):
                act.wait_ge(s.variance, 1)
                act.sem_inc(s.variance, -1)
                nc.scalar.activation(group(deviation, g), bs(bank(4 + g)), ACT.Sqrt,
                                     bias=eps_col(eps)).then_inc(s.deviated, 1)

        def self_attention(n):
            cfg = SELF[SA[n]]
            nsm, vw = cfg["nsm"], cfg["vw"]
            if cfg.get("diff"):
                act.wait_ge(s.bn_var, 1)
                act.sem_inc(s.bn_var, -1)
                nc.scalar.activation(col[:, 2:3], col[:, 2:3], ACT.Sqrt, bias=eps_col(0)).then_inc(s.bn_dev, 1)
                act.wait_ge(s.lam_sum, 1)
                act.sem_inc(s.lam_sum, -1)
                nc.scalar.activation(col[0:S, 4:6], col[0:S, 4:6], ACT.Exp).then_inc(s.lam_exp, 1)
            act.wait_ge(s.stage_act, 1)
            act.sem_inc(s.stage_act, -1)
            with act.Fori(0, NG) as g:
                for m in range(2 * nsm):
                    act.wait_ge(s.proj_full, 1)
                    act.sem_inc(s.proj_full, -1)
                    if cfg["bias"]:
                        ins = nc.scalar.activation(qk[:, m, :], bank(6), ACT.Identity, bias=W(SA[n], "bqk")[:, m:m + 1])
                    else:
                        ins = nc.scalar.activation(qk[:, m, :], bank(6), ACT.Copy)
                    ins.then_inc(s.act_done, 1)
                    act.wait_ge(s.act_done, 1)
                    act.sem_inc(s.act_done, -1)
                    act.sem_inc(s.proj_free, 1)
                    if cfg.get("unit"):
                        nc.scalar.activation(group(squares, 0), bs(qk[:, m, :]), ACT.Square).then_inc(s.head_sq, 1)
                        act.wait_ge(s.head_norm, 1)
                        act.sem_inc(s.head_norm, -1)
                        nc.scalar.activation(group(deviation, 0), bs(bank(7)), ACT.Sqrt).then_inc(s.head_dev, 1)
                        act.wait_ge(s.unit_done, 1)
                        act.sem_inc(s.unit_done, -1)
                    if m % 2 == 1:
                        act.sem_inc(s.keys_ready, 1)
                        for h in range(HEADS // 2):
                            ins = nc.scalar.activation(km[:, HEADS * (m // 2) + h, :], qk[:, m, :], ACT.Copy,
                                                       scale=W("const", "head_of")[:, h:h + 1])
                        ins.then_inc(s.km_act, 1)
                for b in range(GB):
                    act.wait_ge(s.proj_full, 1)
                    act.sem_inc(s.proj_full, -1)
                    v = vaug[:, b, 0:16 * (vw + 1)].rearrange("p (h w) -> p h w", w=vw + 1)
                    nc.scalar.activation(v[:, :, 0:vw], bank(6, 16 * vw, S).rearrange("p (h w) -> p h w", w=vw), ACT.Copy).then_inc(s.act_done, 1)
                    act.wait_ge(s.act_done, 1)
                    act.sem_inc(s.act_done, -1)
                    if cfg.get("gate"):
                        nc.scalar.activation(gate[:, b:b + 1], bank(6, 1, S, 128), ACT.Exp, scale=-1.0).then_inc(s.act_done, 1)
                        act.wait_ge(s.act_done, 1)
                        act.sem_inc(s.act_done, -1)
                    act.sem_inc(s.proj_free, 1)
                    act.sem_inc(s.gate_ready if cfg.get("gate") else s.v_ready, 1)
                N = GB * nsm * 2
                for k in range(N):
                    act.wait_ge(s.shifted, 1)
                    act.sem_inc(s.shifted, -1)
                    nc.scalar.activation(probs[:, k % 2, :].rearrange("p (c t) -> p c t", c=2),
                                         ps[0:S, 2 * (k % 2):2 * (k % 2) + 2, 0:GT], ACT.Exp,
                                         scale=float(cfg["scale"])).then_inc(s.probs_ready, 1)
                    for c in range(2):
                        act.wait_ge(s.turned, 1)
                        act.sem_inc(s.turned, -1)
                        nc.scalar.activation(probsT[:, k % 2, c * GT:c * GT + GT], bank(4 + c, GT, S),
                                             ACT.Copy).then_inc(s.probsT_ready, 1)
                if cfg.get("diff"):
                    act.wait_ge(s.rms_sum, 1)
                    act.sem_inc(s.rms_sum, -1)
                    nc.scalar.activation(y_rms[:, :], y_rms[:, :], ACT.Sqrt, bias=eps_col(0)[0:S]).then_inc(s.rms_root, 1)
                for c in range(cfg["vw"] // 8):
                    act.wait_ge(s.y_turned, 1)
                    act.sem_inc(s.y_turned, -1)
                    nc.scalar.activation(y_feat[:, c, :], bank(6), ACT.Copy).then_inc(s.act_done, 1)
                    act.wait_ge(s.act_done, 1)
                    act.sem_inc(s.act_done, -1)
                    act.sem_inc(s.proj_free, 1)
                    act.sem_inc(s.y_feat_ready, 1)

        def cross_attention(n):
            H = CROSS[CA[n]]["H"]
            nU = -(-H // 4)
            act.wait_ge(s.stage_act, 1)
            act.sem_inc(s.stage_act, -1)

            def main(par):
                for u, unit in enumerate(units(H)):
                    act.wait_ge(s.scoresT, 1)
                    act.sem_inc(s.scoresT, -1)
                    t0, rows = unit[0][0], key_rows_of(unit[-1][0])
                    full = GT if rows == 128 else GT - S if H == 1 else 0
                    if full:
                        ins = nc.scalar.activation(pexp[u % 3][:, 0:full], bank(u % 2, full), ACT.Exp,
                                                   scale=CROSS[CA[n]]["scale"])
                    if full < GT:
                        if full:
                            ins.then_inc(s.act_done, 1)
                            act.wait_ge(s.act_done, 1)
                            act.sem_inc(s.act_done, -1)
                        ins = nc.scalar.activation(pexp[u % 3][0:rows, full:GT], bank(u % 2, GT - full, rows, full), ACT.Exp,
                                                   scale=CROSS[CA[n]]["scale"])
                    ins.then_inc(s.pexp_ready, 1)
                for g in range(nU):
                    act.wait_ge(s.u_full, 1)
                    act.sem_inc(s.u_full, -1)
                    w = min(H, 4)
                    nc.scalar.activation(u_raw[:, 4 * g:4 * g + w, :], bs(bank(2 + g, w * S, C + 1)),
                                         ACT.Copy).then_inc(s.u_raw_ready, 1)
                act.sem_inc(ctx_free[par], 1)
            main(0)
            with act.Fori(0, B // 2 - 1) as i:
                main(1)
                main(0)
            main(1)

        def film_block(layernorm, feed_forward):
            layernorm(x)
            act.wait_ge(s.angles, 1)
            act.sem_inc(s.angles, -1)
            nc.scalar.activation(ssm[:, 2:4, :], ssm[:, 2:4, :], ACT.Sin).then_inc(s.rotation, 1)
            act.wait_ge(s.decays, 1)
            act.sem_inc(s.decays, -1)
            nc.scalar.activation(ssm[:, 0, :], ssm[:, 0, :], ACT.Exp).then_inc(s.rotation, 1)
            act.wait_ge(s.stage_act, 1)
            act.sem_inc(s.stage_act, -1)

            def scores(b, h):
                if h == 0:
                    act.wait_ge(s.proj_full, 1)
                    act.sem_inc(s.proj_full, -1)
                    nc.scalar.activation(qv[:, :, :], bank(6, TH * S, C).rearrange("p (h t) -> p h t", t=S), ACT.Copy).then_inc(s.act_done, 1)
                    act.wait_ge(s.act_done, 1)
                    act.sem_inc(s.act_done, -1)
                    act.sem_inc(s.proj_free, 1)
                    act.sem_inc(s.qv_ready, 1)
                act.wait_ge(s.row_scores, 1)
                act.sem_inc(s.row_scores, -1)
                act.wait_ge(s.scores_sb_free, 1)
                act.sem_inc(s.scores_sb_free, -1)
                for c, (a, z) in enumerate(CHUNKS):
                    ins = nc.scalar.activation(scores_sb[h % 2][:, a:z], bank(3 * (h % 2) + c, z - a, S), ACT.Copy, scale=32 ** -0.5)
                ins.then_inc(s.act_done, 1)
                act.wait_ge(s.act_done, 1)
                act.sem_inc(s.act_done, -1)
                act.sem_inc(s.row_scores_free, 1)
                act.sem_inc(s.scores_there, 1)

            def exponents(h):
                act.wait_ge(s.low_ready, 1)
                act.sem_inc(s.low_ready, -1)
                nc.scalar.activation(expd[h % 2], scores_sb[h % 2], ACT.Exp, bias=low[:, h % 2:h % 2 + 1]).then_inc(s.expd_ready, 1)

            def mean(b, par):
                for u in range(KT // 4):
                    act.wait_ge(s.proj_full, 1)
                    act.sem_inc(s.proj_full, -1)
                    full = 4 if u < KT // 4 - 1 else 3
                    ins = nc.scalar.activation(meanT[:, 4 * u:4 * u + full, :], bs(bank(6, full * S)), ACT.Copy)
                    if full < 4:
                        ins.then_inc(s.act_done, 1)
                        act.wait_ge(s.act_done, 1)
                        act.sem_inc(s.act_done, -1)
                        ins = nc.scalar.activation(meanT[0:KTAIL, KT - 1, :], bank(6, S, KTAIL, 3 * S), ACT.Copy)
                    ins.then_inc(s.act_done, 1)
                    act.wait_ge(s.act_done, 1)
                    act.sem_inc(s.act_done, -1)
                    act.sem_inc(s.proj_free, 1)
                    act.sem_inc(s.mean_ready, 1)
                act.sem_inc(s.kept_free, 1)
                act.wait_ge(s.proj_full, 1)
                act.sem_inc(s.proj_full, -1)
                nc.scalar.activation(uv, bank(6, S, C), ACT.Copy).then_inc(s.act_done, 1)
                act.wait_ge(s.act_done, 1)
                act.sem_inc(s.act_done, -1)
                act.sem_inc(s.proj_free, 1)
                act.sem_inc(s.uv_ready, 1)
                act.sem_inc(ctx_free[par], 1)
                act.wait_ge(s.proj_full, 1)
                act.sem_inc(s.proj_full, -1)
                nc.scalar.activation(ct[:, bass.ds(b, 1), :], bs(bank(6, S)), ACT.Copy).then_inc(s.act_done, 1)
                act.wait_ge(s.act_done, 1)
                act.sem_inc(s.act_done, -1)
                act.sem_inc(s.proj_free, 1)

            def batch(b, par, first=False, last=False):
                for h in range(TH):
                    if h < TH - 1:
                        scores(b, h + 1)
                    elif not last:
                        scores(b + 1, 0)
                    exponents(h)
                    if h == 0 and not first:
                        mean(b - 1, 1 - par)
            scores(0, 0)
            batch(0, 0, first=True)
            with act.Fori(0, B // 2 - 1) as i:
                batch(2 * i + 1, 1)
                batch(2 * i + 2, 0)
            batch(B - 1, 1, last=True)
            mean(B - 1, 1)
            act.sem_inc(s.ct_ready, 1)
            layernorm(mid)
            layernorm(mid)
            feed_forward(3)
            layernorm(xn)

        def feed_forward(n):
            cfg = FEED[FF[n]]
            act.wait_ge(s.stage_act, 1)
            act.sem_inc(s.stage_act, -1)
            if cfg["gate"]:
                E = cfg["E"]
                act.wait_ge(s.weights_asked, 1)
                act.sem_inc(s.weights_asked, -1)
                nc.scalar.activation(weight[:, :, 0:E], logits[:, :, 0:E], ACT.Exp,
                                     scale=-1.0 if cfg.get("sigmoid") else 1.0).then_inc(s.weights_exp, 1)
                for g in range(NG):
                    act.wait_ge(s.gates_turned, 1)
                    act.sem_inc(s.gates_turned, -1)
                    ins = nc.scalar.activation(gateT[0:E, g * GT:g * GT + GT], bank(g, GT, E), ACT.Copy)
                    ins.then_inc(s.act_done, 1)
                    act.wait_ge(s.act_done, 1)
                    act.sem_inc(s.act_done, -1)
                act.sem_inc(s.gates_ready, 1)
                act.sem_inc(s.gates_there, 1)

            def block(chunks):
                for u in range(NG * len(chunks)):
                    c = chunks[u // NG]
                    act.wait_ge(s.up_done, 1)
                    act.sem_inc(s.up_done, -1)
                    bias = chunk[c][:, 384:385] if cfg.get("hidden_bias") else 0.0
                    to = h_act if cfg["up2"] else h_all
                    nc.scalar.activation(to[u % 2], bank(u % 2), cfg["func"], bias=bias).then_inc(
                        s.h_act_ready if cfg["up2"] else s.h_ready, 1)
            if cfg["loop"]:
                with act.Fori(0, cfg["loop"]) as i:
                    block(range(4))
            block(range(cfg["last"]))

        act.sem_inc(s.row_scores_free, 2)
        act.sem_inc(s.proj_free, 1)
        act.wait_ge(s.start_act, 1)
        act.sem_inc(s.start_act, -1)
        stages(layernorm, self_attention, cross_attention, feed_forward, film_block)

    @block.vector
    def _(dve):
        def stage_ready(ins):
            ins.then_inc(s.dve_done, 1)
            dve.wait_ge(s.dve_done, 1)
            dve.sem_inc(s.dve_done, -1)
            dve.sem_inc(s.stage_pe, 1)
            dve.sem_inc(s.stage_act, 1)

        def layernorm(src, eps=0, affine=None, add=False):
            for g in range(NG):
                dve.wait_ge(s.mean, 1)
                dve.sem_inc(s.mean, -1)
                nc.vector.tensor_tensor(group(xn, g), group(src, g), bs(bank(g)), ALU.subtract).then_inc(s.dve_done, 1)
                dve.wait_ge(s.dve_done, 1)
                dve.sem_inc(s.dve_done, -1)
                dve.sem_inc(s.centred, 1)
            for g in range(NG):
                dve.wait_ge(s.deviated, 1)
                dve.sem_inc(s.deviated, -1)
                nc.vector.reciprocal(group(deviation, g), group(deviation, g)).then_inc(s.dve_done, 1)
                dve.wait_ge(s.dve_done, 1)
                dve.sem_inc(s.dve_done, -1)
                ins = nc.vector.tensor_tensor(group(xn, g), group(xn, g), group(deviation, g), ALU.mult)
                if affine:
                    ins.then_inc(s.dve_done, 1)
                    dve.wait_ge(s.dve_done, 1)
                    dve.sem_inc(s.dve_done, -1)
                    ins = nc.vector.tensor_scalar(group(xn, g), group(xn, g), affine[0], affine[1], ALU.mult, ALU.add)
                ins.then_inc(s.dve_done, 1)
                dve.wait_ge(s.dve_done, 1)
                dve.sem_inc(s.dve_done, -1)
                if add:
                    nc.vector.tensor_tensor(group(x, g), group(x, g), group(xn, g), ALU.add).then_inc(s.dve_done, 1)
                    dve.wait_ge(s.dve_done, 1)
                    dve.sem_inc(s.dve_done, -1)
            dve.sem_inc(s.stage_pe, 1)

        def quantise(w, total, n):
            nc.vector.tensor_scalar(total, total, 1.0 / n, 1e-8, ALU.mult, ALU.max).then_inc(s.dve_done, 1)
            dve.wait_ge(s.dve_done, 1)
            dve.sem_inc(s.dve_done, -1)
            nc.vector.reciprocal(col[:, 15:16], total).then_inc(s.dve_done, 1)
            dve.wait_ge(s.dve_done, 1)
            dve.sem_inc(s.dve_done, -1)
            for v in w:
                t = squares[:, :, :].rearrange("p b t -> p (b t)")[:, 0:v.shape[1]]
                nc.vector.tensor_scalar(t, v, col[:, 15:16], ROUND, ALU.mult, ALU.add).then_inc(s.dve_done, 1)
                dve.wait_ge(s.dve_done, 1)
                dve.sem_inc(s.dve_done, -1)
                nc.vector.tensor_scalar(t, t, ROUND, 2.0, ALU.subtract, ALU.min).then_inc(s.dve_done, 1)
                dve.wait_ge(s.dve_done, 1)
                dve.sem_inc(s.dve_done, -1)
                nc.vector.tensor_scalar(t, t, -2.0, total, ALU.max, ALU.mult).then_inc(s.dve_done, 1)
                dve.wait_ge(s.dve_done, 1)
                dve.sem_inc(s.dve_done, -1)
                nc.vector.tensor_tensor(t, t, v, ALU.subtract).then_inc(s.dve_done, 1)
                dve.wait_ge(s.dve_done, 1)
                dve.sem_inc(s.dve_done, -1)
                nc.vector.tensor_tensor(v, t, v, ALU.add).then_inc(s.dve_done, 1)
                dve.wait_ge(s.dve_done, 1)
                dve.sem_inc(s.dve_done, -1)

        def magnitude(w, c):
            nc.vector.tensor_reduce(col[:, c:c + 1], w, AX.X, ALU.add, apply_absolute_value=True).then_inc(s.dve_done, 1)
            dve.wait_ge(s.dve_done, 1)
            dve.sem_inc(s.dve_done, -1)

        def self_attention(n):
            cfg = SELF[SA[n]]
            nsm, vw = cfg["nsm"], cfg["vw"]
            wst = SA[n]
            dve.wait_ge(loaded[wst], 16)
            if cfg.get("quant"):
                magnitude(W(wst, "wqk"), 0)
                magnitude(W(wst, "wv"), 1)
                magnitude(W(wst, "wo"), 2)
                nc.vector.tensor_tensor(col[:, 0:1], col[:, 0:1], col[:, 1:2], ALU.add).then_inc(s.dve_done, 1)
                dve.wait_ge(s.dve_done, 1)
                dve.sem_inc(s.dve_done, -1)
                dve.sem_inc(s.magnitudes, 1)
                dve.wait_ge(s.totals, 1)
                dve.sem_inc(s.totals, -1)
                nc.vector.tensor_copy(col[:, 3:6], ps[:, 0, 0:3]).then_inc(s.dve_done, 1)
                dve.wait_ge(s.dve_done, 1)
                dve.sem_inc(s.dve_done, -1)
                quantise([W(wst, "wqk"), W(wst, "wv")], col[:, 3:4], 384 * 128)
                quantise([W(wst, "wo")], col[:, 5:6], 128 * 128)
            if cfg.get("diff"):
                for g in range(NG):
                    nc.vector.bn_stats(bn[:, g, :], group(xn, g).rearrange("p b t -> p (b t)")).then_inc(s.dve_done, 1)
                    dve.wait_ge(s.dve_done, 1)
                    dve.sem_inc(s.dve_done, -1)
                nc.vector.bn_aggr(col[:, 0:2], bn[:, :, :]).then_inc(s.dve_done, 1)
                dve.wait_ge(s.dve_done, 1)
                dve.sem_inc(s.dve_done, -1)
                nc.vector.tensor_copy(col[:, 2:3], col[:, 1:2]).then_inc(s.dve_done, 1)
                dve.wait_ge(s.dve_done, 1)
                dve.sem_inc(s.dve_done, -1)
                dve.sem_inc(s.bn_var, 1)
                dve.wait_ge(s.bn_dev, 1)
                dve.sem_inc(s.bn_dev, -1)
                nc.vector.reciprocal(col[:, 3:4], col[:, 2:3]).then_inc(s.dve_done, 1)
                dve.wait_ge(s.dve_done, 1)
                dve.sem_inc(s.dve_done, -1)
                nc.vector.tensor_tensor(col[:, 3:4], col[:, 3:4], W(wst, "bn_g"), ALU.mult).then_inc(s.dve_done, 1)
                dve.wait_ge(s.dve_done, 1)
                dve.sem_inc(s.dve_done, -1)
                for g in range(NG):
                    nc.vector.tensor_scalar(group(xn, g), group(xn, g), col[:, 0:1], col[:, 3:4], ALU.subtract, ALU.mult).then_inc(s.dve_done, 1)
                    dve.wait_ge(s.dve_done, 1)
                    dve.sem_inc(s.dve_done, -1)
                    nc.vector.tensor_scalar(group(xn, g), group(xn, g), W(wst, "bn_b"), None, ALU.add).then_inc(s.dve_done, 1)
                    dve.wait_ge(s.dve_done, 1)
                    dve.sem_inc(s.dve_done, -1)
                lam = W(wst, "lam").rearrange("p (k w) -> p k w", w=8)
                for i in range(2):
                    nc.vector.tensor_tensor(y_rms[:, 8 * i:8 * i + 8], lam[0:S, 2 * i, :], lam[0:S, 2 * i + 1, :], ALU.mult).then_inc(s.dve_done, 1)
                    dve.wait_ge(s.dve_done, 1)
                    dve.sem_inc(s.dve_done, -1)
                nc.vector.tensor_reduce(col[0:S, 4:6], y_rms[:, 0:16].rearrange("p (k w) -> p k w", w=8), AX.X, ALU.add).then_inc(s.dve_done, 1)
                dve.wait_ge(s.dve_done, 1)
                dve.sem_inc(s.dve_done, -1)
                dve.sem_inc(s.lam_sum, 1)
                dve.wait_ge(s.lam_exp, 1)
                dve.sem_inc(s.lam_exp, -1)
                nc.vector.tensor_tensor(col[0:S, 6:7], col[0:S, 5:6], col[0:S, 4:5], ALU.subtract).then_inc(s.dve_done, 1)
                dve.wait_ge(s.dve_done, 1)
                dve.sem_inc(s.dve_done, -1)
                nc.vector.tensor_scalar(col[0:S, 6:7], col[0:S, 6:7], -LAMBDA_INIT, None, ALU.add).then_inc(s.dve_done, 1)
                dve.wait_ge(s.dve_done, 1)
                dve.sem_inc(s.dve_done, -1)
            for b in range(GB):
                nc.vector.memset(vaug[:, b, 0:16 * (vw + 1)], 1.0).then_inc(s.dve_done, 1)
                dve.wait_ge(s.dve_done, 1)
                dve.sem_inc(s.dve_done, -1)
            dve.sem_inc(s.stage_act, 1)
            dve.sem_inc(s.stage_pe, 1)
            with dve.Fori(0, NG) as g:
                nc.vector.tensor_copy(bs(xg[:, :]), xn[:, bass.ds(GB * g, GB), :]).then_inc(s.dve_done, 1)
                dve.wait_ge(s.dve_done, 1)
                dve.sem_inc(s.dve_done, -1)
                dve.sem_inc(s.xg_ready, 1)
                if cfg.get("unit"):
                    for m in range(2):
                        dve.wait_ge(s.head_dev, 1)
                        dve.sem_inc(s.head_dev, -1)
                        norm = group(deviation, 0).rearrange("p b t -> p (b t)")
                        nc.vector.tensor_scalar(norm, norm, 1e-8, None, ALU.max).then_inc(s.dve_done, 1)
                        dve.wait_ge(s.dve_done, 1)
                        dve.sem_inc(s.dve_done, -1)
                        nc.vector.reciprocal(norm, norm).then_inc(s.dve_done, 1)
                        dve.wait_ge(s.dve_done, 1)
                        dve.sem_inc(s.dve_done, -1)
                        nc.vector.tensor_tensor(qk[:, m, :], qk[:, m, :], norm, ALU.mult).then_inc(s.dve_done, 1)
                        dve.wait_ge(s.dve_done, 1)
                        dve.sem_inc(s.dve_done, -1)
                        dve.sem_inc(s.unit_done, 1)
                        dve.sem_inc(s.qk_ready, 1)
                if cfg.get("gate"):
                    dve.wait_ge(s.gate_ready, GB)
                    dve.sem_inc(s.gate_ready, -GB)
                    nc.vector.tensor_scalar(gate[:, :], gate[:, :], 1.0, None, ALU.add).then_inc(s.dve_done, 1)
                    dve.wait_ge(s.dve_done, 1)
                    dve.sem_inc(s.dve_done, -1)
                    nc.vector.reciprocal(gate[:, :], gate[:, :]).then_inc(s.dve_done, 1)
                    dve.wait_ge(s.dve_done, 1)
                    dve.sem_inc(s.dve_done, -1)
                    nc.vector.tensor_scalar(gate[:, :], gate[:, :], 0.1, 2.0, ALU.max, ALU.min).then_inc(s.dve_done, 1)
                    dve.wait_ge(s.dve_done, 1)
                    dve.sem_inc(s.dve_done, -1)
                    for b in range(GB):
                        v = vaug[:, b, 0:16 * (vw + 1)].rearrange("p (h w) -> p h w", w=vw + 1)[:, :, 0:vw]
                        nc.vector.tensor_scalar(v, v, gate[:, b:b + 1], None, ALU.mult).then_inc(s.dve_done, 1)
                        dve.wait_ge(s.dve_done, 1)
                        dve.sem_inc(s.dve_done, -1)
                        dve.sem_inc(s.v_ready, 1)
                N = GB * nsm * 2
                for k in range(N + 1):
                    if k < N:
                        dve.wait_ge(s.scores, 1)
                        dve.sem_inc(s.scores, -1)
                        sc = ps[0:S, 2 * (k % 2):2 * (k % 2) + 2, 0:GT].rearrange("p c (h t) -> p c h t", t=S)
                        mx = smax[:, k % 2, :]
                        nc.vector.tensor_reduce(mx.rearrange("p (c h) -> p c h", c=2), sc, AX.X, ALU.max).then_inc(s.dve_done, 1)
                        dve.wait_ge(s.dve_done, 1)
                        dve.sem_inc(s.dve_done, -1)
                        for c in range(2):
                            one = sc[:, c, :, :]
                            ins = nc.vector.tensor_tensor(one, one, mx[:, 4 * c:4 * c + 4].unsqueeze(2).to_broadcast([S, 4, S]), ALU.subtract)
                            if c == 0:
                                ins.then_inc(s.dve_done, 1)
                                dve.wait_ge(s.dve_done, 1)
                                dve.sem_inc(s.dve_done, -1)
                        ins.then_inc(s.dve_done, 1)
                        dve.wait_ge(s.dve_done, 1)
                        dve.sem_inc(s.dve_done, -1)
                        dve.sem_inc(s.shifted, 1)
                    if k % 2 == 0 and k > 0:
                        item = k // 2 - 1
                        b, sm = item // nsm, item % nsm
                        dve.wait_ge(s.o_full, 1)
                        dve.sem_inc(s.o_full, -1)
                        o = bank(7, 16 * (vw + 1), S).rearrange("p (h w) -> p h w", w=vw + 1)
                        y = y_tok[:, b, 0:16 * vw].rearrange("p (h w) -> p h w", w=vw)
                        nc.vector.reciprocal(rden[:, :].unsqueeze(2), o[:, :, vw:vw + 1]).then_inc(s.dve_done, 1)
                        dve.wait_ge(s.dve_done, 1)
                        dve.sem_inc(s.dve_done, -1)
                        r = rden[:, :].unsqueeze(2).to_broadcast([S, 16, vw])
                        if sm == 0:
                            nc.vector.tensor_tensor(y, o[:, :, 0:vw], r, ALU.mult).then_inc(s.dve_done, 1)
                            dve.wait_ge(s.dve_done, 1)
                            dve.sem_inc(s.dve_done, -1)
                            dve.sem_inc(s.o_free, 1)
                        else:
                            y2 = y_sq[:, b, :].rearrange("p (h w) -> p h w", w=vw)
                            nc.vector.tensor_tensor(y2, o[:, :, 0:vw], r, ALU.mult).then_inc(s.dve_done, 1)
                            dve.wait_ge(s.dve_done, 1)
                            dve.sem_inc(s.dve_done, -1)
                            dve.sem_inc(s.o_free, 1)
                            nc.vector.scalar_tensor_tensor(y_tok[:, b, :], y_sq[:, b, :], col[0:S, 6:7], y_tok[:, b, :], ALU.mult, ALU.add).then_inc(s.dve_done, 1)
                            dve.wait_ge(s.dve_done, 1)
                            dve.sem_inc(s.dve_done, -1)
                if cfg.get("diff"):
                    yf = y_tok[:, :, :].rearrange("p b c -> p (b c)")
                    sq = y_sq[:, :, :].rearrange("p b c -> p (b c)")
                    y3 = yf.rearrange("p (h w) -> p h w", w=16)
                    nc.vector.tensor_tensor(sq, yf, yf, ALU.mult).then_inc(s.dve_done, 1)
                    dve.wait_ge(s.dve_done, 1)
                    dve.sem_inc(s.dve_done, -1)
                    nc.vector.tensor_reduce(y_rms[:, :], sq.rearrange("p (h w) -> p h w", w=16), AX.X, ALU.add).then_inc(s.dve_done, 1)
                    dve.wait_ge(s.dve_done, 1)
                    dve.sem_inc(s.dve_done, -1)
                    nc.vector.tensor_scalar(y_rms[:, :], y_rms[:, :], 1 / 16, None, ALU.mult).then_inc(s.dve_done, 1)
                    dve.wait_ge(s.dve_done, 1)
                    dve.sem_inc(s.dve_done, -1)
                    dve.sem_inc(s.rms_sum, 1)
                    dve.wait_ge(s.rms_root, 1)
                    dve.sem_inc(s.rms_root, -1)
                    nc.vector.reciprocal(y_rms[:, :], y_rms[:, :]).then_inc(s.dve_done, 1)
                    dve.wait_ge(s.dve_done, 1)
                    dve.sem_inc(s.dve_done, -1)
                    nc.vector.tensor_scalar(y_rms[:, :], y_rms[:, :], 1 - LAMBDA_INIT, None, ALU.mult).then_inc(s.dve_done, 1)
                    dve.wait_ge(s.dve_done, 1)
                    dve.sem_inc(s.dve_done, -1)
                    nc.vector.tensor_tensor(y3, y3, y_rms[:, :].unsqueeze(2).to_broadcast([S, GB * 16, 16]), ALU.mult).then_inc(s.dve_done, 1)
                    dve.wait_ge(s.dve_done, 1)
                    dve.sem_inc(s.dve_done, -1)
                    nc.vector.tensor_tensor(y3, y3, W(wst, "subln")[0:S, :].unsqueeze(1).to_broadcast([S, GB * 16, 16]), ALU.mult).then_inc(s.dve_done, 1)
                    dve.wait_ge(s.dve_done, 1)
                    dve.sem_inc(s.dve_done, -1)
                dve.sem_inc(s.y_ready, 1)
                dve.wait_ge(s.out_full, 1)
                dve.sem_inc(s.out_full, -1)
                add = group(squares, 0)
                if cfg["bias"]:
                    nc.vector.tensor_scalar(add, bs(bank(7)), W(wst, "bo"), cfg["out_scale"], ALU.add, ALU.mult).then_inc(s.dve_done, 1)
                    dve.wait_ge(s.dve_done, 1)
                    dve.sem_inc(s.dve_done, -1)
                else:
                    nc.vector.tensor_copy(add, bs(bank(7))).then_inc(s.dve_done, 1)
                    dve.wait_ge(s.dve_done, 1)
                    dve.sem_inc(s.dve_done, -1)
                xd = x[:, bass.ds(GB * g, GB), :]
                nc.vector.tensor_tensor(xd, xd, add, ALU.add).then_inc(s.dve_done, 1)
                dve.wait_ge(s.dve_done, 1)
                dve.sem_inc(s.dve_done, -1)
                dve.sem_inc(s.o_free, 1)
            dve.sem_inc(s.stage_pe, 1)

        def cross_attention(n):
            cfg = CROSS[CA[n]]
            H, wst = cfg["H"], CA[n]
            nU = -(-H // 4)
            w = min(H, 4)
            parts = where[wst]
            dve.wait_ge(loaded[wst], 16)
            dve.sem_inc(s.stage_pe, 1)
            folds = [0]

            def fold(to, cols, rows):
                dve.wait_ge(s.side_full, 1)
                dve.sem_inc(s.side_full, -1)
                nc.vector.tensor_copy(to, bank(6 + folds[0] % 2, cols, rows)).then_inc(s.dve_done, 1)
                dve.wait_ge(s.dve_done, 1)
                dve.sem_inc(s.dve_done, -1)
                dve.sem_inc(s.side_free, 1)
                folds[0] += 1

            for h in range(H):
                fold(wfold[:, h * QR:h * QR + QR], QR, 128)
                if "bq" in parts:
                    fold(bfold[:, h:h + 1], 1, QR)
                if "wo" in parts:
                    fold(vfold[:, h * 128:h * 128 + 128], 128, C + 1)
            if "wvo" in parts:
                nc.vector.tensor_copy(vfold[:, 0:128], W(wst, "wvo")).then_inc(s.dve_done, 1)
                dve.wait_ge(s.dve_done, 1)
                dve.sem_inc(s.dve_done, -1)
            if "bo" in parts:
                nc.vector.tensor_copy(col[:, 7:8], W(wst, "bo")).then_inc(s.dve_done, 1)
                dve.wait_ge(s.dve_done, 1)
                dve.sem_inc(s.dve_done, -1)
            dve.sem_inc(s.w_cross_free, 1)
            dve.sem_inc(s.stage_pe, 1)
            dve.sem_inc(s.stage_act, 1)
            dve.sem_inc(s.ctx_bf_free, 1)
            count = [0]

            def side(kind, arg, b, par):
                k = 6 + count[0] % 2
                count[0] += 1
                if kind == "spread":
                    g = arg
                    hs = slice(4 * g, 4 * g + w)
                    dve.wait_ge(s.side_full, 1)
                    dve.sem_inc(s.side_full, -1)
                    nc.vector.reciprocal(u_rec[:, hs, :], bs(bank(k, w * S, C + 1))).then_inc(s.dve_done, 1)
                    dve.wait_ge(s.dve_done, 1)
                    dve.sem_inc(s.dve_done, -1)
                    dve.sem_inc(s.side_free, 1)
                    nc.vector.tensor_tensor(u_rec[:, hs, :], u_rec[:, hs, :], u_raw[:, hs, :], ALU.mult).then_inc(s.dve_done, 1)
                    dve.wait_ge(s.dve_done, 1)
                    dve.sem_inc(s.dve_done, -1)
                    dve.sem_inc(s.u_ready, 1)
                elif kind == "project":
                    dve.wait_ge(s.side_full, 1)
                    dve.sem_inc(s.side_full, -1)
                    xd = x[:, bass.ds(b - 1, 1), :]
                    y = bs(bank(k, S))
                    if "bo" in parts:
                        nc.vector.scalar_tensor_tensor(xd, y, col[:, 7:8], xd, ALU.add, ALU.add).then_inc(s.dve_done, 1)
                        dve.wait_ge(s.dve_done, 1)
                        dve.sem_inc(s.dve_done, -1)
                        dve.sem_inc(s.side_free, 1)
                    else:
                        nc.vector.tensor_tensor(xd, y, xd, ALU.add).then_inc(s.dve_done, 1)
                        dve.wait_ge(s.dve_done, 1)
                        dve.sem_inc(s.dve_done, -1)
                        dve.sem_inc(s.side_free, 1)
                elif kind == "query":
                    g = arg
                    hs = slice(4 * g, 4 * g + w)
                    dve.wait_ge(s.side_full, 1)
                    dve.sem_inc(s.side_full, -1)
                    o, i = qa[1 - par][:, hs, :], bs(bank(k, w * S, QR))
                    if "bq" in parts:
                        ins = nc.vector.tensor_tensor(o, i, bfold[:, hs].unsqueeze(2).to_broadcast([QR, w, S]), ALU.add)
                    else:
                        ins = nc.vector.tensor_copy(o, i)
                    ins.then_inc(s.dve_done, 1)
                    dve.wait_ge(s.dve_done, 1)
                    dve.sem_inc(s.dve_done, -1)
                    dve.sem_inc(s.side_free, 1)
                    dve.sem_inc(s.q_ready, 1)
                elif kind == "chunk":
                    h, c = arg
                    dve.wait_ge(s.side_full, 1)
                    dve.sem_inc(s.side_full, -1)
                    a, z = CHUNKS[c]
                    ins = nc.vector.tensor_reduce(mparts[:, h, c:c + 1], bank(k, z - a, S), AX.X, ALU.max)
                    if (h, c) == (H - 1, 2):
                        ins.then_inc(s.dve_done, 1)
                        dve.wait_ge(s.dve_done, 1)
                        dve.sem_inc(s.dve_done, -1)
                        dve.sem_inc(s.side_free, 1)
                        dve.sem_inc(s.ctx_bf_free, 1)
                        nc.vector.tensor_reduce(mrows[:, C:C + H], mparts[:, 0:H, :], AX.X, ALU.max).then_inc(s.dve_done, 1)
                        dve.wait_ge(s.dve_done, 1)
                        dve.sem_inc(s.dve_done, -1)
                        dve.sem_inc(s.maxima_ready, 1)
                    else:
                        ins.then_inc(s.side_free, 1)
                else:
                    dve.wait_ge(s.side_full, 1)
                    dve.sem_inc(s.side_full, -1)
                    p = slice(C, C + HEADS)
                    nc.vector.tensor_tensor(qa[1 - par][p, 0:H, :], ps[p, k, 0:S].unsqueeze(1).to_broadcast([HEADS, H, S]),
                                            own_head[p, 0:H].unsqueeze(2).to_broadcast([HEADS, H, S]), ALU.mult).then_inc(s.dve_done, 1)
                    dve.wait_ge(s.dve_done, 1)
                    dve.sem_inc(s.dve_done, -1)
                    dve.sem_inc(s.side_free, 1)
                    dve.sem_inc(s.qa_ready, 1)

            own_head = W("const", "own_head")

            def batch(b, par, prep, tail):
                for kind, arg in side_items(H, prep, tail):
                    side(kind, arg, b, par)
            batch(-1, 1, True, False)
            batch(0, 0, True, False)
            assert count[0] % 2 == 0 or True
            c0 = count[0]
            with dve.Fori(0, B // 2 - 1) as i:
                batch(2 * i + 1, 1, True, True)
                batch(2 * i + 2, 0, True, True)
            assert (count[0] - c0) % 2 == 0
            batch(B - 1, 1, False, True)
            batch(B, 0, False, True)
            dve.sem_inc(s.stage_pe, 1)

        def route(n):
            cfg = FEED[FF[n]]
            E = cfg["E"]
            dve.wait_ge(s.logits_ready, 1)
            dve.sem_inc(s.logits_ready, -1)
            lg, bi, rk, wt = (t[:, :, 0:E] for t in (logits, biased, rank, weight))
            nc.vector.tensor_copy(lg, ps[0:S, 0, 0:B * E].rearrange("p (b e) -> p b e", e=E)).then_inc(s.dve_done, 1)
            dve.wait_ge(s.dve_done, 1)
            dve.sem_inc(s.dve_done, -1)
            by = lg
            if cfg.get("sigmoid"):
                nc.vector.tensor_tensor(bi, lg, W(FF[n], "expert_b")[0:S, :].unsqueeze(1).to_broadcast([S, B, E]), ALU.add).then_inc(s.dve_done, 1)
                dve.wait_ge(s.dve_done, 1)
                dve.sem_inc(s.dve_done, -1)
                by = bi
            else:
                nc.vector.tensor_reduce(best[:, :], lg, AX.X, ALU.max).then_inc(s.dve_done, 1)
                dve.wait_ge(s.dve_done, 1)
                dve.sem_inc(s.dve_done, -1)
                nc.vector.tensor_tensor(lg, lg, best[:, :].unsqueeze(2).to_broadcast([S, B, E]), ALU.subtract).then_inc(s.dve_done, 1)
                dve.wait_ge(s.dve_done, 1)
                dve.sem_inc(s.dve_done, -1)
            dve.sem_inc(s.weights_asked, 1)
            p1 = pairs[:, 0:B * E * E].rearrange("p (b e f) -> p b e f", e=E, f=E)
            p2 = pairs2[:, 0:B * E * E].rearrange("p (b e f) -> p b e f", e=E, f=E)
            mine, other = by.unsqueeze(3).to_broadcast([S, B, E, E]), by.unsqueeze(2).to_broadcast([S, B, E, E])
            before = W("const", "before")[0:S, :].rearrange("p (e f) -> p e f", f=16)[:, 0:E, 0:E]
            nc.vector.tensor_tensor(p1, other, mine, ALU.is_equal).then_inc(s.dve_done, 1)
            dve.wait_ge(s.dve_done, 1)
            dve.sem_inc(s.dve_done, -1)
            nc.vector.tensor_tensor(p1, p1, before.unsqueeze(1).to_broadcast([S, B, E, E]), ALU.mult).then_inc(s.dve_done, 1)
            dve.wait_ge(s.dve_done, 1)
            dve.sem_inc(s.dve_done, -1)
            nc.vector.tensor_tensor(p2, other, mine, ALU.is_gt).then_inc(s.dve_done, 1)
            dve.wait_ge(s.dve_done, 1)
            dve.sem_inc(s.dve_done, -1)
            nc.vector.tensor_tensor(p1, p1, p2, ALU.add).then_inc(s.dve_done, 1)
            dve.wait_ge(s.dve_done, 1)
            dve.sem_inc(s.dve_done, -1)
            nc.vector.tensor_reduce(rk, p1, AX.X, ALU.add).then_inc(s.dve_done, 1)
            dve.wait_ge(s.dve_done, 1)
            dve.sem_inc(s.dve_done, -1)
            nc.vector.tensor_scalar(rk, rk, 2.0, None, ALU.is_lt).then_inc(s.dve_done, 1)
            dve.wait_ge(s.dve_done, 1)
            dve.sem_inc(s.dve_done, -1)
            dve.wait_ge(s.weights_exp, 1)
            dve.sem_inc(s.weights_exp, -1)
            if cfg.get("sigmoid"):
                nc.vector.tensor_scalar(wt, wt, 1.0, None, ALU.add).then_inc(s.dve_done, 1)
                dve.wait_ge(s.dve_done, 1)
                dve.sem_inc(s.dve_done, -1)
                nc.vector.reciprocal(wt, wt).then_inc(s.dve_done, 1)
                dve.wait_ge(s.dve_done, 1)
                dve.sem_inc(s.dve_done, -1)
            nc.vector.tensor_tensor(wt, wt, rk, ALU.mult).then_inc(s.dve_done, 1)
            dve.wait_ge(s.dve_done, 1)
            dve.sem_inc(s.dve_done, -1)
            nc.vector.tensor_reduce(best[:, :], wt, AX.X, ALU.add).then_inc(s.dve_done, 1)
            dve.wait_ge(s.dve_done, 1)
            dve.sem_inc(s.dve_done, -1)
            if cfg.get("sigmoid"):
                nc.vector.tensor_scalar(best[:, :], best[:, :], 1e-10, None, ALU.add).then_inc(s.dve_done, 1)
                dve.wait_ge(s.dve_done, 1)
                dve.sem_inc(s.dve_done, -1)
            nc.vector.reciprocal(best[:, :], best[:, :]).then_inc(s.dve_done, 1)
            dve.wait_ge(s.dve_done, 1)
            dve.sem_inc(s.dve_done, -1)
            nc.vector.tensor_tensor(wt, wt, best[:, :].unsqueeze(2).to_broadcast([S, B, E]), ALU.mult).then_inc(s.dve_done, 1)
            dve.wait_ge(s.dve_done, 1)
            dve.sem_inc(s.dve_done, -1)
            dve.sem_inc(s.weights_ready, 1)

        def impulse_response():
            p = {k: W("tk", k) for k in ("A_re", "A_im", "C_re", "C_im", "log_dt")}
            dt, z = col[:, 0:1], col[:, 1:2]
            row = [ssm[:, i, :] for i in range(12)]

            def tt(o, a, b, op):
                nc.vector.tensor_tensor(o, a, b, op).then_inc(s.dve_done, 1)
                dve.wait_ge(s.dve_done, 1)
                dve.sem_inc(s.dve_done, -1)

            def ts(o, a, c1, c2, op1, op2):
                nc.vector.tensor_scalar(o, a, c1, c2, op1, op2).then_inc(s.dve_done, 1)
                dve.wait_ge(s.dve_done, 1)
                dve.sem_inc(s.dve_done, -1)

            ts(z, p["log_dt"], 1 / 32, None, ALU.mult, ALU.bypass)
            ts(dt, z, 1 / math.factorial(8), 1 / math.factorial(7), ALU.mult, ALU.add)
            for k in range(6, -1, -1):
                ts(dt, dt, z, 1 / math.factorial(k), ALU.mult, ALU.add)
            for _ in range(5):
                tt(dt, dt, dt, ALU.mult)
            ts(row[1], p["A_im"], dt, None, ALU.mult, ALU.bypass)
            ts(row[4], row[1], 1 / (2 * math.pi), ROUND, ALU.mult, ALU.add)
            ts(row[4], row[4], ROUND, None, ALU.subtract, ALU.bypass)
            part1 = 6.28125
            part2 = float(np.float32(np.round((2 * math.pi - part1) * 2 ** 20) / 2 ** 20))
            for part in (part1, part2, 2 * math.pi - part1 - part2):
                ts(row[5], row[4], part, None, ALU.mult, ALU.bypass)
                tt(row[1], row[1], row[5], ALU.subtract)
            ts(row[2], row[1], math.pi / 2, None, ALU.add, ALU.bypass)
            ts(row[5], row[2], math.pi, 2 * math.pi, ALU.is_gt, ALU.mult)
            tt(row[2], row[2], row[5], ALU.subtract)
            ts(row[2], row[2], 3.1415925, -3.1415925, ALU.min, ALU.max)
            ts(row[3], row[1], 3.1415925, -3.1415925, ALU.min, ALU.max)
            dve.sem_inc(s.angles, 1)
            ts(row[0], p["A_re"], dt, None, ALU.mult, ALU.bypass)
            dve.sem_inc(s.decays, 1)
            dve.wait_ge(s.rotation, 2)
            dve.sem_inc(s.rotation, -2)
            w1r, w1i = powers[0][0][:, 1, :], powers[0][1][:, 1, :]
            tt(w1r, row[0], row[2], ALU.mult)
            tt(w1i, row[0], row[3], ALU.mult)
            ts(row[4], w1r, -1.0, None, ALU.add, ALU.bypass)
            tt(row[5], p["C_re"], row[4], ALU.mult)
            tt(row[6], p["C_im"], w1i, ALU.mult)
            tt(row[5], row[5], row[6], ALU.subtract)
            tt(row[6], p["C_re"], w1i, ALU.mult)
            tt(row[7], p["C_im"], row[4], ALU.mult)
            tt(row[6], row[6], row[7], ALU.add)
            tt(row[7], p["A_re"], p["A_re"], ALU.mult)
            tt(row[8], p["A_im"], p["A_im"], ALU.mult)
            tt(row[7], row[7], row[8], ALU.add)
            nc.vector.reciprocal(row[7], row[7]).then_inc(s.dve_done, 1)
            dve.wait_ge(s.dve_done, 1)
            dve.sem_inc(s.dve_done, -1)
            ts(row[7], row[7], 2.0, None, ALU.mult, ALU.bypass)
            tt(row[8], row[5], p["A_re"], ALU.mult)
            tt(row[9], row[6], p["A_im"], ALU.mult)
            tt(row[8], row[8], row[9], ALU.add)
            tt(row[8], row[8], row[7], ALU.mult)
            tt(row[9], row[6], p["A_re"], ALU.mult)
            tt(row[10], row[5], p["A_im"], ALU.mult)
            tt(row[9], row[9], row[10], ALU.subtract)
            tt(row[9], row[9], row[7], ALU.mult)

            def times(o, a, b, n):
                t0, t1 = (t.rearrange("p (r k) -> p r k", k=STATES)[:, 0:n, :] for t in scratch[:2])
                tt(t0, a[0], b[0], ALU.mult)
                tt(t1, a[1], b[1], ALU.mult)
                t2 = scratch[2].rearrange("p (r k) -> p r k", k=STATES)[:, 0:n, :]
                tt(t2, a[0], b[1], ALU.mult)
                tt(t0, t0, t1, ALU.subtract)
                tt(t1, a[1], b[0], ALU.mult)
                tt(o[1], t2, t1, ALU.add)
                nc.vector.tensor_copy(o[0], t0).then_inc(s.dve_done, 1)
                dve.wait_ge(s.dve_done, 1)
                dve.sem_inc(s.dve_done, -1)

            for base in range(2):
                P = powers[base]
                nc.vector.memset(P[0][:, 0, :], 1.0).then_inc(s.dve_done, 1)
                dve.wait_ge(s.dve_done, 1)
                dve.sem_inc(s.dve_done, -1)
                nc.vector.memset(P[1][:, 0, :], 0.0).then_inc(s.dve_done, 1)
                dve.wait_ge(s.dve_done, 1)
                dve.sem_inc(s.dve_done, -1)
                if base == 1:
                    for part in range(2):
                        nc.vector.tensor_copy(P[part][:, 1, :], powers[0][part][:, LAGS, :]).then_inc(s.dve_done, 1)
                        dve.wait_ge(s.dve_done, 1)
                        dve.sem_inc(s.dve_done, -1)
                have = 1
                while have < LAGS:
                    n = min(have, LAGS - have)
                    times([q[:, have + 1:have + 1 + n, :] for q in P], [q[:, 1:1 + n, :] for q in P],
                          [q[:, have:have + 1, :].to_broadcast([128, n, STATES]) for q in P], n)
                    have += n
            P = powers[1]
            times([q[:, 0:LAGS, :] for q in P], [q[:, 0:LAGS, :] for q in P],
                  [row[i].unsqueeze(1).to_broadcast([128, LAGS, STATES]) for i in (8, 9)], LAGS)
            v = [q.rearrange("p (a b) k -> p a b k", b=LAGS) for q in prods]
            for part in range(2):
                tt(v[part], powers[1][part][:, 0:LAGS, :].unsqueeze(2).to_broadcast([128, LAGS, LAGS, STATES]),
                   powers[0][part][:, 0:LAGS, :].unsqueeze(1).to_broadcast([128, LAGS, LAGS, STATES]), ALU.mult)
            tt(prods[0], prods[0], prods[1], ALU.subtract)
            nc.vector.tensor_reduce(kernel_l[:, :], prods[0], AX.X, ALU.add).then_inc(s.dve_done, 1)
            dve.wait_ge(s.dve_done, 1)
            dve.sem_inc(s.dve_done, -1)

        def film_block(layernorm, feed_forward):
            layernorm(x)
            dve.wait_ge(loaded["tk"], 16)
            impulse_response()
            nc.vector.tensor_copy(mid[:, :, :], xn[:, :, :]).then_inc(s.dve_done, 1)
            dve.wait_ge(s.dve_done, 1)
            dve.sem_inc(s.dve_done, -1)
            dve.sem_inc(s.stage_pe, 1)
            dve.sem_inc(s.stage_act, 1)
            dve.sem_inc(s.masks_asked, 1)
            for h in range(TH):
                dve.wait_ge(s.side_full, 1)
                dve.sem_inc(s.side_full, -1)
                nc.vector.tensor_copy(wf4[:, h * C:h * C + C], bank(6 + h % 2, C)).then_inc(s.dve_done, 1)
                dve.wait_ge(s.dve_done, 1)
                dve.sem_inc(s.dve_done, -1)
                dve.sem_inc(s.side_free, 1)
            dve.sem_inc(s.stage_pe, 1)

            def head(h, last):
                dve.wait_ge(s.scores_there, 1)
                dve.sem_inc(s.scores_there, -1)
                sc = scores_sb[h % 2]
                nc.vector.max(top8[:, 0, :], sc).then_inc(s.dve_done, 1)
                dve.wait_ge(s.dve_done, 1)
                dve.sem_inc(s.dve_done, -1)
                nc.vector.tensor_scalar(low[:, h % 2:h % 2 + 1], top8[:, 0, 0:1], -1.0, None, ALU.mult).then_inc(s.dve_done, 1)
                dve.wait_ge(s.dve_done, 1)
                dve.sem_inc(s.dve_done, -1)
                dve.sem_inc(s.low_ready, 1)
                for r in range(TOP // 8):
                    if r:
                        nc.vector.max(top8[:, r, :], left).then_inc(s.dve_done, 1)
                        dve.wait_ge(s.dve_done, 1)
                        dve.sem_inc(s.dve_done, -1)
                    nc.vector.match_replace(left, top8[:, r, :], sc if r == 0 else left, TAKEN).then_inc(s.dve_done, 1)
                    dve.wait_ge(s.dve_done, 1)
                    dve.sem_inc(s.dve_done, -1)
                dve.wait_ge(s.expd_ready, 1)
                dve.sem_inc(s.expd_ready, -1)
                if h == 0:
                    dve.wait_ge(s.kept_free, 1)
                    dve.sem_inc(s.kept_free, -1)
                nc.vector.scalar_tensor_tensor(kept[:, h, :], left, TAKEN, expd[h % 2], ALU.is_equal, ALU.mult,
                                               accum_out=den[:, h:h + 1]).then_inc(s.dve_done, 1)
                dve.wait_ge(s.dve_done, 1)
                dve.sem_inc(s.dve_done, -1)
                dve.sem_inc(s.scores_sb_free, 1)
                nc.vector.reciprocal(den[:, h:h + 1], den[:, h:h + 1]).then_inc(s.dve_done, 1)
                dve.wait_ge(s.dve_done, 1)
                dve.sem_inc(s.dve_done, -1)
                nc.vector.tensor_scalar(turn_scale[:, h, :], W("const", "ident")[0:S, 0:S], den[:, h:h + 1], 1 / TH,
                                        ALU.mult, ALU.mult).then_inc(s.dve_done, 1)
                dve.wait_ge(s.dve_done, 1)
                dve.sem_inc(s.dve_done, -1)
                dve.sem_inc(s.kept_ready, 1)
            dve.sem_inc(s.kept_free, 1)
            dve.sem_inc(s.scores_sb_free, 2)
            with dve.Fori(0, B) as i:
                for h in range(TH):
                    head(h, False)
            dve.wait_ge(s.kept_free, 1)
            dve.sem_inc(s.kept_free, -1)
            dve.wait_ge(s.ct_ready, 1)
            dve.sem_inc(s.ct_ready, -1)
            dve.wait_ge(s.text_mask_loaded, 16)
            dve.sem_inc(s.text_mask_loaded, -16)
            nc.vector.tensor_tensor(ct[:, :, :].rearrange("p b t -> p (b t)"), ct[:, :, :].rearrange("p b t -> p (b t)"),
                                    text_mask.bitcast(U8), ALU.mult).then_inc(s.dve_done, 1)
            dve.wait_ge(s.dve_done, 1)
            dve.sem_inc(s.dve_done, -1)
            dve.sem_inc(s.stage_pe, 1)
            layernorm(mid, affine=(W("tk", "g_in"), W("tk", "b_in")))
            modulate("film_in", xn)
            y = squares
            nc.vector.tensor_scalar(y[:, :, :], xn[:, :, :], W("tk", "skip"), None, ALU.mult).then_inc(s.dve_done, 1)
            dve.wait_ge(s.dve_done, 1)
            dve.sem_inc(s.dve_done, -1)
            for j in range(S):
                nc.vector.scalar_tensor_tensor(y[:, :, j:S], xn[:, :, 0:S - j], kernel_l[:, j:j + 1], y[:, :, j:S],
                                               ALU.mult, ALU.add).then_inc(s.dve_done, 1)
                dve.wait_ge(s.dve_done, 1)
                dve.sem_inc(s.dve_done, -1)
            modulate("film_out", y)
            nc.vector.tensor_tensor(mid[:, :, :], mid[:, :, :], y[:, :, :], ALU.add).then_inc(s.dve_done, 1)
            dve.wait_ge(s.dve_done, 1)
            dve.sem_inc(s.dve_done, -1)
            dve.sem_inc(s.stage_pe, 1)
            layernorm(mid, affine=(W("tk", "g_ffn"), W("tk", "b_ffn")))
            feed_forward(3)
            layernorm(xn, affine=(W("tk", "g_out"), W("tk", "b_out")), add=True)

        def modulate(name, t):
            bias, mod = W("tk", "b_" + name), W("tk", "mod")
            for g in range(NG):
                dve.wait_ge(s.film_full, 1)
                dve.sem_inc(s.film_full, -1)
                for c in range(2):
                    f = group(deviation, g)
                    nc.vector.tensor_scalar(f, bs(bank(2 * (g % 2) + c)), bias[:, c:c + 1], mod, ALU.add, ALU.mult).then_inc(s.dve_done, 1)
                    dve.wait_ge(s.dve_done, 1)
                    dve.sem_inc(s.dve_done, -1)
                    if c == 0:
                        nc.vector.scalar_tensor_tensor(group(t, g), f, 1.0, group(t, g), ALU.add, ALU.mult).then_inc(s.dve_done, 1)
                        dve.wait_ge(s.dve_done, 1)
                        dve.sem_inc(s.dve_done, -1)
                    else:
                        nc.vector.tensor_tensor(group(t, g), group(t, g), f, ALU.add).then_inc(s.dve_done, 1)
                        dve.wait_ge(s.dve_done, 1)
                        dve.sem_inc(s.dve_done, -1)
                dve.sem_inc(s.film_free, 1)

        def feed_forward(n):
            cfg = FEED[FF[n]]
            dve.wait_ge(loaded[FF[n]], 16)
            dve.sem_inc(s.stage_pe, 1)
            dve.sem_inc(s.stage_act, 1)
            if cfg["gate"]:
                route(n)
                for g in range(NG):
                    dve.sem_inc(gate_free[g], 1)

            def block(chunks, gated):
                for u in range(NG * len(chunks)):
                    c, g = chunks[u // NG], u % NG
                    dve.wait_ge(s.h_act_ready, 1)
                    dve.sem_inc(s.h_act_ready, -1)
                    if gated and (c == 0 or cfg["gate"] == "chunk"):
                        dve.wait_ge(gate_loaded[g], 16 if cfg["gate"] == "block" else 32)
                        dve.sem_inc(gate_loaded[g], -(16 if cfg["gate"] == "block" else 32))
                    up2 = bank(2 + u % 2)
                    to = h_all[u % 2]
                    if cfg.get("hidden_bias"):
                        ins = nc.vector.scalar_tensor_tensor(to, up2, chunk[c][:, 385:386], h_act[u % 2], ALU.add, ALU.mult)
                    else:
                        ins = nc.vector.tensor_tensor(to, up2, h_act[u % 2], ALU.mult)
                    if gated:
                        ins.then_inc(s.dve_done, 1)
                        dve.wait_ge(s.dve_done, 1)
                        dve.sem_inc(s.dve_done, -1)
                        ins = nc.vector.tensor_tensor(to, to, gate_rows[g], ALU.mult)
                        if c == 3 or cfg["gate"] == "chunk":
                            ins.then_inc(s.dve_done, 1)
                            dve.wait_ge(s.dve_done, 1)
                            dve.sem_inc(s.dve_done, -1)
                            dve.sem_inc(s.h_ready, 1)
                            dve.sem_inc(gate_free[g], 1)
                            continue
                    ins.then_inc(s.h_ready, 1)
            if cfg["up2"]:
                if cfg["loop"]:
                    with dve.Fori(0, cfg["loop"]) as i:
                        block(range(4), True)
                block(range(cfg["last"]), cfg["last"] == 4)
            for g in range(NG):
                dve.wait_ge(s.down_done, 1)
                dve.sem_inc(s.down_done, -1)
                xd = group(x, g)
                if n in (2, 3):
                    nc.vector.tensor_tensor(group(xn, g), bs(bank(4 + g)), group(xn if n == 2 else mid, g), ALU.add).then_inc(s.dve_done, 1)
                    dve.wait_ge(s.dve_done, 1)
                    dve.sem_inc(s.dve_done, -1)
                else:
                    nc.vector.tensor_tensor(xd, bs(bank(4 + g)), xd, ALU.add).then_inc(s.dve_done, 1)
                    dve.wait_ge(s.dve_done, 1)
                    dve.sem_inc(s.dve_done, -1)
            dve.sem_inc(s.stage_pe, 1)

        dve.sem_inc(s.o_free, 1)
        dve.sem_inc(s.side_free, 2)
        dve.wait_ge(s.x_loaded, 16)
        dve.wait_ge(loaded["const"], 16)
        dve.wait_ge(loaded["sa0"], 16)
        for i, v in enumerate((1e-5, 1e-6)):
            nc.vector.memset(eps[:, i:i + 1], v).then_inc(s.dve_done, 1)
            dve.wait_ge(s.dve_done, 1)
            dve.sem_inc(s.dve_done, -1)
        nc.vector.memset(mrows[:, :], 0.0).then_inc(s.dve_done, 1)
        dve.wait_ge(s.dve_done, 1)
        dve.sem_inc(s.dve_done, -1)
        for i in range(2):
            nc.vector.memset(ctxT[i][C:QR, :], 1.0).then_inc(s.dve_done, 1)
            dve.wait_ge(s.dve_done, 1)
            dve.sem_inc(s.dve_done, -1)
            nc.vector.memset(ctxk[i][:, :, C:C + 1], 1.0).then_inc(s.dve_done, 1)
            dve.wait_ge(s.dve_done, 1)
            dve.sem_inc(s.dve_done, -1)
        nc.vector.tensor_copy(ident_bf[:, :], W("const", "ident")).then_inc(s.dve_done, 1)
        dve.wait_ge(s.dve_done, 1)
        dve.sem_inc(s.dve_done, -1)
        nc.vector.memset(ones_bf[:, :], 1.0).then_inc(s.dve_done, 1)
        dve.wait_ge(s.dve_done, 1)
        dve.sem_inc(s.dve_done, -1)
        dve.sem_inc(s.film_free, 2)
        nc.vector.tensor_copy(causal_bf[:, :], W("const", "causal")).then_inc(s.dve_done, 1)
        dve.wait_ge(s.dve_done, 1)
        dve.sem_inc(s.dve_done, -1)
        dve.sem_inc(s.start_act, 1)
        dve.sem_inc(s.w_cross_free, 1)
        dve.sem_inc(ctx_free[0], 1)
        dve.sem_inc(ctx_free[1], 1)
        dve.sem_inc(s.stage_pe, 1)
        stages(layernorm, self_attention, cross_attention, feed_forward, film_block)
        dve.sem_inc(s.x_final, 1)

    @block.tensor
    def _(pe):
        mm = nc.tensor.matmul
        ident = W("const", "ident")

        def layernorm(src, eps=0, affine=None, add=False):
            pe.wait_ge(s.stage_pe, 1)
            pe.sem_inc(s.stage_pe, -1)
            for g in range(NG):
                mm(bank(g), W("const", "mean"), group(src, g), start=True, stop=True).then_inc(s.mean, 1)
            for g in range(NG):
                pe.wait_ge(s.squared, 1)
                pe.sem_inc(s.squared, -1)
                mm(bank(4 + g), W("const", "mean"), group(squares, g), start=True, stop=True).then_inc(s.variance, 1)

        def self_attention(n):
            cfg = SELF[SA[n]]
            nsm, vw, wst = cfg["nsm"], cfg["vw"], SA[n]
            pe.wait_ge(s.stage_pe, 1)
            pe.sem_inc(s.stage_pe, -1)
            if cfg.get("quant"):
                pe.wait_ge(s.magnitudes, 1)
                pe.sem_inc(s.magnitudes, -1)
                mm(ps[:, 0, 0:3], W("const", "ones"), col[:, 0:3], start=True, stop=True).then_inc(s.totals, 1)
            pe.wait_ge(s.stage_pe, 1)
            pe.sem_inc(s.stage_pe, -1)
            wqk, wv, wo = W(wst, "wqk"), W(wst, "wv"), W(wst, "wo")
            N = GB * nsm * 2

            def scores(k):
                b, sm, half = k // (2 * nsm), k // 2 % nsm, k % 2
                for c in range(2):
                    if cfg["causal"]:
                        mm(bank(2 * (k % 2) + c, GT, S), ident_bf[0:S, 0:S], causal_bf[:, :], start=True, stop=False)
                    h = HEADS * sm + 8 * half + 4 * c
                    last = mm(bank(2 * (k % 2) + c, GT, S), qk[:, 2 * sm, b * S:b * S + S], km[:, h:h + 4, b * S:b * S + S],
                              start=not cfg["causal"], stop=True)
                last.then_inc(s.scores, 1)

            def turn(k):
                pe.wait_ge(s.probs_ready, 1)
                pe.sem_inc(s.probs_ready, -1)
                for c in range(2):
                    for j in range(4):
                        at = c * GT + j * S
                        last = nc.tensor.transpose(bank(4 + c, S, S, j * S), probs[:, k % 2, at:at + S], ident[0:S, 0:S])
                    last.then_inc(s.turned, 1)

            def values(k):
                b, half = k // (2 * nsm), k % 2
                if half == 0:
                    pe.wait_ge(s.o_free, 1)
                    pe.sem_inc(s.o_free, -1)
                for c in range(2):
                    pe.wait_ge(s.probsT_ready, 1)
                    pe.sem_inc(s.probsT_ready, -1)
                    for j in range(4):
                        h = 8 * half + 4 * c + j
                        last = mm(bank(7, vw + 1, S, h * (vw + 1)), probsT[:, k % 2, c * GT + j * S:c * GT + j * S + S],
                                  vaug[:, b, h * (vw + 1):(h + 1) * (vw + 1)], start=True, stop=True)
                if half == 1:
                    last.then_inc(s.o_full, 1)

            with pe.Fori(0, NG) as g:
                pe.wait_ge(s.xg_ready, 1)
                pe.sem_inc(s.xg_ready, -1)
                for m in range(2 * nsm):
                    pe.wait_ge(s.proj_free, 1)
                    pe.sem_inc(s.proj_free, -1)
                    mm(bank(6), wqk[:, m * 128:m * 128 + 128], xg[:, :], start=True, stop=True).then_inc(s.proj_full, 1)
                    if cfg.get("unit"):
                        if m == 0:
                            pe.wait_ge(s.o_free, 1)
                            pe.sem_inc(s.o_free, -1)
                        pe.wait_ge(s.head_sq, 1)
                        pe.sem_inc(s.head_sq, -1)
                        mm(bank(7), W("const", "head_rows"), group(squares, 0), start=True, stop=True).then_inc(s.head_norm, 1)
                        pe.wait_ge(s.qk_ready, 1)
                        pe.sem_inc(s.qk_ready, -1)
                        if m == 1:
                            pe.sem_inc(s.o_free, 1)
                for b in range(GB):
                    pe.wait_ge(s.proj_free, 1)
                    pe.sem_inc(s.proj_free, -1)
                    vc = wv.shape[1]
                    if cfg["bias"]:
                        mm(bank(6, vc, S), W("const", "ones")[0:1, 0:S], W(wst, "bv"), start=True, stop=False)
                    mm(bank(6, vc, S), xg[:, b * S:b * S + S], wv, start=not cfg["bias"], stop=True).then_inc(s.proj_full, 1)
                for b in range(GB):
                    pe.wait_ge(s.v_ready, 1)
                    pe.sem_inc(s.v_ready, -1)
                pe.wait_ge(s.km_act, nsm)
                pe.sem_inc(s.km_act, -nsm)
                pe.wait_ge(s.km_pool, nsm)
                pe.sem_inc(s.km_pool, -nsm)
                scores(0)
                scores(1)
                for k in range(N + 1):
                    if k > 0:
                        values(k - 1)
                    if k < N:
                        turn(k)
                    if k + 2 < N:
                        scores(k + 2)
                pe.wait_ge(s.y_ready, 1)
                pe.sem_inc(s.y_ready, -1)
                for c in range(vw // 8):
                    pe.wait_ge(s.proj_free, 1)
                    pe.sem_inc(s.proj_free, -1)
                    for b in range(GB):
                        last = nc.tensor.transpose(bank(6, S, 128, b * S), y_tok[:, b, 128 * c:128 * c + 128], ident[0:S, 0:S])
                    last.then_inc(s.y_turned, 1)
                pe.wait_ge(s.o_free, 1)
                pe.sem_inc(s.o_free, -1)
                for c in range(vw // 8):
                    pe.wait_ge(s.y_feat_ready, 1)
                    pe.sem_inc(s.y_feat_ready, -1)
                    last = mm(bank(7), wo[:, 128 * c:128 * c + 128], y_feat[:, c, :], start=c == 0, stop=c == vw // 8 - 1)
                last.then_inc(s.out_full, 1)

        def cross_attention(n):
            cfg = CROSS[CA[n]]
            H, hd, wst = cfg["H"], cfg["hd"], CA[n]
            nU, w = -(-H // 4), min(H, 4)
            parts = where[wst]
            pe.wait_ge(s.stage_pe, 1)
            pe.sem_inc(s.stage_pe, -1)
            pe.wait_ge(s.stage_pe, 1)
            pe.sem_inc(s.stage_pe, -1)
            folds = [0]

            def fold(cols, rows, lhsT, rhs):
                pe.wait_ge(s.side_free, 1)
                pe.sem_inc(s.side_free, -1)
                mm(bank(6 + folds[0] % 2, cols, rows), lhsT, rhs, start=True, stop=True).then_inc(s.side_full, 1)
                folds[0] += 1

            for h in range(H):
                wk = W(wst, "wk")[:, h * QR:h * QR + QR]
                wq = W(wst, "wq")[:, h * 128:h * 128 + 128]
                fold(QR, 128, wq, wk)
                if "bq" in parts:
                    fold(1, QR, wk, W(wst, "bq")[:, h:h + 1])
                if "wo" in parts:
                    fold(128, C + 1, W(wst, "wv")[:, h * 97:h * 97 + 97], W(wst, "wo")[:, h * 128:h * 128 + 128])
            pe.wait_ge(s.stage_pe, 1)
            pe.sem_inc(s.stage_pe, -1)
            count = [0]

            def side(kind, arg, b, par):
                k = 6 + count[0] % 2
                count[0] += 1
                if kind == "maxima":
                    pe.wait_ge(s.maxima_ready, 1)
                    pe.sem_inc(s.maxima_ready, -1)
                if kind == "project":
                    pe.wait_ge(s.u_ready, nU)
                    pe.sem_inc(s.u_ready, -nU)
                if kind == "chunk" and arg == (0, 0):
                    pe.wait_ge(s.ctx_bf, 1)
                    pe.sem_inc(s.ctx_bf, -1)
                    pe.wait_ge(s.q_bf, nU)
                    pe.sem_inc(s.q_bf, -nU)
                pe.wait_ge(s.side_free, 1)
                pe.sem_inc(s.side_free, -1)
                if kind == "spread":
                    g = arg
                    ins = mm(bank(k, w * S, C + 1), W("const", "row96"), u_raw[:, 4 * g:4 * g + w, :], start=True, stop=True)
                elif kind == "project":
                    for h in range(H):
                        ins = mm(bank(k, S), vfold[:, h * 128:h * 128 + 128], u_rec[:, h, :], start=h == 0, stop=h == H - 1)
                elif kind == "query":
                    for j in range(w):
                        h = 4 * arg + j
                        ins = mm(bank(k, S, QR, j * S), wfold[:, h * QR:h * QR + QR], xn[:, bass.ds(b + 1, 1), :], start=True, stop=True)
                elif kind == "chunk":
                    h, c = arg
                    a, z = CHUNKS[c]
                    ins = mm(bank(k, z - a, S), qa_bf[:, h, :], ctxT_bf[:, a:z], start=True, stop=True)
                else:
                    ins = nc.tensor.transpose(bank(k, S, C + HEADS), mrows[:, :], ident[0:S, 0:S])
                ins.then_inc(s.side_full, 1)

            def batch(b, par, prep, tail, main=True, first=False):
                us = units(H) if main else []
                items = side_items(H, prep, tail)
                lead = 2 if H > 1 else len(us)
                at = {}
                for i, it in enumerate(items):
                    p = lead + i * max(1, len(us) - 4 - lead) // len(items) if H > 1 and main else len(us)
                    if H == 1 and main and it[0] in ("spread", "project"):
                        p = 1
                    at.setdefault(p, []).append(it)

                def scoresT(u):
                    if u == 0:
                        pe.wait_ge(s.qa_ready, 1)
                        pe.sem_inc(s.qa_ready, -1)
                    for t, pc, h0, nh, g in us[u]:
                        r = key_rows_of(t)
                        ins = mm(bank(u % 2, nh * S, r, pc), ctxT[par][:, 128 * t:128 * t + r], qa[par][:, h0:h0 + nh, :] if H > 1 else qa[par][:, 0, :],
                                 start=True, stop=True)
                    ins.then_inc(s.scoresT, 1)

                def values(u):
                    pe.wait_ge(s.pexp_ready, 1)
                    pe.sem_inc(s.pexp_ready, -1)
                    for t, pc, h0, nh, g in us[u]:
                        r = key_rows_of(t)
                        if t == 0 and not first:
                            pe.wait_ge(s.u_raw_ready, 1)
                            pe.sem_inc(s.u_raw_ready, -1)
                        ins = mm(bank(2 + g, nh * S, C + 1), ctxk[par][0:r, t, :], pexp[u % 3][0:r, pc:pc + nh * S],
                                 start=t == 0, stop=t == KT - 1, skip_group_check=True)
                        if t == KT - 1:
                            ins.then_inc(s.u_full, 1)
                if main:
                    scoresT(0)
                    scoresT(1)
                else:
                    if not prep:
                        pe.wait_ge(s.u_raw_ready, nU)
                        pe.sem_inc(s.u_raw_ready, -nU)
                for u in range(len(us)):
                    values(u)
                    if u + 2 < len(us):
                        scoresT(u + 2)
                    for it in at.get(u, []):
                        side(*it, b, par)
                for p in sorted(at):
                    if p >= len(us):
                        for it in at[p]:
                            side(*it, b, par)

            batch(-1, 1, True, False, main=False)
            batch(0, 0, True, False, first=True)
            with pe.Fori(0, B // 2 - 1) as i:
                batch(2 * i + 1, 1, True, True)
                batch(2 * i + 2, 0, True, True)
            batch(B - 1, 1, False, True)
            batch(B, 0, False, True, main=False)

        def film_block(layernorm, feed_forward):
            layernorm(x)
            pe.wait_ge(s.stage_pe, 1)
            pe.sem_inc(s.stage_pe, -1)
            pe.wait_ge(s.stage_pe, 1)
            pe.sem_inc(s.stage_pe, -1)
            for h in range(TH):
                pe.wait_ge(s.side_free, 1)
                pe.sem_inc(s.side_free, -1)
                mm(bank(6 + h % 2, C), W("tk", "wq")[:, h * 128:h * 128 + 128], W("tk", "wk")[:, h * C:h * C + C],
                   start=True, stop=True).then_inc(s.side_full, 1)
            pe.wait_ge(s.stage_pe, 1)
            pe.sem_inc(s.stage_pe, -1)

            def queries(b):
                pe.wait_ge(s.proj_free, 1)
                pe.sem_inc(s.proj_free, -1)
                for h in range(TH):
                    ins = mm(bank(6, S, C, h * S), wf4[:, h * C:h * C + C], xn[:, bass.ds(b, 1), :], start=True, stop=True)
                ins.then_inc(s.proj_full, 1)
                pe.wait_ge(s.qv_ready, 1)
                pe.sem_inc(s.qv_ready, -1)
                pe.wait_ge(s.mask_ready, 1)
                pe.sem_inc(s.mask_ready, -1)

            def scores(h, par):
                pe.wait_ge(s.row_scores_free, 1)
                pe.sem_inc(s.row_scores_free, -1)
                for c, (a, z) in enumerate(CHUNKS):
                    to = bank(3 * (h % 2) + c, z - a, S)
                    mm(to, ones_bf[:, 0:S], mask_bf[par][:, a:z], start=True, stop=False)
                    ins = mm(to, qv[:, h, :], ctxT[par][0:C, a:z], start=False, stop=True)
                ins.then_inc(s.row_scores, 1)

            def mean(par):
                pe.wait_ge(s.kept_ready, TH)
                pe.sem_inc(s.kept_ready, -TH)
                for u in range(KT // 4):
                    pe.wait_ge(s.proj_free, 1)
                    pe.sem_inc(s.proj_free, -1)
                    for t in range(4 * u, 4 * u + 4):
                        r = key_rows_of(t)
                        for h in range(TH):
                            ins = mm(bank(6, S, r, t % 4 * S), kept[:, h, 128 * t:128 * t + r], turn_scale[:, h, :],
                                     start=h == 0, stop=h == TH - 1)
                    ins.then_inc(s.proj_full, 1)
                pe.wait_ge(s.mean_ready, KT // 4)
                pe.sem_inc(s.mean_ready, -(KT // 4))
                pe.wait_ge(s.proj_free, 1)
                pe.sem_inc(s.proj_free, -1)
                for t in range(KT):
                    r = key_rows_of(t)
                    ins = mm(bank(6, S, C), ctxk[par][0:r, t, 0:C], meanT[0:r, t, :], start=t == 0, stop=t == KT - 1)
                ins.then_inc(s.proj_full, 1)
                pe.wait_ge(s.uv_ready, 1)
                pe.sem_inc(s.uv_ready, -1)
                pe.wait_ge(s.proj_free, 1)
                pe.sem_inc(s.proj_free, -1)
                mm(bank(6, S), W("tk", "wv"), uv, start=True, stop=True).then_inc(s.proj_full, 1)

            def batch(b, par, last=False):
                scores(2, par)
                scores(3, par)
                if not last:
                    queries(b + 1)
                    scores(0, 1 - par)
                    scores(1, 1 - par)
                mean(par)
            queries(0)
            scores(0, 0)
            scores(1, 0)
            batch(0, 0)
            with pe.Fori(0, B // 2 - 1) as i:
                batch(2 * i + 1, 1)
                batch(2 * i + 2, 0)
            batch(B - 1, 1, last=True)
            layernorm(mid)
            pe.wait_ge(s.stage_pe, 1)
            pe.sem_inc(s.stage_pe, -1)
            modulate("film_in")
            modulate("film_out")
            layernorm(mid)
            feed_forward(3)
            layernorm(xn)

        def modulate(name):
            for g in range(NG):
                pe.wait_ge(s.film_free, 1)
                pe.sem_inc(s.film_free, -1)
                for c in range(2):
                    ins = mm(bank(2 * (g % 2) + c), W("tk", name)[:, 128 * c:128 * c + 128], group(ct, g), start=True, stop=True)
                ins.then_inc(s.film_full, 1)

        def feed_forward(n):
            cfg = FEED[FF[n]]
            w = FF[n]
            pe.wait_ge(s.stage_pe, 1)
            pe.sem_inc(s.stage_pe, -1)
            pe.wait_ge(s.stage_pe, 1)
            pe.sem_inc(s.stage_pe, -1)
            if cfg["gate"]:
                E = cfg["E"]
                for b in range(B):
                    to = bank(0, E, S, b * E)
                    if "gate_b" in where[w]:
                        mm(to, W("const", "ones")[0:1, 0:S], W(w, "gate_b"), start=True, stop=False)
                    ins = mm(to, xn[:, b, :], W(w, "gate"), start="gate_b" not in where[w], stop=True)
                ins.then_inc(s.logits_ready, 1)
                pe.wait_ge(s.weights_ready, 1)
                pe.sem_inc(s.weights_ready, -1)
                for b in range(B):
                    ins = nc.tensor.transpose(bank(b // GB, S, E, b % GB * S), weight[:, b, 0:E], ident[0:S, 0:S])
                    if b % GB == GB - 1:
                        ins.then_inc(s.gates_turned, 1)
                pe.wait_ge(s.gates_there, 1)
                pe.sem_inc(s.gates_there, -1)
            for g in range(NG):
                if n == 1:
                    mm(bank(4 + g), W(w, "b2"), gateT[0:16, g * GT:g * GT + GT], start=True, stop=False)
                    mm(bank(4 + g), W(w, "sb2"), W("const", "ones_row"), start=False, stop=False)
                elif "b2" in where[w]:
                    mm(bank(4 + g), W(w, "b2"), W("const", "ones_row"), start=True, stop=False)
                else:
                    mm(bank(4 + g), W("const", "zeros")[0:1, :], W("const", "ones_row"), start=True, stop=False)

            def up(c, g, k):
                if g == 0:
                    pe.wait_ge(chunk_loaded[c], 16)
                    pe.sem_inc(chunk_loaded[c], -16)
                ins = mm(bank(k), chunk[c][:, 0:128], group(xn, g), start=True, stop=True)
                if cfg["up2"]:
                    ins = mm(bank(2 + k), chunk[c][:, 128:256], group(xn, g), start=True, stop=True)
                ins.then_inc(s.up_done, 1)

            def down(c, g, k, last):
                pe.wait_ge(s.h_ready, 1)
                pe.sem_inc(s.h_ready, -1)
                ins = mm(bank(4 + g), chunk[c][:, 256:384], h_all[k], start=False, stop=last)
                if g == NG - 1:
                    ins.then_inc(chunk_free[c], 1)
                if last and g < NG - 1:
                    ins.then_inc(s.down_done, 1)
                if last and g == NG - 1:
                    nc.tensor.drain().then_inc(s.down_done, 1)

            def block(chunks, more):
                us = [(c, g) for c in chunks for g in range(NG)]
                for u, (c, g) in enumerate(us):
                    down(c, g, u % 2, not more and c == chunks[-1])
                    if u + 2 < len(us):
                        up(*us[u + 2], u % 2)
                    elif more:
                        up(0, u + 2 - len(us), u % 2)
            up(0, 0, 0)
            up(0, 1, 1)
            if cfg["loop"]:
                with pe.Fori(0, cfg["loop"]) as i:
                    block(range(4), True)
            block(range(cfg["last"]), False)

        pe.wait_ge(loaded["const"], 16)
        for c in range(4):
            pe.sem_inc(chunk_free[c], 1)
        stages(layernorm, self_attention, cross_attention, feed_forward, film_block)
        pe.wait_ge(s.stage_pe, 1)
        pe.sem_inc(s.stage_pe, -1)

    ctx.close()


def kernel(**inputs):
    import concourse.bacc as bacc
    from concourse.bass_utils import run_bass_kernel_spmd

    p = {k: np.asarray(v) for k, v in inputs.items()}
    arrays, where = {}, {}
    parts = {"const": constants(), "sa0": self_parts(0, p), "ca0": cross_parts(0, p), "sa1": self_parts(1, p),
             "ca1": cross_parts(1, p), "sa2": self_parts(2, p), "ca2": cross_parts(2, p), "sa3": self_parts(3, p),
             "tk": film_parts(p)}
    for n, name in zip((0, 1, 2, "g", 3), FEED):
        arrays[name + "_chunks"], parts[name] = feed_parts(n, p)
    for name, value in parts.items():
        arrays[name], where[name] = pack(value)
    arrays["x"] = np.ascontiguousarray(p["x"].transpose(2, 0, 1))
    arrays["text_mask"] = np.ascontiguousarray(p["mask_BxS_bf1"]).view(np.uint8).reshape(1, -1)
    arrays["ctx_mask"] = np.ascontiguousarray(p["mask_BxS2_bf1"]).view(np.uint8)
    arrays["ctx"] = np.ascontiguousarray(p["ctx_768"])
    arrays["ctxT"] = np.ascontiguousarray(p["ctx_768"].transpose(0, 2, 1))
    nc = bacc.Bacc("TRN2", target_bir_lowering=False, num_devices=1)
    dram = {k: nc.dram_tensor("in_" + k, a.shape, mybir.dt.from_np(a.dtype), kind="ExternalInput").ap() for k, a in arrays.items()}
    out = nc.dram_tensor("out", (D, B, S), F32, kind="ExternalOutput").ap()
    build(nc, dram, where, out)
    r = run_bass_kernel_spmd(nc, [{"in_" + k: a for k, a in arrays.items()}], core_ids=[0])
    return np.ascontiguousarray(r.results[0]["out"].transpose(1, 2, 0))
```

```python
import math
from contextlib import ExitStack

import numpy as np

import concourse.bass as bass
from concourse import mybir

F32 = mybir.dt.float32
BF16 = mybir.dt.bfloat16
F32R = mybir.dt.float32r
U8 = mybir.dt.uint8
ACT = mybir.ActivationFunctionType
ALU = mybir.AluOpType
AX = mybir.AxisListType

B, S, D = 16, 100, 128
K, C = 1444, 96
GB = 4
NG = B // GB
GT = GB * S
T = B * S
KT = -(-K // 128)
KTAIL = K - 128 * (KT - 1)
HEADS = 16
ACT_KEYS, DVE_KEYS = 5, 14
ARENA = 22200
K_WORDS, CK_WORDS = -(-K // 8) * 8, -(-KT * (C + 1) // 8) * 8
TRAIL = 6
SIDE_COST = dict(query=600, q_round=650, q_low=600, recips=1300, maxima=900, spread=500, project=300, chunk=540)
ROUND = 1.5 * 2 ** 23


class Semaphores:
    def __init__(self, made):
        self.x_loaded = made("x_loaded")
        self.x_final = made("x_final")
        self.stored = made("stored")
        self.start_act = made("start_act")
        self.stage_pe = made("stage_pe")
        self.stage_act = made("stage_act")
        self.stage_pool = made("stage_pool")
        self.pool_done = made("pool_done")
        self.act_done = made("act_done")
        self.dve_done = made("dve_done")
        self.mean = made("mean")
        self.centred = made("centred")
        self.squared = made("squared")
        self.variance = made("variance")
        self.deviated = made("deviated")
        self.inverse_ready = made("inverse_ready")
        self.inverse_spread = made("inverse_spread")
        self.magnitudes = made("magnitudes")
        self.totals = made("totals")
        self.bn_var = made("bn_var")
        self.bn_dev = made("bn_dev")
        self.lam_sum = made("lam_sum")
        self.lam_exp = made("lam_exp")
        self.xg_ready = made("xg_ready")
        self.proj_full = made("proj_full")
        self.proj_free = made("proj_free")
        self.proj_even_free = made("proj_even_free")
        self.proj_odd_free = made("proj_odd_free")
        self.head_sq = made("head_sq")
        self.head_norm = made("head_norm")
        self.head_dev = made("head_dev")
        self.unit_done = made("unit_done")
        self.qk_ready = made("qk_ready")
        self.v_ready = made("v_ready")
        self.gate_ready = made("gate_ready")
        self.scores = made("scores")
        self.shifted = made("shifted")
        self.probs_ready = made("probs_ready")
        self.turned = made("turned")
        self.probsT_ready = made("probsT_ready")
        self.o_full = made("o_full")
        self.o_free = made("o_free")
        self.rms_sum = made("rms_sum")
        self.rms_root = made("rms_root")
        self.y_ready = made("y_ready")
        self.y_turned = made("y_turned")
        self.y_feat_ready = made("y_feat_ready")
        self.out_full = made("out_full")
        self.ctx_bf = made("ctx_bf")
        self.q_ready = made("q_ready")
        self.q_bf = made("q_bf")
        self.side_full = made("side_full")
        self.side_free = made("side_free")
        self.scoresT = made("scoresT")
        self.pexp_ready = made("pexp_ready")
        self.u_full = made("u_full")
        self.u_raw_ready = made("u_raw_ready")
        self.u_ready = made("u_ready")
        self.maxima_ready = made("maxima_ready")
        self.qa_ready = made("qa_ready")
        self.w_cross_free = made("w_cross_free")
        self.ctx_bf_free = made("ctx_bf_free")
        self.ctxT_free = made("ctxT_free")
        self.ctxT_loaded = made("ctxT_loaded")
        self.u_raw_free = made("u_raw_free")
        self.pexp_hi_ready = made("pexp_hi_ready")
        self.pexp_hi_there = made("pexp_hi_there")
        self.pexp_lo_ready = made("pexp_lo_ready")
        self.ctx_split = made("ctx_split")
        self.u_all_raw = made("u_all_raw")
        self.den_loaded = made("den_loaded")
        self.rexp_ready = made("rexp_ready")
        self.masks_asked = made("masks_asked")
        self.text_mask_loaded = made("text_mask_loaded")
        self.mask_ready = made("mask_ready")
        self.angles = made("angles")
        self.decays = made("decays")
        self.rotation = made("rotation")
        self.qv_ready = made("qv_ready")
        self.row_scores = made("row_scores")
        self.row_scores_free = made("row_scores_free")
        self.scores_sb_free = made("scores_sb_free")
        self.scores_there = made("scores_there")
        self.low_ready = made("low_ready")
        self.expd_ready = made("expd_ready")
        self.mean_ready = made("mean_ready")
        self.kept_free = made("kept_free")
        self.kept_ready = made("kept_ready")
        self.uv_ready = made("uv_ready")
        self.ct_ready = made("ct_ready")
        self.film_full = made("film_full")
        self.film_free = made("film_free")
        self.logits_ready = made("logits_ready")
        self.weights_asked = made("weights_asked")
        self.weights_exp = made("weights_exp")
        self.weights_ready = made("weights_ready")
        self.gates_turned = made("gates_turned")
        self.gates_ready = made("gates_ready")
        self.gates_there = made("gates_there")
        self.gates_stored = made("gates_stored")
        self.up_done = made("up_done")
        self.h_act_ready = made("h_act_ready")
        self.h_ready = made("h_ready")
        self.down_done = made("down_done")
        self.keys_ready = made("keys_ready")
        self.keys_there = made("keys_there")
        self.km_act = made("km_act")
        self.km_dve = made("km_dve")
        self.km_pool = made("km_pool")


SELF = {
    "sa0": dict(nsm=1, vw=8, causal=True, scale=1 / math.sqrt(8) / 0.1, bias=True, gate=True, out_scale=0.1),
    "sa1": dict(nsm=1, vw=8, causal=True, scale=1 / math.sqrt(8), bias=False, quant=True, out_scale=1.0),
    "sa2": dict(nsm=2, vw=16, causal=False, scale=1 / math.sqrt(8), bias=False, diff=True, out_scale=1.0),
    "sa3": dict(nsm=1, vw=8, causal=True, scale=1 / math.sqrt(16) / 1.5, bias=True, unit=True, out_scale=0.5),
}
LAMBDA_INIT = 0.8 - 0.6 * math.exp(-0.3 * (2 - 1))
CROSS = {
    "ca0": dict(H=16, hd=64, scale=64 ** -0.5),
    "ca1": dict(H=1, hd=128, scale=128 ** -0.5),
    "ca2": dict(H=16, hd=8, scale=8 ** -0.5),
}
FEED = {
    "ff0": dict(E=8, loop=7, last=4, func=ACT.Silu, up2=True, gate="block"),
    "ff1": dict(E=16, loop=2, last=1, func=ACT.Silu, up2=True, gate="chunk", hidden_bias=True, sigmoid=True),
    "ff2": dict(loop=0, last=4, func=ACT.Relu, up2=False, gate=None, hidden_bias=True),
    "ffg": dict(loop=0, last=4, func=ACT.Gelu, up2=False, gate=None, hidden_bias=True),
    "ff3": dict(E=8, loop=7, last=4, func=ACT.Silu, up2=True, gate="block"),
}
TH, TOP = 4, 32
TAKEN = -3e38
STATES = 64
LAGS = 10
CW = 3 * 128 + 2
QR = C + HEADS + 1
RMAX, RBIAS = C, C + HEADS


def column(v):
    return v.reshape(-1, 1)


def self_parts(n, p):
    if n == 0:
        w, b = p["L0_attn_w_qkv"], p["L0_attn_b_qkv"]
        return dict(wqk=w[:256].T, bqk=b[:256].reshape(2, 128).T,
                    wv=np.concatenate([w[256:].T, p["L0_attn_w_ent"].T], 1),
                    bv=np.concatenate([b[256:], p["L0_attn_b_ent"]])[None],
                    wo=p["L0_attn_w_out"].T, bo=column(p["L0_attn_b_out"]),
                    ln_g=column(p["L0_attn_ln_g"]), ln_b=column(p["L0_attn_ln_b"]))
    if n == 1:
        w = p["L1_attn_w_attn"]
        return dict(wqk=w[:256].T, wv=w[256:].T, wo=p["L1_attn_w_proj"].T)
    if n == 2:
        c = p["L2_attn_c_w"].T
        return dict(wqk=np.concatenate([p["L2_attn_" + k].T for k in ("q1_w", "k1_w", "q2_w", "k2_w")], 1),
                    wv=p["L2_attn_v_w"].T, wo=np.concatenate([c[:128], c[128:]], 1),
                    subln=np.tile(p["L2_attn_subln_w"], (128, 1)),
                    lam=np.tile(np.concatenate([p["L2_attn_" + k] for k in ("lq1", "lk1", "lq2", "lk2")]), (128, 1)),
                    bn_g=column(p["L2_attn_bn_gamma"]), bn_b=column(p["L2_attn_bn_beta"]))
    return dict(wqk=np.concatenate([p["L3_attn_Wq"].T, p["L3_attn_Wk"].T], 1),
                bqk=np.stack([p["L3_attn_bq"], p["L3_attn_bk"]], 1),
                wv=p["L3_attn_Wv"].T, bv=p["L3_attn_bv"][None],
                wo=p["L3_attn_Wo"].T, bo=column(p["L3_attn_bo"]))


def by_head(w, H):
    return np.transpose(w.reshape(w.shape[0], H, -1), (2, 1, 0))


def key_rows(wk, bk, H):
    k = by_head(wk, H)
    out = np.zeros((k.shape[0], H, QR), wk.dtype)
    out[:, :, :C] = k
    if bk is not None:
        out[:, :, RBIAS] = bk.reshape(H, -1).T
    return out.reshape(k.shape[0], -1)


def cross_parts(n, p):
    if n == 0:
        wv = np.concatenate([p["L0_xattn_Wv"], np.zeros((1, 1024), np.float32)], 0)
        return dict(wq=by_head(p["L0_xattn_Wq"], 16).reshape(64, -1), wk=key_rows(p["L0_xattn_Wk"], None, 16),
                    wv=by_head(wv, 16).reshape(64, -1),
                    wo=p["L0_xattn_Wo"].reshape(16, 64, 128).transpose(1, 0, 2).reshape(64, -1),
                    bo=column(p["L0_xattn_bo"]))
    if n == 1:
        return dict(wq=p["L1_xattn_Wq"], wk=key_rows(p["L1_xattn_Wk"].T, p["L1_xattn_bk"], 1),
                    bq=column(p["L1_xattn_bq"]),
                    wvo=np.concatenate([p["L1_xattn_Wv"].T, p["L1_xattn_bv"][None]], 0))
    wv = np.concatenate([p["L2_xattn_wv"], p["L2_xattn_bv"][None]], 0)
    return dict(wq=by_head(p["L2_xattn_wq"], 16).reshape(8, -1), wk=key_rows(p["L2_xattn_wk"], p["L2_xattn_bk"], 16),
                bq=p["L2_xattn_bq"].reshape(16, 8).T, wv=by_head(wv, 16).reshape(8, -1),
                wo=p["L2_xattn_wo"].reshape(16, 8, 128).transpose(1, 0, 2).reshape(8, -1),
                bo=column(p["L2_xattn_bo"]))


def chunks_of(up, up2, down, b1=None, b2=None):
    n = up.shape[1] // 128
    out = np.zeros((n, 128, CW), np.float32)
    out[:, :, 0:128] = up.reshape(128, n, 128).transpose(1, 0, 2)
    if up2 is not None:
        out[:, :, 128:256] = up2.reshape(128, n, 128).transpose(1, 0, 2)
    out[:, :, 256:384] = down.reshape(n, 128, 128)
    if b1 is not None:
        out[:, :, 384] = b1.reshape(n, 128)
    if b2 is not None:
        out[:, :, 385] = b2.reshape(n, 128)
    return out


def feed_parts(n, p):
    def wide(w):
        return w.transpose(1, 0, 2).reshape(w.shape[1], -1)

    if n == 0:
        return (chunks_of(wide(p["L0_ffn_w1"]), wide(p["L0_ffn_w3"]), p["L0_ffn_w2"].reshape(-1, 128)),
                dict(gate=p["L0_ffn_gate_w"], gate_b=p["L0_ffn_gate_b"][None]))
    if n == 1:
        up = [np.concatenate([wide(p[f"L1_ffn_w{k}"].transpose(0, 2, 1)), p[f"L1_ffn_sw{k}"].T], 1) for k in (1, 3)]
        down = np.concatenate([p["L1_ffn_w2"].transpose(0, 2, 1).reshape(-1, 128), p["L1_ffn_sw2"].T], 0)
        bias = [np.concatenate([p[f"L1_ffn_b{k}"].reshape(-1), p[f"L1_ffn_sb{k}"]]) for k in (1, 3)]
        return (chunks_of(up[0], up[1], down, *bias),
                dict(gate=p["L1_ffn_gate_w"].T, expert_b=np.tile(p["L1_ffn_expert_bias"], (128, 1)),
                     b2=p["L1_ffn_b2"], sb2=p["L1_ffn_sb2"][None]))
    if n == 2:
        return (chunks_of(p["L2_ffn_w1"][0], None, p["L2_ffn_w2"][0], p["L2_ffn_b1"][0]),
                dict(b2=p["L2_ffn_b2"][0][None], ln_g=column(p["L2_ffn_gamma"]), ln_b=column(p["L2_ffn_beta"])))
    if n == "g":
        return (chunks_of(p["L3_xattn_W1"], None, p["L3_xattn_W2"], p["L3_xattn_b1"]), dict(b2=p["L3_xattn_b2"][None]))
    return (chunks_of(wide(p["L3_ffn_Wgate"].transpose(0, 2, 1)), wide(p["L3_ffn_Wup"].transpose(0, 2, 1)),
                      p["L3_ffn_Wdown"].transpose(0, 2, 1).reshape(-1, 128)),
            dict(gate=p["L3_ffn_wg"].T, gate_b=p["L3_ffn_bg"][None]))


def film_parts(p):
    q = {k[len("L3_xattn_"):]: v for k, v in p.items() if k.startswith("L3_xattn_")}
    return dict(wq=by_head(q["Wq"], TH).reshape(32, -1), wk=by_head(q["Wk"], TH).reshape(32, -1), wv=q["Wv"],
                film_in=q["W_film_in"], film_out=q["W_film_out"],
                b_film_in=q["b_film_in"].reshape(2, 128).T, b_film_out=q["b_film_out"].reshape(2, 128).T,
                g_in=column(q["g_norm_in"]), b_in=column(q["b_norm_in"]), g_out=column(q["g_norm_out"]),
                b_out=column(q["b_norm_out"]), g_ffn=column(q["g_ffn"]), b_ffn=column(q["b_ffn"]),
                log_dt=column(q["log_dt"]), A_re=q["A_re"], A_im=q["A_im"], C_re=q["C_re"], C_im=q["C_im"],
                skip=column(q["D_skip"]), mod=np.tile(q["mod_gate"].reshape(1, 1), (128, 1)))


def pack(parts):
    where, n = {}, 0
    for name, a in parts.items():
        where[name] = (a.shape[0], n, a.shape[1])
        n += a.shape[1]
    out = np.zeros((128, n), np.float32)
    for name, a in parts.items():
        rows, at, cols = where[name]
        out[:rows, at:at + cols] = a
    return out, where


def constants():
    i = np.arange(128)
    ident = np.eye(128, dtype=np.float32)
    mean = np.full((128, 128), 1 / 128, np.float32)
    ones = np.ones((128, 128), np.float32)
    causal = np.where(np.arange(S)[None, :] <= np.arange(S)[:, None], 0.0, -1e30).astype(np.float32)
    row96 = np.zeros((C + 1, C + 1), np.float32)
    row96[C] = 1
    own_head = np.zeros((C + HEADS, HEADS), np.float32)
    for h in range(HEADS):
        own_head[C + h, h] = -1
    head_rows = (i[:, None] // 8 == i[None, :] // 8).astype(np.float32)
    head_of = (i[:, None] // 8 == np.arange(HEADS)[None, :]).astype(np.float32)
    return dict(ident=ident, mean=mean, ones=ones, causal=np.tile(causal, (1, 4)), row96=row96,
                own_head=own_head, head_rows=head_rows, head_of=head_of,
                zeros=np.zeros((HEADS, 128), np.float32),
                ones_row=np.ones((1, GT), np.float32),
                before=np.tile((np.arange(16)[None, :] < np.arange(16)[:, None]).astype(np.float32).reshape(1, -1), (128, 1)))


def build(nc, dram, where, out):
    ctx = ExitStack()

    def sb(name, shape, dt=F32):
        return ctx.enter_context(nc.sbuf_tensor(name, shape, dt))

    def place(t):
        return nc.sbuf_base - 4 * math.prod(t.shape[1:])

    cross_cols = max(dram[k].shape[1] for k in CROSS)
    w_cross = sb("w_cross", [128, max(cross_cols, 3 * K_WORDS + 2 * CK_WORDS)])
    w_cross_at = place(w_cross)
    packed = {k: w_cross if k in CROSS else sb("w_" + k, [128, dram[k].shape[1]]) for k in where}

    def W(stage, name):
        rows, at, cols = where[stage][name]
        return packed[stage][0:rows, at:at + cols]

    s = Semaphores(lambda name: ctx.enter_context(nc.semaphore(name)))
    loaded = {k: ctx.enter_context(nc.semaphore("loaded_" + k)) for k in where}
    ctx_loaded = [ctx.enter_context(nc.semaphore(f"ctx_loaded_{i}")) for i in range(2)]
    chunk_loaded = [ctx.enter_context(nc.semaphore(f"chunk_loaded_{i}")) for i in range(4)]
    chunk_free = [ctx.enter_context(nc.semaphore(f"chunk_free_{i}")) for i in range(4)]
    gate_loaded = [ctx.enter_context(nc.semaphore(f"gate_loaded_{i}")) for i in range(NG)]
    gate_free = [ctx.enter_context(nc.semaphore(f"gate_free_{i}")) for i in range(NG)]
    ctx_free = [ctx.enter_context(nc.semaphore(f"ctx_free_{i}")) for i in range(2)]
    proj_bank_free = [s.proj_even_free, s.proj_odd_free]
    ps = ctx.enter_context(nc.psum_tensor("ps", [128, 8, 512], F32))

    x = sb("x", [128, B, S])
    xn = sb("xn", [128, B, S])
    mid = sb("mid", [128, B, S])
    squares = sb("squares", [128, B, S])
    deviation = sb("deviation", [128, B, S])
    eps = sb("eps", [128, 2])
    ident_bf = sb("ident_bf", [128, 128], BF16)
    causal_bf = sb("causal_bf", [S, GT], BF16)
    bn = sb("bn", [128, 4, 6])
    token_dev = sb("token_dev", [S, B])
    col = sb("col", [128, 16])

    arena = sb("arena", [128, ARENA])
    arena_at = place(arena)
    filled = [0]

    def shared(shape, dt=F32):
        n = math.prod(shape[1:])
        words = {F32: n, F32R: n, BF16: -(-n // 2), U8: -(-n // 4)}[dt]
        v = arena[0:shape[0], filled[0]:filled[0] + words]
        filled[0] += words
        assert filled[0] <= ARENA, filled
        if dt != F32:
            v = v.bitcast(dt)[:, 0:n]
        if len(shape) == 3:
            v = v.rearrange("p (a b) -> p a b", b=shape[2])
        return v

    xg = shared([128, GT])
    qk = shared([128, 4, GT])
    km = shared([128, 2 * HEADS, GT])
    vaug = shared([S, GB, 16 * 17])
    gate = shared([S, GB])
    probs = shared([S, 2, 8 * S])
    probsT = shared([S, 2, 8 * S])
    smax = shared([S, 2, 8])
    rden = shared([S, 16])
    y_tok = shared([S, GB, 256])
    y_sq = shared([S, GB, 256])
    y_rms = shared([S, GB * 16])
    y_feat = shared([128, 2, GT])

    filled[0] = 0
    ctxT, ctxk, ctxT_lo, ctxk_lo = [], [], [], []

    def rounded(name, shape, at):
        return nc.alloc_sbuf_tensor_at(name, shape, F32R, offset=at)

    for i in range(2):
        ctxT.append(sb(f"ctxT{i}", [QR, K]))
        ctxT_lo.append(rounded(f"ctxT_lo{i}", [QR, K], place(ctxT[i])))
        ctxk.append(sb(f"ctxk{i}", [128, KT, C + 1]))
        ctxk_lo.append(rounded(f"ctxk_lo{i}", [128, KT, C + 1], place(ctxk[i])))
    ctxT_bf = shared([QR, K], BF16)
    wfold = shared([128, 16 * QR])
    bfold = shared([QR, 16])
    vfold = shared([C + 1, 16 * 128])
    qa = [shared([QR, 1, S]) for i in range(2)]
    qa_bf = shared([QR, HEADS, S], BF16)
    mparts = shared([S, HEADS, 3])
    mrows = shared([S, C + HEADS])
    pexp = [shared([128, GT]) for i in range(3)]
    u_raw = shared([C + 1, HEADS, S])
    u_rec = shared([C + 1, HEADS, S])
    q_full = shared([QR, GT])
    den_rows = shared([HEADS, S])
    rexp = shared([HEADS, HEADS, S])

    def rounded_in_arena(name, shape):
        filled[0] = -(-filled[0] // 8) * 8
        at = arena_at + 4 * filled[0]
        filled[0] += math.prod(shape[1:])
        assert filled[0] <= ARENA, filled
        return rounded(name, shape, at)

    qa_hi = [rounded_in_arena(f"qa_hi{i}", [QR, HEADS, S]) for i in range(2)]
    qa_lo = [rounded_in_arena(f"qa_lo{i}", [QR, HEADS, S]) for i in range(2)]
    pexp_hi = [rounded_in_arena(f"pexp_hi{i}", [128, GT]) for i in range(3)]
    pexp_lo = [rounded_in_arena(f"pexp_lo{i}", [128, GT]) for i in range(3)]
    ctxT_raw = w_cross[0:C, 0:K]
    ctxT_hi = [rounded(f"ctxT_hi{i}", [QR, K], w_cross_at + 4 * (1 + i) * K_WORDS) for i in range(2)]
    ctxk_hi = [rounded(f"ctxk_hi{i}", [128, KT, C + 1], w_cross_at + 4 * (3 * K_WORDS + i * CK_WORDS)) for i in range(2)]

    filled[0] = 0
    text_mask = shared([128, T // 4])
    ct = shared([128, B, S])
    scores_sb = [shared([S, K]) for i in range(2)]
    left = shared([S, K])
    expd = [shared([S, K]) for i in range(2)]
    kept = shared([S, TH, K])
    turn_scale = shared([S, TH, S])
    meanT = shared([128, KT, S])
    uv = shared([C, S])
    qv = shared([C, TH, S])
    top8 = shared([S, 4, 8])
    low = shared([S, 2])
    den = shared([S, TH])
    wf4 = shared([128, TH * C])
    mask_u8 = [shared([1, K], U8) for i in range(2)]
    mask_bf = [shared([1, K], BF16) for i in range(2)]
    ones_bf = sb("ones_bf", [1, 128], BF16)
    kernel_l = sb("kernel_l", [128, S])
    filled[0] = 0
    ssm = shared([128, 12, STATES])
    powers = [[shared([128, LAGS + 1, STATES]) for part in range(2)] for base in range(2)]
    prods = [shared([128, S, STATES]) for i in range(2)]
    scratch = [shared([128, LAGS * STATES]) for i in range(3)]
    ssm_words = filled[0]
    filled[0] = 0
    logits = shared([S, B, 16])
    biased = shared([S, B, 16])
    rank = shared([S, B, 16])
    weight = shared([S, B, 16])
    best = shared([S, B])
    pairs = shared([S, B * 256])
    pairs2 = shared([S, B * 256])
    gateT = shared([16, T])
    gate_rows = [shared([128, GT]) for g in range(NG)]
    filled[0] = max(filled[0], ssm_words)
    h_act = [shared([128, GT]) for i in range(2)]
    h_all = [shared([128, GT]) for i in range(2)]
    chunk = [sb(f"chunk{c}", [128, CW]) for c in range(4)]
    gate_dram = nc.dram_tensor("gate_dram", (16, T), F32).ap()

    block = ctx.enter_context(nc.Block())
    FF = list(FEED)
    SA, CA = list(SELF), list(CROSS)

    def bank(n, cols=GT, rows=128, at=0):
        return ps[0:rows, n, at:at + cols]

    def group(t, g):
        return t[:, GB * g:GB * g + GB, :]

    def eps_col(i):
        return eps[:, i:i + 1]

    def bs(v):
        return v.rearrange("p (b t) -> p b t", t=S)

    def stages(layernorm, self_attention, cross_attention, feed_forward, film_block):
        layernorm(x)
        layernorm(xn, eps=1, affine=(W("sa0", "ln_g"), W("sa0", "ln_b")))
        self_attention(0)
        layernorm(x)
        cross_attention(0)
        layernorm(x)
        feed_forward(0)
        layernorm(x)
        self_attention(1)
        layernorm(x)
        cross_attention(1)
        layernorm(x)
        feed_forward(1)
        layernorm(x)
        self_attention(2)
        layernorm(x)
        cross_attention(2)
        layernorm(x)
        feed_forward(2)
        layernorm(xn, affine=(W("ff2", "ln_g"), W("ff2", "ln_b")), add=True)
        layernorm(x)
        self_attention(3)
        film_block(layernorm, feed_forward)
        layernorm(x)
        feed_forward(4)

    CHUNKS = [(0, 482), (482, 962), (962, K)]

    def key_rows_of(t):
        return 128 if t < KT - 1 else KTAIL

    def units(H):
        if H == 1:
            return [[(4 * u + j, j * S, 0, 1, 0) for j in range(4)] for u in range(KT // 4)]
        return [[(t, 0, 4 * g, 4, g)] for t in range(KT) for g in range(H // 4)]

    def side_places(H, prep, tail, main):
        us = len(units(H)) if main else 0
        nG = -(-H // 4)
        spreads = [("spread", g) for g in range(nG)] + [("project", 0)] if tail else []
        recips = [("recips", 0), ("recips", 1)] if tail and H > 1 else []
        queries = [("query", g) for g in range(nG)] if prep else []
        chunks = [("chunk", (h, c)) for h in range(H) for c in range(3)] if prep else []
        maxima = [("maxima", g) for g in range(2 if H > 1 else 1)] if prep else []
        if H > 1:
            queries = [[("query", g), ("q_round", g), ("q_low", g)] for g in range(nG)] if prep else [[], [], [], []]
            items = (queries[0] + queries[1] + chunks[0:6] + recips[:1] + chunks[6:8] + recips[1:] + chunks[8:12] + spreads
                     + queries[2] + chunks[12:24] + queries[3] + chunks[24:])
        at = {}
        if not main:
            at[0] = (items if H > 1 else spreads + queries + chunks) + maxima
        elif H == 1:
            at[1] = spreads
            at[us] = queries + chunks + maxima
        else:
            total, spent = sum(SIDE_COST[it[0]] for it in items), 0
            for it in items:
                at.setdefault(int(spent * (us - TRAIL) / total), []).append(it)
                spent += SIDE_COST[it[0]]
            for i, it in enumerate(maxima):
                at.setdefault(us - 4 + i, []).append(it)
        return at

    @block.sync
    def _(sp):
        sp.dma_start(x[:, :, :], dram["x"]).then_inc(s.x_loaded, 16)
        for k in where:
            if k not in CROSS:
                sp.dma_start(packed[k][:, :], dram[k]).then_inc(loaded[k], 16)

        def layernorm(src, eps=0, affine=None, add=False):
            pass

        def self_attention(n):
            pass

        def cross_attention(n):
            def load_turned(b):
                sp.wait_ge(s.ctxT_free, 1)
                sp.sem_inc(s.ctxT_free, -1)
                sp.dma_start(ctxT_raw, dram["ctxT"][b, :, :]).then_inc(s.ctxT_loaded, 16)

            def load(b, par):
                sp.wait_ge(ctx_free[par], 1)
                sp.sem_inc(ctx_free[par], -1)
                if not split:
                    sp.dma_start(ctxT[par][0:C, :], dram["ctxT"][b, :, :]).then_inc(ctx_loaded[par], 16)
                sp.dma_start(ctxk[par][:, 0:KT - 1, 0:C],
                             dram["ctx"][b, 0:128 * (KT - 1), :].rearrange("(t p) c -> p t c", p=128)).then_inc(ctx_loaded[par], 16)
                sp.dma_start(ctxk[par][0:KTAIL, KT - 1, 0:C],
                             dram["ctx"][b, 128 * (KT - 1):K, :]).then_inc(ctx_loaded[par], 16)
            def denominators():
                sp.wait_ge(s.u_all_raw, 1)
                sp.sem_inc(s.u_all_raw, -1)
                sp.dma_start(den_rows[:, :], u_raw[C:C + 1, :, :]).then_inc(s.den_loaded, 16)

            split = CROSS[CA[n]]["H"] > 1
            k = CA[n]
            sp.wait_ge(s.w_cross_free, 1)
            sp.sem_inc(s.w_cross_free, -1)
            sp.dma_start(w_cross[:, 0:dram[k].shape[1]], dram[k]).then_inc(loaded[k], 16)
            if not split:
                load(0, 0)
                load(1, 1)
                with sp.Fori(0, B // 2 - 1) as i:
                    load(2 * i + 2, 0)
                    load(2 * i + 3, 1)
            else:
                load(0, 0)
                load(1, 1)
                load_turned(0)
                load_turned(1)
                with sp.Fori(0, B // 2 - 1) as i:
                    for par in range(2):
                        load_turned(2 * i + 2 + par)
                        denominators()
                        load(2 * i + 2 + par, par)
                denominators()
                denominators()
                sp.wait_ge(s.ctxT_free, 1)
                sp.sem_inc(s.ctxT_free, -1)

        def film_block(layernorm, feed_forward):
            def load(b, par):
                sp.wait_ge(ctx_free[par], 1)
                sp.sem_inc(ctx_free[par], -1)
                sp.dma_start(ctxT[par][0:C, :], dram["ctxT"][bass.ds(b, 1), :, :].rearrange("o c k -> (o c) k")).then_inc(ctx_loaded[par], 16)
                sp.dma_start(ctxk[par][:, 0:KT - 1, 0:C],
                             dram["ctx"][bass.ds(b, 1), 0:128 * (KT - 1), :].rearrange("o (t p) c -> p (o t) c", p=128)).then_inc(ctx_loaded[par], 16)
                sp.dma_start(ctxk[par][0:KTAIL, KT - 1, 0:C],
                             dram["ctx"][bass.ds(b, 1), 128 * (KT - 1):K, :].rearrange("o k c -> (o k) c")).then_inc(ctx_loaded[par], 16)
                sp.dma_start(mask_u8[par][:, :], dram["ctx_mask"][bass.ds(b, 1), :]).then_inc(ctx_loaded[par], 16)
            sp.wait_ge(s.masks_asked, 1)
            sp.sem_inc(s.masks_asked, -1)
            sp.dma_start(text_mask.bitcast(U8), dram["text_mask"].to_broadcast([128, T])).then_inc(s.text_mask_loaded, 16)
            load(0, 0)
            with sp.Fori(0, B // 2 - 1) as i:
                load(2 * i + 1, 1)
                load(2 * i + 2, 0)
            load(B - 1, 1)
            feed_forward(3)

        def feed_forward(n):
            cfg = FEED[FF[n]]
            blobs = dram[FF[n] + "_chunks"]

            def weights(i, c):
                sp.wait_ge(chunk_free[c], 1)
                sp.sem_inc(chunk_free[c], -1)
                sp.dma_start(chunk[c][:, :], blobs[bass.ds(4 * i + c, 1), :, :].rearrange("o p c -> (o p) c")).then_inc(chunk_loaded[c], 16)

            def gates(i, c):
                per = 1 if cfg["gate"] == "block" else 2
                for g in range(NG):
                    sp.wait_ge(gate_free[g], 1)
                    sp.sem_inc(gate_free[g], -1)
                    for e in range(per):
                        row = i if per == 1 else 8 * i + 2 * c + e
                        rows = 128 // per
                        sp.dma_start(gate_rows[g][rows * e:rows * e + rows, :],
                                     gate_dram[bass.ds(row, 1), g * GT:g * GT + GT].to_broadcast([rows, GT])).then_inc(gate_loaded[g], 16)

            def block(i, chunks):
                for c in chunks:
                    if cfg["gate"] == "chunk" and not (len(chunks) == 1):
                        weights(i, c)
                        gates(i, c)
                    elif cfg["gate"] == "block" and c == 3:
                        gates(i, c)
                        weights(i, c)
                    else:
                        weights(i, c)

            if cfg["gate"]:
                sp.wait_ge(s.gates_ready, 1)
                sp.sem_inc(s.gates_ready, -1)
                sp.dma_start(gate_dram[0:cfg["E"], :], gateT[0:cfg["E"], :]).then_inc(s.gates_stored, 16)
                sp.wait_ge(s.gates_stored, 16)
                sp.sem_inc(s.gates_stored, -16)
            if cfg["loop"]:
                with sp.Fori(0, cfg["loop"]) as i:
                    block(i, range(4))
            block(cfg["loop"], range(cfg["last"]))
            if cfg["gate"]:
                for g in range(NG):
                    sp.wait_ge(gate_free[g], 1)
                    sp.sem_inc(gate_free[g], -1)

        stages(layernorm, self_attention, cross_attention, feed_forward, film_block)
        sp.wait_ge(s.x_final, 1)
        sp.sem_inc(s.x_final, -1)
        sp.dma_start(out, x[:, :, :]).then_inc(s.stored, 16)
        sp.wait_ge(s.stored, 16)

    @block.gpsimd
    def _(pool):
        def layernorm(src, eps=0, affine=None, add=False):
            pass

        def self_attention(n):
            nsm = SELF[SA[n]]["nsm"]
            pool.wait_ge(loaded["const"], 16)
            with pool.Fori(0, NG) as g:
                for sm in range(nsm):
                    pool.wait_ge(s.keys_ready, 1)
                    pool.sem_inc(s.keys_ready, -1)
                    for h in range(DVE_KEYS, HEADS):
                        ins = nc.gpsimd.tensor_scalar(km[:, HEADS * sm + h, :], qk[:, 2 * sm + 1, :],
                                                      W("const", "head_of")[:, h:h + 1], None, ALU.mult)
                    ins.then_inc(s.km_pool, 1)

        def cross_attention(n):
            H = CROSS[CA[n]]["H"]

            def halves(x, hi, lo):
                nc.gpsimd.tensor_copy(hi, x).then_inc(s.pool_done, 1)
                pool.wait_ge(s.pool_done, 1)
                pool.sem_inc(s.pool_done, -1)
                nc.gpsimd.tensor_tensor(lo, x, hi, ALU.subtract).then_inc(s.pool_done, 1)
                pool.wait_ge(s.pool_done, 1)
                pool.sem_inc(s.pool_done, -1)

            def prep(par):
                if H == 1:
                    pool.wait_ge(ctx_loaded[par], 48)
                    pool.sem_inc(ctx_loaded[par], -48)
                    pool.wait_ge(s.ctx_bf_free, 1)
                    pool.sem_inc(s.ctx_bf_free, -1)
                    nc.gpsimd.tensor_copy(ctxT_bf[:, :], ctxT[par][:, :]).then_inc(s.ctx_bf)
                    pool.wait_ge(s.q_ready, 1)
                    pool.sem_inc(s.q_ready, -1)
                    nc.gpsimd.tensor_copy(qa_bf[:, 0:1, :], qa[par][:, 0:1, :]).then_inc(s.q_bf)
                    return
                pool.wait_ge(s.ctxT_loaded, 16)
                pool.sem_inc(s.ctxT_loaded, -16)
                pool.wait_ge(s.ctx_bf_free, 1)
                pool.sem_inc(s.ctx_bf_free, -1)
                nc.gpsimd.tensor_copy(ctxT_bf[0:C, :], ctxT_raw).then_inc(s.ctx_bf)
                pool.wait_ge(ctx_loaded[par], 32)
                pool.sem_inc(ctx_loaded[par], -32)
                halves(ctxT_raw, ctxT_hi[par][0:C, :], ctxT_lo[par][0:C, :])
                pool.sem_inc(s.ctxT_free, 1)
                halves(ctxk[par][:, 0:KT - 1, 0:C], ctxk_hi[par][:, 0:KT - 1, 0:C], ctxk_lo[par][:, 0:KT - 1, 0:C])
                halves(ctxk[par][0:KTAIL, KT - 1, 0:C], ctxk_hi[par][0:KTAIL, KT - 1, 0:C], ctxk_lo[par][0:KTAIL, KT - 1, 0:C])
                pool.sem_inc(s.ctx_split, 1)
            if H > 1:
                pool.wait_ge(s.stage_pool, 1)
                pool.sem_inc(s.stage_pool, -1)
            prep(0)
            with pool.Fori(0, B // 2 - 1) as i:
                prep(1)
                prep(0)
            prep(1)
            pool.wait_ge(s.ctx_bf_free, 1)
            pool.sem_inc(s.ctx_bf_free, -1)

        def feed_forward(n):
            pass

        def film_block(layernorm, feed_forward):
            def mask(par):
                pool.wait_ge(ctx_loaded[par], 64)
                pool.sem_inc(ctx_loaded[par], -64)
                nc.gpsimd.tensor_scalar(mask_bf[par][:, :], mask_u8[par][:, :], 1.0, 1e30, ALU.subtract, ALU.mult).then_inc(s.mask_ready, 1)
            mask(0)
            with pool.Fori(0, B // 2 - 1) as i:
                mask(1)
                mask(0)
            mask(1)

        stages(layernorm, self_attention, cross_attention, feed_forward, film_block)

    @block.scalar
    def _(act):
        def layernorm(src, eps=0, affine=None, add=False):
            for g in range(NG):
                act.wait_ge(s.centred, 1)
                act.sem_inc(s.centred, -1)
                nc.scalar.activation(group(squares, g), group(xn, g), ACT.Square).then_inc(s.squared, 1)
            for g in range(NG):
                act.wait_ge(s.variance, 1)
                act.sem_inc(s.variance, -1)
                nc.scalar.activation(token_dev[:, GB * g:GB * g + GB], bank(4 + g, GB, S), ACT.Sqrt,
                                     bias=eps_col(eps)[0:S]).then_inc(s.deviated, 1)

        def self_attention(n):
            cfg = SELF[SA[n]]
            nsm, vw = cfg["nsm"], cfg["vw"]
            if cfg.get("diff"):
                act.wait_ge(s.bn_var, 1)
                act.sem_inc(s.bn_var, -1)
                nc.scalar.activation(col[:, 2:3], col[:, 2:3], ACT.Sqrt, bias=eps_col(0)).then_inc(s.bn_dev, 1)
                act.wait_ge(s.lam_sum, 1)
                act.sem_inc(s.lam_sum, -1)
                nc.scalar.activation(col[0:S, 4:6], col[0:S, 4:6], ACT.Exp).then_inc(s.lam_exp, 1)
            act.wait_ge(s.stage_act, 1)
            act.sem_inc(s.stage_act, -1)
            with act.Fori(0, NG) as g:
                for m in range(2 * nsm):
                    act.wait_ge(s.proj_full, 1)
                    act.sem_inc(s.proj_full, -1)
                    if cfg["bias"]:
                        ins = nc.scalar.activation(qk[:, m, :], bank(6 - m % 2), ACT.Identity, bias=W(SA[n], "bqk")[:, m:m + 1])
                    else:
                        ins = nc.scalar.activation(qk[:, m, :], bank(6 - m % 2), ACT.Copy)
                    ins.then_inc(s.act_done, 1)
                    act.wait_ge(s.act_done, 1)
                    act.sem_inc(s.act_done, -1)
                    act.sem_inc(proj_bank_free[m % 2], 1)
                    if cfg.get("unit"):
                        nc.scalar.activation(group(squares, 0), bs(qk[:, m, :]), ACT.Square).then_inc(s.head_sq, 1)
                        act.wait_ge(s.head_norm, 1)
                        act.sem_inc(s.head_norm, -1)
                        nc.scalar.activation(group(deviation, 0), bs(bank(7)), ACT.Sqrt).then_inc(s.head_dev, 1)
                        act.wait_ge(s.unit_done, 1)
                        act.sem_inc(s.unit_done, -1)
                    if m % 2 == 1:
                        act.sem_inc(s.keys_ready, 1)
                        act.sem_inc(s.keys_there, 1)
                for b in range(GB):
                    act.wait_ge(s.proj_full, 1)
                    act.sem_inc(s.proj_full, -1)
                    v = vaug[:, b, 0:16 * (vw + 1)].rearrange("p (h w) -> p h w", w=vw + 1)
                    nc.scalar.activation(v[:, :, 0:vw], bank(6 - b % 2, 16 * vw, S).rearrange("p (h w) -> p h w", w=vw), ACT.Copy).then_inc(s.act_done, 1)
                    act.wait_ge(s.act_done, 1)
                    act.sem_inc(s.act_done, -1)
                    if cfg.get("gate"):
                        nc.scalar.activation(gate[:, b:b + 1], bank(6 - b % 2, 1, S, 128), ACT.Exp, scale=-1.0).then_inc(s.act_done, 1)
                        act.wait_ge(s.act_done, 1)
                        act.sem_inc(s.act_done, -1)
                    act.sem_inc(proj_bank_free[b % 2], 1)
                    act.sem_inc(s.gate_ready if cfg.get("gate") else s.v_ready, 1)
                for sm in range(nsm):
                    for h in range(ACT_KEYS):
                        ins = nc.scalar.activation(km[:, HEADS * sm + h, :], qk[:, 2 * sm + 1, :], ACT.Copy,
                                                   scale=W("const", "head_of")[:, h:h + 1])
                    ins.then_inc(s.km_act, 1)
                N = GB * nsm * 2
                for k in range(N):
                    act.wait_ge(s.shifted, 1)
                    act.sem_inc(s.shifted, -1)
                    nc.scalar.activation(probs[:, k % 2, :].rearrange("p (c t) -> p c t", c=2),
                                         ps[0:S, 2 * (k % 2):2 * (k % 2) + 2, 0:GT], ACT.Exp,
                                         scale=float(cfg["scale"])).then_inc(s.probs_ready, 1)
                    for c in range(2):
                        act.wait_ge(s.turned, 1)
                        act.sem_inc(s.turned, -1)
                        nc.scalar.activation(probsT[:, k % 2, c * GT:c * GT + GT], bank(4 + c, GT, S),
                                             ACT.Copy).then_inc(s.probsT_ready, 1)
                if cfg.get("diff"):
                    act.wait_ge(s.rms_sum, 1)
                    act.sem_inc(s.rms_sum, -1)
                    nc.scalar.activation(y_rms[:, :], y_rms[:, :], ACT.Sqrt, bias=eps_col(0)[0:S]).then_inc(s.rms_root, 1)
                for c in range(cfg["vw"] // 8):
                    act.wait_ge(s.y_turned, 1)
                    act.sem_inc(s.y_turned, -1)
                    nc.scalar.activation(y_feat[:, c, :], bank(6), ACT.Copy).then_inc(s.act_done, 1)
                    act.wait_ge(s.act_done, 1)
                    act.sem_inc(s.act_done, -1)
                    act.sem_inc(s.proj_free, 1)
                    act.sem_inc(s.y_feat_ready, 1)

        def cross_attention(n):
            H = CROSS[CA[n]]["H"]
            nU = -(-H // 4)
            act.wait_ge(s.stage_act, 1)
            act.sem_inc(s.stage_act, -1)

            def sums(g):
                act.wait_ge(s.u_full, 1)
                act.sem_inc(s.u_full, -1)
                w = min(H, 4)
                ins = nc.scalar.activation(u_raw[:, 4 * g:4 * g + w, :], bs(bank(2 + g, w * S, C + 1)), ACT.Copy)
                ins.then_inc(s.act_done, 1)
                act.wait_ge(s.act_done, 1)
                act.sem_inc(s.act_done, -1)
                act.sem_inc(s.u_raw_ready, 1)
                if H > 1:
                    act.sem_inc(s.u_raw_free, 1)

            def sums_end(par):
                if H > 1:
                    act.sem_inc(s.u_all_raw, 1)
                act.sem_inc(ctx_free[par], 1)

            def main(par, first=False):
                for u, unit in enumerate(units(H)):
                    act.wait_ge(s.scoresT, 1)
                    act.sem_inc(s.scoresT, -1)
                    t0, rows = unit[0][0], key_rows_of(unit[-1][0])
                    full = GT if rows == 128 else GT - S if H == 1 else 0
                    if full:
                        ins = nc.scalar.activation(pexp[u % 3][:, 0:full], bank(u % 2, full), ACT.Exp,
                                                   scale=CROSS[CA[n]]["scale"])
                    if full < GT:
                        if full:
                            ins.then_inc(s.act_done, 1)
                            act.wait_ge(s.act_done, 1)
                            act.sem_inc(s.act_done, -1)
                        ins = nc.scalar.activation(pexp[u % 3][0:rows, full:GT], bank(u % 2, GT - full, rows, full), ACT.Exp,
                                                   scale=CROSS[CA[n]]["scale"])
                    if H > 1:
                        ins.then_inc(s.pexp_ready, 1)
                        ins = nc.scalar.activation(pexp_hi[u % 3][0:rows, :], bank(u % 2, GT, rows), ACT.Exp,
                                                   scale=CROSS[CA[n]]["scale"])
                        ins.then_inc(s.act_done, 1)
                        act.wait_ge(s.act_done, 1)
                        act.sem_inc(s.act_done, -1)
                        act.sem_inc(s.pexp_hi_ready, 1)
                        act.sem_inc(s.pexp_hi_there, 1)
                        if u >= len(units(H)) - 2:
                            sums(u - len(units(H)) + 2)
                        if u < 2 and not first:
                            sums(u + 2)
                        if u == 1 and not first:
                            sums_end(1 - par)
                    else:
                        ins.then_inc(s.pexp_ready, 1)
                if H == 1:
                    sums(0)
                    sums_end(par)
            main(0, first=True)
            with act.Fori(0, B // 2 - 1) as i:
                main(1)
                main(0)
            main(1)
            if H > 1:
                sums(2)
                sums(3)
                sums_end(1)

        def film_block(layernorm, feed_forward):
            layernorm(x)
            act.wait_ge(s.stage_act, 1)
            act.sem_inc(s.stage_act, -1)

            def scores(b, h):
                if h == 0:
                    act.wait_ge(s.proj_full, 1)
                    act.sem_inc(s.proj_full, -1)
                    nc.scalar.activation(qv[:, :, :], bank(6, TH * S, C).rearrange("p (h t) -> p h t", t=S), ACT.Copy).then_inc(s.act_done, 1)
                    act.wait_ge(s.act_done, 1)
                    act.sem_inc(s.act_done, -1)
                    act.sem_inc(s.proj_free, 1)
                    act.sem_inc(s.qv_ready, 1)
                act.wait_ge(s.row_scores, 1)
                act.sem_inc(s.row_scores, -1)
                act.wait_ge(s.scores_sb_free, 1)
                act.sem_inc(s.scores_sb_free, -1)
                for c, (a, z) in enumerate(CHUNKS):
                    ins = nc.scalar.activation(scores_sb[h % 2][:, a:z], bank(3 * (h % 2) + c, z - a, S), ACT.Copy, scale=32 ** -0.5)
                ins.then_inc(s.act_done, 1)
                act.wait_ge(s.act_done, 1)
                act.sem_inc(s.act_done, -1)
                act.sem_inc(s.row_scores_free, 1)
                act.sem_inc(s.scores_there, 1)

            def exponents(h):
                act.wait_ge(s.low_ready, 1)
                act.sem_inc(s.low_ready, -1)
                nc.scalar.activation(expd[h % 2], scores_sb[h % 2], ACT.Exp, bias=low[:, h % 2:h % 2 + 1]).then_inc(s.expd_ready, 1)

            def mean(b, par):
                for u in range(KT // 4):
                    act.wait_ge(s.proj_full, 1)
                    act.sem_inc(s.proj_full, -1)
                    full = 4 if u < KT // 4 - 1 else 3
                    ins = nc.scalar.activation(meanT[:, 4 * u:4 * u + full, :], bs(bank(6, full * S)), ACT.Copy)
                    if full < 4:
                        ins.then_inc(s.act_done, 1)
                        act.wait_ge(s.act_done, 1)
                        act.sem_inc(s.act_done, -1)
                        ins = nc.scalar.activation(meanT[0:KTAIL, KT - 1, :], bank(6, S, KTAIL, 3 * S), ACT.Copy)
                    ins.then_inc(s.act_done, 1)
                    act.wait_ge(s.act_done, 1)
                    act.sem_inc(s.act_done, -1)
                    act.sem_inc(s.proj_free, 1)
                    act.sem_inc(s.mean_ready, 1)
                act.sem_inc(s.kept_free, 1)
                act.wait_ge(s.proj_full, 1)
                act.sem_inc(s.proj_full, -1)
                nc.scalar.activation(uv, bank(6, S, C), ACT.Copy).then_inc(s.act_done, 1)
                act.wait_ge(s.act_done, 1)
                act.sem_inc(s.act_done, -1)
                act.sem_inc(s.proj_free, 1)
                act.sem_inc(s.uv_ready, 1)
                act.sem_inc(ctx_free[par], 1)
                act.wait_ge(s.proj_full, 1)
                act.sem_inc(s.proj_full, -1)
                nc.scalar.activation(ct[:, bass.ds(b, 1), :], bs(bank(6, S)), ACT.Copy).then_inc(s.act_done, 1)
                act.wait_ge(s.act_done, 1)
                act.sem_inc(s.act_done, -1)
                act.sem_inc(s.proj_free, 1)

            def batch(b, par, first=False, last=False):
                for h in range(TH):
                    if h < TH - 1:
                        scores(b, h + 1)
                    elif not last:
                        scores(b + 1, 0)
                    exponents(h)
                    if h == 0 and not first:
                        mean(b - 1, 1 - par)
            scores(0, 0)
            batch(0, 0, first=True)
            with act.Fori(0, B // 2 - 1) as i:
                batch(2 * i + 1, 1)
                batch(2 * i + 2, 0)
            batch(B - 1, 1, last=True)
            mean(B - 1, 1)
            act.sem_inc(s.ct_ready, 1)
            layernorm(mid)
            layernorm(mid)
            feed_forward(3)
            layernorm(xn)

        def feed_forward(n):
            cfg = FEED[FF[n]]
            act.wait_ge(s.stage_act, 1)
            act.sem_inc(s.stage_act, -1)
            if n == 2:
                act.wait_ge(s.angles, 1)
                act.sem_inc(s.angles, -1)
                nc.scalar.activation(ssm[:, 2:4, :], ssm[:, 2:4, :], ACT.Sin).then_inc(s.rotation, 1)
                act.wait_ge(s.decays, 1)
                act.sem_inc(s.decays, -1)
                nc.scalar.activation(ssm[:, 0, :], ssm[:, 0, :], ACT.Exp).then_inc(s.rotation, 1)
            if cfg["gate"]:
                E = cfg["E"]
                act.wait_ge(s.weights_asked, 1)
                act.sem_inc(s.weights_asked, -1)
                nc.scalar.activation(weight[:, :, 0:E], logits[:, :, 0:E], ACT.Exp,
                                     scale=-1.0 if cfg.get("sigmoid") else 1.0).then_inc(s.weights_exp, 1)
                for g in range(NG):
                    act.wait_ge(s.gates_turned, 1)
                    act.sem_inc(s.gates_turned, -1)
                    ins = nc.scalar.activation(gateT[0:E, g * GT:g * GT + GT], bank(g, GT, E), ACT.Copy)
                    ins.then_inc(s.act_done, 1)
                    act.wait_ge(s.act_done, 1)
                    act.sem_inc(s.act_done, -1)
                act.sem_inc(s.gates_ready, 1)
                act.sem_inc(s.gates_there, 1)

            def block(chunks):
                for u in range(NG * len(chunks)):
                    c = chunks[u // NG]
                    act.wait_ge(s.up_done, 1)
                    act.sem_inc(s.up_done, -1)
                    bias = chunk[c][:, 384:385] if cfg.get("hidden_bias") else 0.0
                    to = h_act if cfg["up2"] else h_all
                    nc.scalar.activation(to[u % 2], bank(u % 2), cfg["func"], bias=bias).then_inc(
                        s.h_act_ready if cfg["up2"] else s.h_ready, 1)
            if cfg["loop"]:
                with act.Fori(0, cfg["loop"]) as i:
                    block(range(4))
            block(range(cfg["last"]))

        act.sem_inc(s.row_scores_free, 2)
        act.sem_inc(s.proj_free, 1)
        act.sem_inc(s.proj_even_free, 1)
        act.sem_inc(s.proj_odd_free, 1)
        act.wait_ge(s.start_act, 1)
        act.sem_inc(s.start_act, -1)
        stages(layernorm, self_attention, cross_attention, feed_forward, film_block)

    @block.vector
    def _(dve):
        def stage_ready(ins):
            ins.then_inc(s.dve_done, 1)
            dve.wait_ge(s.dve_done, 1)
            dve.sem_inc(s.dve_done, -1)
            dve.sem_inc(s.stage_pe, 1)
            dve.sem_inc(s.stage_act, 1)

        ident = W("const", "ident")[0:S, 0:S]

        def layernorm(src, eps=0, affine=None, add=False):
            for g in range(NG):
                dve.wait_ge(s.mean, 1)
                dve.sem_inc(s.mean, -1)
                nc.vector.tensor_tensor(group(xn, g), group(src, g), bs(bank(g)), ALU.subtract).then_inc(s.dve_done, 1)
                dve.wait_ge(s.dve_done, 1)
                dve.sem_inc(s.dve_done, -1)
                dve.sem_inc(s.centred, 1)
            for g in range(NG):
                dve.wait_ge(s.deviated, 1)
                dve.sem_inc(s.deviated, -1)
                d = token_dev[:, GB * g:GB * g + GB]
                nc.vector.reciprocal(d, d).then_inc(s.dve_done, 1)
                dve.wait_ge(s.dve_done, 1)
                dve.sem_inc(s.dve_done, -1)
                nc.vector.tensor_tensor(group(deviation, g)[0:S], ident.unsqueeze(1).to_broadcast([S, GB, S]),
                                        d.unsqueeze(2).to_broadcast([S, GB, S]), ALU.mult).then_inc(s.dve_done, 1)
                dve.wait_ge(s.dve_done, 1)
                dve.sem_inc(s.dve_done, -1)
                dve.sem_inc(s.inverse_ready, 1)
            for g in range(NG):
                dve.wait_ge(s.inverse_spread, 1)
                dve.sem_inc(s.inverse_spread, -1)
                ins = nc.vector.tensor_tensor(group(xn, g), group(xn, g), bs(bank(g)), ALU.mult)
                if affine:
                    ins.then_inc(s.dve_done, 1)
                    dve.wait_ge(s.dve_done, 1)
                    dve.sem_inc(s.dve_done, -1)
                    ins = nc.vector.tensor_scalar(group(xn, g), group(xn, g), affine[0], affine[1], ALU.mult, ALU.add)
                ins.then_inc(s.dve_done, 1)
                dve.wait_ge(s.dve_done, 1)
                dve.sem_inc(s.dve_done, -1)
                if add:
                    nc.vector.tensor_tensor(group(x, g), group(x, g), group(xn, g), ALU.add).then_inc(s.dve_done, 1)
                    dve.wait_ge(s.dve_done, 1)
                    dve.sem_inc(s.dve_done, -1)
            dve.sem_inc(s.stage_pe, 1)

        def quantise(w, total, n):
            nc.vector.tensor_scalar(total, total, 1.0 / n, 1e-8, ALU.mult, ALU.max).then_inc(s.dve_done, 1)
            dve.wait_ge(s.dve_done, 1)
            dve.sem_inc(s.dve_done, -1)
            nc.vector.reciprocal(col[:, 15:16], total).then_inc(s.dve_done, 1)
            dve.wait_ge(s.dve_done, 1)
            dve.sem_inc(s.dve_done, -1)
            for v in w:
                t = squares[:, :, :].rearrange("p b t -> p (b t)")[:, 0:v.shape[1]]
                nc.vector.tensor_scalar(t, v, col[:, 15:16], ROUND, ALU.mult, ALU.add).then_inc(s.dve_done, 1)
                dve.wait_ge(s.dve_done, 1)
                dve.sem_inc(s.dve_done, -1)
                nc.vector.tensor_scalar(t, t, ROUND, 2.0, ALU.subtract, ALU.min).then_inc(s.dve_done, 1)
                dve.wait_ge(s.dve_done, 1)
                dve.sem_inc(s.dve_done, -1)
                nc.vector.tensor_scalar(t, t, -2.0, total, ALU.max, ALU.mult).then_inc(s.dve_done, 1)
                dve.wait_ge(s.dve_done, 1)
                dve.sem_inc(s.dve_done, -1)
                nc.vector.tensor_tensor(t, t, v, ALU.subtract).then_inc(s.dve_done, 1)
                dve.wait_ge(s.dve_done, 1)
                dve.sem_inc(s.dve_done, -1)
                nc.vector.tensor_tensor(v, t, v, ALU.add).then_inc(s.dve_done, 1)
                dve.wait_ge(s.dve_done, 1)
                dve.sem_inc(s.dve_done, -1)

        def magnitude(w, c):
            nc.vector.tensor_reduce(col[:, c:c + 1], w, AX.X, ALU.add, apply_absolute_value=True).then_inc(s.dve_done, 1)
            dve.wait_ge(s.dve_done, 1)
            dve.sem_inc(s.dve_done, -1)

        def self_attention(n):
            cfg = SELF[SA[n]]
            nsm, vw = cfg["nsm"], cfg["vw"]
            wst = SA[n]
            dve.wait_ge(loaded[wst], 16)
            if cfg.get("quant"):
                magnitude(W(wst, "wqk"), 0)
                magnitude(W(wst, "wv"), 1)
                magnitude(W(wst, "wo"), 2)
                nc.vector.tensor_tensor(col[:, 0:1], col[:, 0:1], col[:, 1:2], ALU.add).then_inc(s.dve_done, 1)
                dve.wait_ge(s.dve_done, 1)
                dve.sem_inc(s.dve_done, -1)
                dve.sem_inc(s.magnitudes, 1)
                dve.wait_ge(s.totals, 1)
                dve.sem_inc(s.totals, -1)
                nc.vector.tensor_copy(col[:, 3:6], ps[:, 0, 0:3]).then_inc(s.dve_done, 1)
                dve.wait_ge(s.dve_done, 1)
                dve.sem_inc(s.dve_done, -1)
                quantise([W(wst, "wqk"), W(wst, "wv")], col[:, 3:4], 384 * 128)
                quantise([W(wst, "wo")], col[:, 5:6], 128 * 128)
            if cfg.get("diff"):
                for g in range(NG):
                    nc.vector.bn_stats(bn[:, g, :], group(xn, g).rearrange("p b t -> p (b t)")).then_inc(s.dve_done, 1)
                    dve.wait_ge(s.dve_done, 1)
                    dve.sem_inc(s.dve_done, -1)
                nc.vector.bn_aggr(col[:, 0:2], bn[:, :, :]).then_inc(s.dve_done, 1)
                dve.wait_ge(s.dve_done, 1)
                dve.sem_inc(s.dve_done, -1)
                nc.vector.tensor_copy(col[:, 2:3], col[:, 1:2]).then_inc(s.dve_done, 1)
                dve.wait_ge(s.dve_done, 1)
                dve.sem_inc(s.dve_done, -1)
                dve.sem_inc(s.bn_var, 1)
                dve.wait_ge(s.bn_dev, 1)
                dve.sem_inc(s.bn_dev, -1)
                nc.vector.reciprocal(col[:, 3:4], col[:, 2:3]).then_inc(s.dve_done, 1)
                dve.wait_ge(s.dve_done, 1)
                dve.sem_inc(s.dve_done, -1)
                nc.vector.tensor_tensor(col[:, 3:4], col[:, 3:4], W(wst, "bn_g"), ALU.mult).then_inc(s.dve_done, 1)
                dve.wait_ge(s.dve_done, 1)
                dve.sem_inc(s.dve_done, -1)
                for g in range(NG):
                    nc.vector.tensor_scalar(group(xn, g), group(xn, g), col[:, 0:1], col[:, 3:4], ALU.subtract, ALU.mult).then_inc(s.dve_done, 1)
                    dve.wait_ge(s.dve_done, 1)
                    dve.sem_inc(s.dve_done, -1)
                    nc.vector.tensor_scalar(group(xn, g), group(xn, g), W(wst, "bn_b"), None, ALU.add).then_inc(s.dve_done, 1)
                    dve.wait_ge(s.dve_done, 1)
                    dve.sem_inc(s.dve_done, -1)
                lam = W(wst, "lam").rearrange("p (k w) -> p k w", w=8)
                for i in range(2):
                    nc.vector.tensor_tensor(y_rms[:, 8 * i:8 * i + 8], lam[0:S, 2 * i, :], lam[0:S, 2 * i + 1, :], ALU.mult).then_inc(s.dve_done, 1)
                    dve.wait_ge(s.dve_done, 1)
                    dve.sem_inc(s.dve_done, -1)
                nc.vector.tensor_reduce(col[0:S, 4:6], y_rms[:, 0:16].rearrange("p (k w) -> p k w", w=8), AX.X, ALU.add).then_inc(s.dve_done, 1)
                dve.wait_ge(s.dve_done, 1)
                dve.sem_inc(s.dve_done, -1)
                dve.sem_inc(s.lam_sum, 1)
                dve.wait_ge(s.lam_exp, 1)
                dve.sem_inc(s.lam_exp, -1)
                nc.vector.tensor_tensor(col[0:S, 6:7], col[0:S, 5:6], col[0:S, 4:5], ALU.subtract).then_inc(s.dve_done, 1)
                dve.wait_ge(s.dve_done, 1)
                dve.sem_inc(s.dve_done, -1)
                nc.vector.tensor_scalar(col[0:S, 6:7], col[0:S, 6:7], -LAMBDA_INIT, None, ALU.add).then_inc(s.dve_done, 1)
                dve.wait_ge(s.dve_done, 1)
                dve.sem_inc(s.dve_done, -1)
            for b in range(GB):
                nc.vector.memset(vaug[:, b, 0:16 * (vw + 1)], 1.0).then_inc(s.dve_done, 1)
                dve.wait_ge(s.dve_done, 1)
                dve.sem_inc(s.dve_done, -1)
            dve.sem_inc(s.stage_act, 1)
            dve.sem_inc(s.stage_pe, 1)
            with dve.Fori(0, NG) as g:
                nc.vector.tensor_copy(bs(xg[:, :]), xn[:, bass.ds(GB * g, GB), :]).then_inc(s.dve_done, 1)
                dve.wait_ge(s.dve_done, 1)
                dve.sem_inc(s.dve_done, -1)
                dve.sem_inc(s.xg_ready, 1)
                if cfg.get("unit"):
                    for m in range(2):
                        dve.wait_ge(s.head_dev, 1)
                        dve.sem_inc(s.head_dev, -1)
                        norm = group(deviation, 0).rearrange("p b t -> p (b t)")
                        nc.vector.tensor_scalar(norm, norm, 1e-8, None, ALU.max).then_inc(s.dve_done, 1)
                        dve.wait_ge(s.dve_done, 1)
                        dve.sem_inc(s.dve_done, -1)
                        nc.vector.reciprocal(norm, norm).then_inc(s.dve_done, 1)
                        dve.wait_ge(s.dve_done, 1)
                        dve.sem_inc(s.dve_done, -1)
                        nc.vector.tensor_tensor(qk[:, m, :], qk[:, m, :], norm, ALU.mult).then_inc(s.dve_done, 1)
                        dve.wait_ge(s.dve_done, 1)
                        dve.sem_inc(s.dve_done, -1)
                        dve.sem_inc(s.unit_done, 1)
                        dve.sem_inc(s.qk_ready, 1)
                for sm in range(nsm):
                    dve.wait_ge(s.keys_there, 1)
                    dve.sem_inc(s.keys_there, -1)
                    for h in range(ACT_KEYS, DVE_KEYS):
                        ins = nc.vector.tensor_scalar(km[:, HEADS * sm + h, :], qk[:, 2 * sm + 1, :],
                                                      W("const", "head_of")[:, h:h + 1], None, ALU.mult)
                    ins.then_inc(s.km_dve, 1)
                if cfg.get("gate"):
                    dve.wait_ge(s.gate_ready, GB)
                    dve.sem_inc(s.gate_ready, -GB)
                    nc.vector.tensor_scalar(gate[:, :], gate[:, :], 1.0, None, ALU.add).then_inc(s.dve_done, 1)
                    dve.wait_ge(s.dve_done, 1)
                    dve.sem_inc(s.dve_done, -1)
                    nc.vector.reciprocal(gate[:, :], gate[:, :]).then_inc(s.dve_done, 1)
                    dve.wait_ge(s.dve_done, 1)
                    dve.sem_inc(s.dve_done, -1)
                    nc.vector.tensor_scalar(gate[:, :], gate[:, :], 0.1, 2.0, ALU.max, ALU.min).then_inc(s.dve_done, 1)
                    dve.wait_ge(s.dve_done, 1)
                    dve.sem_inc(s.dve_done, -1)
                    for b in range(GB):
                        v = vaug[:, b, 0:16 * (vw + 1)].rearrange("p (h w) -> p h w", w=vw + 1)[:, :, 0:vw]
                        nc.vector.tensor_scalar(v, v, gate[:, b:b + 1], None, ALU.mult).then_inc(s.dve_done, 1)
                        dve.wait_ge(s.dve_done, 1)
                        dve.sem_inc(s.dve_done, -1)
                        dve.sem_inc(s.v_ready, 1)
                N = GB * nsm * 2
                for k in range(N + 1):
                    if k < N:
                        dve.wait_ge(s.scores, 1)
                        dve.sem_inc(s.scores, -1)
                        sc = ps[0:S, 2 * (k % 2):2 * (k % 2) + 2, 0:GT].rearrange("p c (h t) -> p c h t", t=S)
                        mx = smax[:, k % 2, :]
                        nc.vector.tensor_reduce(mx.rearrange("p (c h) -> p c h", c=2), sc, AX.X, ALU.max).then_inc(s.dve_done, 1)
                        dve.wait_ge(s.dve_done, 1)
                        dve.sem_inc(s.dve_done, -1)
                        for c in range(2):
                            one = sc[:, c, :, :]
                            ins = nc.vector.tensor_tensor(one, one, mx[:, 4 * c:4 * c + 4].unsqueeze(2).to_broadcast([S, 4, S]), ALU.subtract)
                            if c == 0:
                                ins.then_inc(s.dve_done, 1)
                                dve.wait_ge(s.dve_done, 1)
                                dve.sem_inc(s.dve_done, -1)
                        ins.then_inc(s.dve_done, 1)
                        dve.wait_ge(s.dve_done, 1)
                        dve.sem_inc(s.dve_done, -1)
                        dve.sem_inc(s.shifted, 1)
                    if k % 2 == 0 and k > 0:
                        item = k // 2 - 1
                        b, sm = item // nsm, item % nsm
                        dve.wait_ge(s.o_full, 1)
                        dve.sem_inc(s.o_full, -1)
                        o = bank(7, 16 * (vw + 1), S).rearrange("p (h w) -> p h w", w=vw + 1)
                        y = y_tok[:, b, 0:16 * vw].rearrange("p (h w) -> p h w", w=vw)
                        nc.vector.reciprocal(rden[:, :].unsqueeze(2), o[:, :, vw:vw + 1]).then_inc(s.dve_done, 1)
                        dve.wait_ge(s.dve_done, 1)
                        dve.sem_inc(s.dve_done, -1)
                        r = rden[:, :].unsqueeze(2).to_broadcast([S, 16, vw])
                        if sm == 0:
                            nc.vector.tensor_tensor(y, o[:, :, 0:vw], r, ALU.mult).then_inc(s.dve_done, 1)
                            dve.wait_ge(s.dve_done, 1)
                            dve.sem_inc(s.dve_done, -1)
                            dve.sem_inc(s.o_free, 1)
                        else:
                            y2 = y_sq[:, b, :].rearrange("p (h w) -> p h w", w=vw)
                            nc.vector.tensor_tensor(y2, o[:, :, 0:vw], r, ALU.mult).then_inc(s.dve_done, 1)
                            dve.wait_ge(s.dve_done, 1)
                            dve.sem_inc(s.dve_done, -1)
                            dve.sem_inc(s.o_free, 1)
                            nc.vector.scalar_tensor_tensor(y_tok[:, b, :], y_sq[:, b, :], col[0:S, 6:7], y_tok[:, b, :], ALU.mult, ALU.add).then_inc(s.dve_done, 1)
                            dve.wait_ge(s.dve_done, 1)
                            dve.sem_inc(s.dve_done, -1)
                if cfg.get("diff"):
                    yf = y_tok[:, :, :].rearrange("p b c -> p (b c)")
                    sq = y_sq[:, :, :].rearrange("p b c -> p (b c)")
                    y3 = yf.rearrange("p (h w) -> p h w", w=16)
                    nc.vector.tensor_tensor(sq, yf, yf, ALU.mult).then_inc(s.dve_done, 1)
                    dve.wait_ge(s.dve_done, 1)
                    dve.sem_inc(s.dve_done, -1)
                    nc.vector.tensor_reduce(y_rms[:, :], sq.rearrange("p (h w) -> p h w", w=16), AX.X, ALU.add).then_inc(s.dve_done, 1)
                    dve.wait_ge(s.dve_done, 1)
                    dve.sem_inc(s.dve_done, -1)
                    nc.vector.tensor_scalar(y_rms[:, :], y_rms[:, :], 1 / 16, None, ALU.mult).then_inc(s.dve_done, 1)
                    dve.wait_ge(s.dve_done, 1)
                    dve.sem_inc(s.dve_done, -1)
                    dve.sem_inc(s.rms_sum, 1)
                    dve.wait_ge(s.rms_root, 1)
                    dve.sem_inc(s.rms_root, -1)
                    nc.vector.reciprocal(y_rms[:, :], y_rms[:, :]).then_inc(s.dve_done, 1)
                    dve.wait_ge(s.dve_done, 1)
                    dve.sem_inc(s.dve_done, -1)
                    nc.vector.tensor_scalar(y_rms[:, :], y_rms[:, :], 1 - LAMBDA_INIT, None, ALU.mult).then_inc(s.dve_done, 1)
                    dve.wait_ge(s.dve_done, 1)
                    dve.sem_inc(s.dve_done, -1)
                    nc.vector.tensor_tensor(y3, y3, y_rms[:, :].unsqueeze(2).to_broadcast([S, GB * 16, 16]), ALU.mult).then_inc(s.dve_done, 1)
                    dve.wait_ge(s.dve_done, 1)
                    dve.sem_inc(s.dve_done, -1)
                    nc.vector.tensor_tensor(y3, y3, W(wst, "subln")[0:S, :].unsqueeze(1).to_broadcast([S, GB * 16, 16]), ALU.mult).then_inc(s.dve_done, 1)
                    dve.wait_ge(s.dve_done, 1)
                    dve.sem_inc(s.dve_done, -1)
                dve.sem_inc(s.y_ready, 1)
                dve.wait_ge(s.out_full, 1)
                dve.sem_inc(s.out_full, -1)
                add = group(squares, 0)
                if cfg["bias"]:
                    nc.vector.tensor_scalar(add, bs(bank(7)), W(wst, "bo"), cfg["out_scale"], ALU.add, ALU.mult).then_inc(s.dve_done, 1)
                    dve.wait_ge(s.dve_done, 1)
                    dve.sem_inc(s.dve_done, -1)
                else:
                    nc.vector.tensor_copy(add, bs(bank(7))).then_inc(s.dve_done, 1)
                    dve.wait_ge(s.dve_done, 1)
                    dve.sem_inc(s.dve_done, -1)
                xd = x[:, bass.ds(GB * g, GB), :]
                nc.vector.tensor_tensor(xd, xd, add, ALU.add).then_inc(s.dve_done, 1)
                dve.wait_ge(s.dve_done, 1)
                dve.sem_inc(s.dve_done, -1)
                dve.sem_inc(s.o_free, 1)
            dve.sem_inc(s.stage_pe, 1)

        def cross_attention(n):
            cfg = CROSS[CA[n]]
            H, wst = cfg["H"], CA[n]
            nU = -(-H // 4)
            w = min(H, 4)
            parts = where[wst]
            dve.wait_ge(loaded[wst], 16)
            dve.sem_inc(s.stage_pe, 1)
            folds = [0]

            def fold(to, cols, rows):
                dve.wait_ge(s.side_full, 1)
                dve.sem_inc(s.side_full, -1)
                nc.vector.tensor_copy(to, bank(6 + folds[0] % 2, cols, rows)).then_inc(s.dve_done, 1)
                dve.wait_ge(s.dve_done, 1)
                dve.sem_inc(s.dve_done, -1)
                dve.sem_inc(s.side_free, 1)
                folds[0] += 1

            for h in range(H):
                fold(wfold[:, h * QR:h * QR + QR], QR, 128)
                if "bq" in parts:
                    fold(bfold[:, h:h + 1], 1, QR)
                if "wo" in parts:
                    fold(vfold[:, h * 128:h * 128 + 128], 128, C + 1)
            if "wvo" in parts:
                nc.vector.tensor_copy(vfold[:, 0:128], W(wst, "wvo")).then_inc(s.dve_done, 1)
                dve.wait_ge(s.dve_done, 1)
                dve.sem_inc(s.dve_done, -1)
            if "bo" in parts:
                nc.vector.tensor_copy(col[:, 7:8], W(wst, "bo")).then_inc(s.dve_done, 1)
                dve.wait_ge(s.dve_done, 1)
                dve.sem_inc(s.dve_done, -1)
            if H == 1:
                dve.sem_inc(s.w_cross_free, 1)
            else:
                nc.vector.memset(ctxT_bf[C:QR, :], 1.0).then_inc(s.dve_done, 1)
                dve.wait_ge(s.dve_done, 1)
                dve.sem_inc(s.dve_done, -1)
                for i in range(2):
                    for v, hi, lo in ((ctxT[i][C:QR, :], ctxT_hi[i][C:QR, :], ctxT_lo[i][C:QR, :]),
                                      (ctxk[i][:, :, C:C + 1], ctxk_hi[i][:, :, C:C + 1], ctxk_lo[i][:, :, C:C + 1])):
                        nc.vector.tensor_copy(hi, v).then_inc(s.dve_done, 1)
                        dve.wait_ge(s.dve_done, 1)
                        dve.sem_inc(s.dve_done, -1)
                        nc.vector.tensor_tensor(lo, v, hi, ALU.subtract).then_inc(s.dve_done, 1)
                        dve.wait_ge(s.dve_done, 1)
                        dve.sem_inc(s.dve_done, -1)
                dve.sem_inc(s.stage_pool, 1)
                dve.sem_inc(s.ctxT_free, 1)
            dve.sem_inc(s.stage_pe, 1)
            dve.sem_inc(s.stage_act, 1)
            dve.sem_inc(s.ctx_bf_free, 1)
            count = [0]

            def side(kind, arg, b, par):
                if kind in ("q_round", "q_low"):
                    hs = slice(4 * arg, 4 * arg + w)
                    o, q = qa_hi[1 - par][:, hs, :], bs(q_full)
                    if kind == "q_round":
                        nc.vector.tensor_copy(qa_bf[:, hs, :], q)
                        nc.vector.tensor_copy(o, q).then_inc(s.dve_done, 1)
                        dve.wait_ge(s.dve_done, 1)
                        dve.sem_inc(s.dve_done, -1)
                        dve.sem_inc(s.q_bf, 1)
                    else:
                        nc.vector.tensor_tensor(qa_lo[1 - par][:, hs, :], q, o, ALU.subtract).then_inc(s.dve_done, 1)
                        dve.wait_ge(s.dve_done, 1)
                        dve.sem_inc(s.dve_done, -1)
                    return
                if kind == "recips":
                    if H > 1:
                        if arg == 0:
                            dve.wait_ge(s.den_loaded, 16)
                            dve.sem_inc(s.den_loaded, -16)
                            dve.wait_ge(s.u_raw_ready, nU)
                            dve.sem_inc(s.u_raw_ready, -nU)
                            nc.vector.reciprocal(den_rows[:, :], den_rows[:, :]).then_inc(s.dve_done, 1)
                            dve.wait_ge(s.dve_done, 1)
                            dve.sem_inc(s.dve_done, -1)
                            return
                        nc.vector.tensor_tensor(rexp, den_rows[:, :].unsqueeze(1).to_broadcast([H, H, S]),
                                                W("const", "ident")[0:H, 0:H].unsqueeze(2).to_broadcast([H, H, S]),
                                                ALU.mult).then_inc(s.dve_done, 1)
                        dve.wait_ge(s.dve_done, 1)
                        dve.sem_inc(s.dve_done, -1)
                        dve.sem_inc(s.rexp_ready, 1)
                    return
                k = 6 + count[0] % 2
                if (kind, arg) != ("maxima", 1):
                    count[0] += 1
                if kind == "spread":
                    g = arg
                    hs = slice(4 * g, 4 * g + w)
                    dve.wait_ge(s.side_full, 1)
                    dve.sem_inc(s.side_full, -1)
                    if H > 1:
                        nc.vector.tensor_tensor(u_rec[:, hs, :], bs(bank(k, w * S, C + 1)), u_raw[:, hs, :], ALU.mult).then_inc(s.dve_done, 1)
                        dve.wait_ge(s.dve_done, 1)
                        dve.sem_inc(s.dve_done, -1)
                        dve.sem_inc(s.side_free, 1)
                        dve.sem_inc(s.u_ready, 1)
                        return
                    nc.vector.reciprocal(u_rec[:, hs, :], bs(bank(k, w * S, C + 1))).then_inc(s.dve_done, 1)
                    dve.wait_ge(s.dve_done, 1)
                    dve.sem_inc(s.dve_done, -1)
                    dve.sem_inc(s.side_free, 1)
                    nc.vector.tensor_tensor(u_rec[:, hs, :], u_rec[:, hs, :], u_raw[:, hs, :], ALU.mult).then_inc(s.dve_done, 1)
                    dve.wait_ge(s.dve_done, 1)
                    dve.sem_inc(s.dve_done, -1)
                    dve.sem_inc(s.u_ready, 1)
                elif kind == "project":
                    dve.wait_ge(s.side_full, 1)
                    dve.sem_inc(s.side_full, -1)
                    xd = x[:, bass.ds(b - 1, 1), :]
                    y = bs(bank(k, S))
                    if "bo" in parts:
                        nc.vector.scalar_tensor_tensor(xd, y, col[:, 7:8], xd, ALU.add, ALU.add).then_inc(s.dve_done, 1)
                        dve.wait_ge(s.dve_done, 1)
                        dve.sem_inc(s.dve_done, -1)
                        dve.sem_inc(s.side_free, 1)
                    else:
                        nc.vector.tensor_tensor(xd, y, xd, ALU.add).then_inc(s.dve_done, 1)
                        dve.wait_ge(s.dve_done, 1)
                        dve.sem_inc(s.dve_done, -1)
                        dve.sem_inc(s.side_free, 1)
                elif kind == "query":
                    g = arg
                    hs = slice(4 * g, 4 * g + w)
                    dve.wait_ge(s.side_full, 1)
                    dve.sem_inc(s.side_full, -1)
                    i = bs(bank(k, w * S, QR))
                    if H > 1:
                        q = bs(q_full)
                        if "bq" in parts:
                            ins = nc.vector.tensor_tensor(q, i, bfold[:, hs].unsqueeze(2).to_broadcast([QR, w, S]), ALU.add)
                        else:
                            ins = nc.vector.tensor_copy(q, i)
                        ins.then_inc(s.dve_done, 1)
                        dve.wait_ge(s.dve_done, 1)
                        dve.sem_inc(s.dve_done, -1)
                        dve.sem_inc(s.side_free, 1)
                        return
                    o = qa[1 - par][:, :, :]
                    if "bq" in parts:
                        ins = nc.vector.tensor_tensor(o, i, bfold[:, hs].unsqueeze(2).to_broadcast([QR, w, S]), ALU.add)
                    else:
                        ins = nc.vector.tensor_copy(o, i)
                    ins.then_inc(s.dve_done, 1)
                    dve.wait_ge(s.dve_done, 1)
                    dve.sem_inc(s.dve_done, -1)
                    dve.sem_inc(s.side_free, 1)
                    dve.sem_inc(s.q_ready, 1)
                elif kind == "chunk":
                    h, c = arg
                    dve.wait_ge(s.side_full, 1)
                    dve.sem_inc(s.side_full, -1)
                    a, z = CHUNKS[c]
                    ins = nc.vector.tensor_reduce(mparts[:, h, c:c + 1], bank(k, z - a, S), AX.X, ALU.max)
                    if (h, c) == (H - 1, 2):
                        ins.then_inc(s.dve_done, 1)
                        dve.wait_ge(s.dve_done, 1)
                        dve.sem_inc(s.dve_done, -1)
                        dve.sem_inc(s.side_free, 1)
                        dve.sem_inc(s.ctx_bf_free, 1)
                        nc.vector.tensor_reduce(mrows[:, C:C + H], mparts[:, 0:H, :], AX.X, ALU.max).then_inc(s.dve_done, 1)
                        dve.wait_ge(s.dve_done, 1)
                        dve.sem_inc(s.dve_done, -1)
                        dve.sem_inc(s.maxima_ready, 1)
                    else:
                        ins.then_inc(s.side_free, 1)
                else:
                    p = slice(C, C + HEADS)
                    if H == 1:
                        dve.wait_ge(s.side_full, 1)
                        dve.sem_inc(s.side_full, -1)
                        nc.vector.tensor_tensor(qa[1 - par][p, 0:1, :], ps[p, k, 0:S].unsqueeze(1).to_broadcast([HEADS, 1, S]),
                                                own_head[p, 0:1].unsqueeze(2).to_broadcast([HEADS, 1, S]), ALU.mult).then_inc(s.dve_done, 1)
                        dve.wait_ge(s.dve_done, 1)
                        dve.sem_inc(s.dve_done, -1)
                        dve.sem_inc(s.side_free, 1)
                        dve.sem_inc(s.qa_ready, 1)
                        return
                    hs = slice(8 * arg, 8 * arg + 8)
                    if arg == 0:
                        dve.wait_ge(s.side_full, 1)
                        dve.sem_inc(s.side_full, -1)
                        max_bank.append(k)
                    ins = nc.vector.tensor_tensor(qa_hi[1 - par][p, hs, :], ps[p, max_bank[-1], 0:S].unsqueeze(1).to_broadcast([HEADS, 8, S]),
                                                  own_head[p, hs].unsqueeze(2).to_broadcast([HEADS, 8, S]), ALU.mult)
                    if arg == 1:
                        ins.then_inc(s.dve_done, 1)
                        dve.wait_ge(s.dve_done, 1)
                        dve.sem_inc(s.dve_done, -1)
                        dve.sem_inc(s.side_free, 1)
                        dve.sem_inc(s.qa_ready, 1)

            max_bank = []
            own_head = W("const", "own_head")

            def lows(u):
                dve.wait_ge(s.pexp_ready, 1)
                dve.sem_inc(s.pexp_ready, -1)
                dve.wait_ge(s.pexp_hi_ready, 1)
                dve.sem_inc(s.pexp_hi_ready, -1)
                rows = key_rows_of(units(H)[u][0][0])
                nc.vector.tensor_tensor(pexp_lo[u % 3][0:rows, :], pexp[u % 3][0:rows, :], pexp_hi[u % 3][0:rows, :],
                                        ALU.subtract).then_inc(s.pexp_lo_ready, 1)

            def batch(b, par, prep, tail, main=True):
                nu = len(units(H)) if main and H > 1 else 0
                at = side_places(H, prep, tail, main)
                if nu:
                    lows(0)
                for u in range(nu):
                    if u + 1 < nu:
                        lows(u + 1)
                    for it in at.pop(u, []):
                        side(*it, b, par)
                for p in sorted(at):
                    for it in at[p]:
                        side(*it, b, par)
            batch(-1, 1, True, False, main=False)
            batch(0, 0, True, False)
            c0 = count[0]
            with dve.Fori(0, B // 2 - 1) as i:
                batch(2 * i + 1, 1, True, True)
                batch(2 * i + 2, 0, True, True)
            assert (count[0] - c0) % 2 == 0
            batch(B - 1, 1, False, True)
            batch(B, 0, False, True, main=False)
            if H > 1:
                for i in range(2):
                    nc.vector.memset(ctxT[i][C:QR, :], 1.0).then_inc(s.dve_done, 1)
                    dve.wait_ge(s.dve_done, 1)
                    dve.sem_inc(s.dve_done, -1)
                    nc.vector.memset(ctxk[i][:, :, C:C + 1], 1.0).then_inc(s.dve_done, 1)
                    dve.wait_ge(s.dve_done, 1)
                    dve.sem_inc(s.dve_done, -1)
                dve.sem_inc(s.w_cross_free, 1)
            dve.sem_inc(s.stage_pe, 1)

        def route(n):
            cfg = FEED[FF[n]]
            E = cfg["E"]
            dve.wait_ge(s.logits_ready, 1)
            dve.sem_inc(s.logits_ready, -1)
            lg, bi, rk, wt = (t[:, :, 0:E] for t in (logits, biased, rank, weight))
            nc.vector.tensor_copy(lg, ps[0:S, 0, 0:B * E].rearrange("p (b e) -> p b e", e=E)).then_inc(s.dve_done, 1)
            dve.wait_ge(s.dve_done, 1)
            dve.sem_inc(s.dve_done, -1)
            by = lg
            if cfg.get("sigmoid"):
                nc.vector.tensor_tensor(bi, lg, W(FF[n], "expert_b")[0:S, :].unsqueeze(1).to_broadcast([S, B, E]), ALU.add).then_inc(s.dve_done, 1)
                dve.wait_ge(s.dve_done, 1)
                dve.sem_inc(s.dve_done, -1)
                by = bi
            else:
                nc.vector.tensor_reduce(best[:, :], lg, AX.X, ALU.max).then_inc(s.dve_done, 1)
                dve.wait_ge(s.dve_done, 1)
                dve.sem_inc(s.dve_done, -1)
                nc.vector.tensor_tensor(lg, lg, best[:, :].unsqueeze(2).to_broadcast([S, B, E]), ALU.subtract).then_inc(s.dve_done, 1)
                dve.wait_ge(s.dve_done, 1)
                dve.sem_inc(s.dve_done, -1)
            dve.sem_inc(s.weights_asked, 1)
            p1 = pairs[:, 0:B * E * E].rearrange("p (b e f) -> p b e f", e=E, f=E)
            p2 = pairs2[:, 0:B * E * E].rearrange("p (b e f) -> p b e f", e=E, f=E)
            mine, other = by.unsqueeze(3).to_broadcast([S, B, E, E]), by.unsqueeze(2).to_broadcast([S, B, E, E])
            before = W("const", "before")[0:S, :].rearrange("p (e f) -> p e f", f=16)[:, 0:E, 0:E]
            nc.vector.tensor_tensor(p1, other, mine, ALU.is_equal).then_inc(s.dve_done, 1)
            dve.wait_ge(s.dve_done, 1)
            dve.sem_inc(s.dve_done, -1)
            nc.vector.tensor_tensor(p1, p1, before.unsqueeze(1).to_broadcast([S, B, E, E]), ALU.mult).then_inc(s.dve_done, 1)
            dve.wait_ge(s.dve_done, 1)
            dve.sem_inc(s.dve_done, -1)
            nc.vector.tensor_tensor(p2, other, mine, ALU.is_gt).then_inc(s.dve_done, 1)
            dve.wait_ge(s.dve_done, 1)
            dve.sem_inc(s.dve_done, -1)
            nc.vector.tensor_tensor(p1, p1, p2, ALU.add).then_inc(s.dve_done, 1)
            dve.wait_ge(s.dve_done, 1)
            dve.sem_inc(s.dve_done, -1)
            nc.vector.tensor_reduce(rk, p1, AX.X, ALU.add).then_inc(s.dve_done, 1)
            dve.wait_ge(s.dve_done, 1)
            dve.sem_inc(s.dve_done, -1)
            nc.vector.tensor_scalar(rk, rk, 2.0, None, ALU.is_lt).then_inc(s.dve_done, 1)
            dve.wait_ge(s.dve_done, 1)
            dve.sem_inc(s.dve_done, -1)
            dve.wait_ge(s.weights_exp, 1)
            dve.sem_inc(s.weights_exp, -1)
            if cfg.get("sigmoid"):
                nc.vector.tensor_scalar(wt, wt, 1.0, None, ALU.add).then_inc(s.dve_done, 1)
                dve.wait_ge(s.dve_done, 1)
                dve.sem_inc(s.dve_done, -1)
                nc.vector.reciprocal(wt, wt).then_inc(s.dve_done, 1)
                dve.wait_ge(s.dve_done, 1)
                dve.sem_inc(s.dve_done, -1)
            nc.vector.tensor_tensor(wt, wt, rk, ALU.mult).then_inc(s.dve_done, 1)
            dve.wait_ge(s.dve_done, 1)
            dve.sem_inc(s.dve_done, -1)
            nc.vector.tensor_reduce(best[:, :], wt, AX.X, ALU.add).then_inc(s.dve_done, 1)
            dve.wait_ge(s.dve_done, 1)
            dve.sem_inc(s.dve_done, -1)
            if cfg.get("sigmoid"):
                nc.vector.tensor_scalar(best[:, :], best[:, :], 1e-10, None, ALU.add).then_inc(s.dve_done, 1)
                dve.wait_ge(s.dve_done, 1)
                dve.sem_inc(s.dve_done, -1)
            nc.vector.reciprocal(best[:, :], best[:, :]).then_inc(s.dve_done, 1)
            dve.wait_ge(s.dve_done, 1)
            dve.sem_inc(s.dve_done, -1)
            nc.vector.tensor_tensor(wt, wt, best[:, :].unsqueeze(2).to_broadcast([S, B, E]), ALU.mult).then_inc(s.dve_done, 1)
            dve.wait_ge(s.dve_done, 1)
            dve.sem_inc(s.dve_done, -1)
            dve.sem_inc(s.weights_ready, 1)

        def impulse_response():
            p = {k: W("tk", k) for k in ("A_re", "A_im", "C_re", "C_im", "log_dt")}
            dt, z = col[:, 0:1], col[:, 1:2]
            row = [ssm[:, i, :] for i in range(12)]

            def tt(o, a, b, op):
                nc.vector.tensor_tensor(o, a, b, op).then_inc(s.dve_done, 1)
                dve.wait_ge(s.dve_done, 1)
                dve.sem_inc(s.dve_done, -1)

            def ts(o, a, c1, c2, op1, op2):
                nc.vector.tensor_scalar(o, a, c1, c2, op1, op2).then_inc(s.dve_done, 1)
                dve.wait_ge(s.dve_done, 1)
                dve.sem_inc(s.dve_done, -1)

            ts(z, p["log_dt"], 1 / 32, None, ALU.mult, ALU.bypass)
            ts(dt, z, 1 / math.factorial(8), 1 / math.factorial(7), ALU.mult, ALU.add)
            for k in range(6, -1, -1):
                ts(dt, dt, z, 1 / math.factorial(k), ALU.mult, ALU.add)
            for _ in range(5):
                tt(dt, dt, dt, ALU.mult)
            ts(row[1], p["A_im"], dt, None, ALU.mult, ALU.bypass)
            ts(row[4], row[1], 1 / (2 * math.pi), ROUND, ALU.mult, ALU.add)
            ts(row[4], row[4], ROUND, None, ALU.subtract, ALU.bypass)
            part1 = 6.28125
            part2 = float(np.float32(np.round((2 * math.pi - part1) * 2 ** 20) / 2 ** 20))
            for part in (part1, part2, 2 * math.pi - part1 - part2):
                ts(row[5], row[4], part, None, ALU.mult, ALU.bypass)
                tt(row[1], row[1], row[5], ALU.subtract)
            ts(row[2], row[1], math.pi / 2, None, ALU.add, ALU.bypass)
            ts(row[5], row[2], math.pi, 2 * math.pi, ALU.is_gt, ALU.mult)
            tt(row[2], row[2], row[5], ALU.subtract)
            ts(row[2], row[2], 3.1415925, -3.1415925, ALU.min, ALU.max)
            ts(row[3], row[1], 3.1415925, -3.1415925, ALU.min, ALU.max)
            dve.sem_inc(s.angles, 1)
            ts(row[0], p["A_re"], dt, None, ALU.mult, ALU.bypass)
            dve.sem_inc(s.decays, 1)
            dve.wait_ge(s.rotation, 2)
            dve.sem_inc(s.rotation, -2)
            w1r, w1i = powers[0][0][:, 1, :], powers[0][1][:, 1, :]
            tt(w1r, row[0], row[2], ALU.mult)
            tt(w1i, row[0], row[3], ALU.mult)
            ts(row[4], w1r, -1.0, None, ALU.add, ALU.bypass)
            tt(row[5], p["C_re"], row[4], ALU.mult)
            tt(row[6], p["C_im"], w1i, ALU.mult)
            tt(row[5], row[5], row[6], ALU.subtract)
            tt(row[6], p["C_re"], w1i, ALU.mult)
            tt(row[7], p["C_im"], row[4], ALU.mult)
            tt(row[6], row[6], row[7], ALU.add)
            tt(row[7], p["A_re"], p["A_re"], ALU.mult)
            tt(row[8], p["A_im"], p["A_im"], ALU.mult)
            tt(row[7], row[7], row[8], ALU.add)
            nc.vector.reciprocal(row[7], row[7]).then_inc(s.dve_done, 1)
            dve.wait_ge(s.dve_done, 1)
            dve.sem_inc(s.dve_done, -1)
            ts(row[7], row[7], 2.0, None, ALU.mult, ALU.bypass)
            tt(row[8], row[5], p["A_re"], ALU.mult)
            tt(row[9], row[6], p["A_im"], ALU.mult)
            tt(row[8], row[8], row[9], ALU.add)
            tt(row[8], row[8], row[7], ALU.mult)
            tt(row[9], row[6], p["A_re"], ALU.mult)
            tt(row[10], row[5], p["A_im"], ALU.mult)
            tt(row[9], row[9], row[10], ALU.subtract)
            tt(row[9], row[9], row[7], ALU.mult)

            def times(o, a, b, n):
                t0, t1 = (t.rearrange("p (r k) -> p r k", k=STATES)[:, 0:n, :] for t in scratch[:2])
                tt(t0, a[0], b[0], ALU.mult)
                tt(t1, a[1], b[1], ALU.mult)
                t2 = scratch[2].rearrange("p (r k) -> p r k", k=STATES)[:, 0:n, :]
                tt(t2, a[0], b[1], ALU.mult)
                tt(t0, t0, t1, ALU.subtract)
                tt(t1, a[1], b[0], ALU.mult)
                tt(o[1], t2, t1, ALU.add)
                nc.vector.tensor_copy(o[0], t0).then_inc(s.dve_done, 1)
                dve.wait_ge(s.dve_done, 1)
                dve.sem_inc(s.dve_done, -1)

            for base in range(2):
                P = powers[base]
                nc.vector.memset(P[0][:, 0, :], 1.0).then_inc(s.dve_done, 1)
                dve.wait_ge(s.dve_done, 1)
                dve.sem_inc(s.dve_done, -1)
                nc.vector.memset(P[1][:, 0, :], 0.0).then_inc(s.dve_done, 1)
                dve.wait_ge(s.dve_done, 1)
                dve.sem_inc(s.dve_done, -1)
                if base == 1:
                    for part in range(2):
                        nc.vector.tensor_copy(P[part][:, 1, :], powers[0][part][:, LAGS, :]).then_inc(s.dve_done, 1)
                        dve.wait_ge(s.dve_done, 1)
                        dve.sem_inc(s.dve_done, -1)
                have = 1
                while have < LAGS:
                    n = min(have, LAGS - have)
                    times([q[:, have + 1:have + 1 + n, :] for q in P], [q[:, 1:1 + n, :] for q in P],
                          [q[:, have:have + 1, :].to_broadcast([128, n, STATES]) for q in P], n)
                    have += n
            P = powers[1]
            times([q[:, 0:LAGS, :] for q in P], [q[:, 0:LAGS, :] for q in P],
                  [row[i].unsqueeze(1).to_broadcast([128, LAGS, STATES]) for i in (8, 9)], LAGS)
            v = [q.rearrange("p (a b) k -> p a b k", b=LAGS) for q in prods]
            for part in range(2):
                tt(v[part], powers[1][part][:, 0:LAGS, :].unsqueeze(2).to_broadcast([128, LAGS, LAGS, STATES]),
                   powers[0][part][:, 0:LAGS, :].unsqueeze(1).to_broadcast([128, LAGS, LAGS, STATES]), ALU.mult)
            tt(prods[0], prods[0], prods[1], ALU.subtract)
            nc.vector.tensor_reduce(kernel_l[:, :], prods[0], AX.X, ALU.add).then_inc(s.dve_done, 1)
            dve.wait_ge(s.dve_done, 1)
            dve.sem_inc(s.dve_done, -1)

        def film_block(layernorm, feed_forward):
            layernorm(x)
            nc.vector.tensor_copy(mid[:, :, :], xn[:, :, :]).then_inc(s.dve_done, 1)
            dve.wait_ge(s.dve_done, 1)
            dve.sem_inc(s.dve_done, -1)
            dve.sem_inc(s.stage_pe, 1)
            dve.sem_inc(s.stage_act, 1)
            dve.sem_inc(s.masks_asked, 1)
            for h in range(TH):
                dve.wait_ge(s.side_full, 1)
                dve.sem_inc(s.side_full, -1)
                nc.vector.tensor_copy(wf4[:, h * C:h * C + C], bank(6 + h % 2, C)).then_inc(s.dve_done, 1)
                dve.wait_ge(s.dve_done, 1)
                dve.sem_inc(s.dve_done, -1)
                dve.sem_inc(s.side_free, 1)
            dve.sem_inc(s.stage_pe, 1)

            def head(h, last):
                dve.wait_ge(s.scores_there, 1)
                dve.sem_inc(s.scores_there, -1)
                sc = scores_sb[h % 2]
                nc.vector.max(top8[:, 0, :], sc).then_inc(s.dve_done, 1)
                dve.wait_ge(s.dve_done, 1)
                dve.sem_inc(s.dve_done, -1)
                nc.vector.tensor_scalar(low[:, h % 2:h % 2 + 1], top8[:, 0, 0:1], -1.0, None, ALU.mult).then_inc(s.dve_done, 1)
                dve.wait_ge(s.dve_done, 1)
                dve.sem_inc(s.dve_done, -1)
                dve.sem_inc(s.low_ready, 1)
                for r in range(TOP // 8):
                    if r:
                        nc.vector.max(top8[:, r, :], left).then_inc(s.dve_done, 1)
                        dve.wait_ge(s.dve_done, 1)
                        dve.sem_inc(s.dve_done, -1)
                    nc.vector.match_replace(left, top8[:, r, :], sc if r == 0 else left, TAKEN).then_inc(s.dve_done, 1)
                    dve.wait_ge(s.dve_done, 1)
                    dve.sem_inc(s.dve_done, -1)
                dve.wait_ge(s.expd_ready, 1)
                dve.sem_inc(s.expd_ready, -1)
                if h == 0:
                    dve.wait_ge(s.kept_free, 1)
                    dve.sem_inc(s.kept_free, -1)
                nc.vector.scalar_tensor_tensor(kept[:, h, :], left, TAKEN, expd[h % 2], ALU.is_equal, ALU.mult,
                                               accum_out=den[:, h:h + 1]).then_inc(s.dve_done, 1)
                dve.wait_ge(s.dve_done, 1)
                dve.sem_inc(s.dve_done, -1)
                dve.sem_inc(s.scores_sb_free, 1)
                nc.vector.reciprocal(den[:, h:h + 1], den[:, h:h + 1]).then_inc(s.dve_done, 1)
                dve.wait_ge(s.dve_done, 1)
                dve.sem_inc(s.dve_done, -1)
                nc.vector.tensor_scalar(turn_scale[:, h, :], W("const", "ident")[0:S, 0:S], den[:, h:h + 1], 1 / TH,
                                        ALU.mult, ALU.mult).then_inc(s.dve_done, 1)
                dve.wait_ge(s.dve_done, 1)
                dve.sem_inc(s.dve_done, -1)
                dve.sem_inc(s.kept_ready, 1)
            dve.sem_inc(s.kept_free, 1)
            dve.sem_inc(s.scores_sb_free, 2)
            with dve.Fori(0, B) as i:
                for h in range(TH):
                    head(h, False)
            dve.wait_ge(s.kept_free, 1)
            dve.sem_inc(s.kept_free, -1)
            dve.wait_ge(s.ct_ready, 1)
            dve.sem_inc(s.ct_ready, -1)
            dve.wait_ge(s.text_mask_loaded, 16)
            dve.sem_inc(s.text_mask_loaded, -16)
            nc.vector.tensor_tensor(ct[:, :, :].rearrange("p b t -> p (b t)"), ct[:, :, :].rearrange("p b t -> p (b t)"),
                                    text_mask.bitcast(U8), ALU.mult).then_inc(s.dve_done, 1)
            dve.wait_ge(s.dve_done, 1)
            dve.sem_inc(s.dve_done, -1)
            dve.sem_inc(s.stage_pe, 1)
            layernorm(mid, affine=(W("tk", "g_in"), W("tk", "b_in")))
            modulate("film_in", xn)
            y = squares
            nc.vector.tensor_scalar(y[:, :, :], xn[:, :, :], W("tk", "skip"), None, ALU.mult).then_inc(s.dve_done, 1)
            dve.wait_ge(s.dve_done, 1)
            dve.sem_inc(s.dve_done, -1)
            for j in range(S):
                nc.vector.scalar_tensor_tensor(y[:, :, j:S], xn[:, :, 0:S - j], kernel_l[:, j:j + 1], y[:, :, j:S],
                                               ALU.mult, ALU.add).then_inc(s.dve_done, 1)
                dve.wait_ge(s.dve_done, 1)
                dve.sem_inc(s.dve_done, -1)
            modulate("film_out", y)
            nc.vector.tensor_tensor(mid[:, :, :], mid[:, :, :], y[:, :, :], ALU.add).then_inc(s.dve_done, 1)
            dve.wait_ge(s.dve_done, 1)
            dve.sem_inc(s.dve_done, -1)
            dve.sem_inc(s.stage_pe, 1)
            layernorm(mid, affine=(W("tk", "g_ffn"), W("tk", "b_ffn")))
            feed_forward(3)
            layernorm(xn, affine=(W("tk", "g_out"), W("tk", "b_out")), add=True)

        def modulate(name, t):
            bias, mod = W("tk", "b_" + name), W("tk", "mod")
            for g in range(NG):
                dve.wait_ge(s.film_full, 1)
                dve.sem_inc(s.film_full, -1)
                for c in range(2):
                    f = group(deviation, g)
                    nc.vector.tensor_scalar(f, bs(bank(2 * (g % 2) + c)), bias[:, c:c + 1], mod, ALU.add, ALU.mult).then_inc(s.dve_done, 1)
                    dve.wait_ge(s.dve_done, 1)
                    dve.sem_inc(s.dve_done, -1)
                    if c == 0:
                        nc.vector.scalar_tensor_tensor(group(t, g), f, 1.0, group(t, g), ALU.add, ALU.mult).then_inc(s.dve_done, 1)
                        dve.wait_ge(s.dve_done, 1)
                        dve.sem_inc(s.dve_done, -1)
                    else:
                        nc.vector.tensor_tensor(group(t, g), group(t, g), f, ALU.add).then_inc(s.dve_done, 1)
                        dve.wait_ge(s.dve_done, 1)
                        dve.sem_inc(s.dve_done, -1)
                dve.sem_inc(s.film_free, 1)

        def feed_forward(n):
            cfg = FEED[FF[n]]
            dve.wait_ge(loaded[FF[n]], 16)
            dve.sem_inc(s.stage_pe, 1)
            dve.sem_inc(s.stage_act, 1)
            if cfg["gate"]:
                route(n)
                for g in range(NG):
                    dve.sem_inc(gate_free[g], 1)

            def block(chunks, gated):
                for u in range(NG * len(chunks)):
                    c, g = chunks[u // NG], u % NG
                    dve.wait_ge(s.h_act_ready, 1)
                    dve.sem_inc(s.h_act_ready, -1)
                    if gated and (c == 0 or cfg["gate"] == "chunk"):
                        dve.wait_ge(gate_loaded[g], 16 if cfg["gate"] == "block" else 32)
                        dve.sem_inc(gate_loaded[g], -(16 if cfg["gate"] == "block" else 32))
                    up2 = bank(2 + u % 2)
                    to = h_all[u % 2]
                    if cfg.get("hidden_bias"):
                        ins = nc.vector.scalar_tensor_tensor(to, up2, chunk[c][:, 385:386], h_act[u % 2], ALU.add, ALU.mult)
                    else:
                        ins = nc.vector.tensor_tensor(to, up2, h_act[u % 2], ALU.mult)
                    if gated:
                        ins.then_inc(s.dve_done, 1)
                        dve.wait_ge(s.dve_done, 1)
                        dve.sem_inc(s.dve_done, -1)
                        ins = nc.vector.tensor_tensor(to, to, gate_rows[g], ALU.mult)
                        if c == 3 or cfg["gate"] == "chunk":
                            ins.then_inc(s.dve_done, 1)
                            dve.wait_ge(s.dve_done, 1)
                            dve.sem_inc(s.dve_done, -1)
                            dve.sem_inc(s.h_ready, 1)
                            dve.sem_inc(gate_free[g], 1)
                            continue
                    ins.then_inc(s.h_ready, 1)
            if cfg["up2"]:
                if cfg["loop"]:
                    with dve.Fori(0, cfg["loop"]) as i:
                        block(range(4), True)
                block(range(cfg["last"]), cfg["last"] == 4)
            if n == 2:
                dve.wait_ge(loaded["tk"], 16)
                impulse_response()
            for g in range(NG):
                dve.wait_ge(s.down_done, 1)
                dve.sem_inc(s.down_done, -1)
                xd = group(x, g)
                if n in (2, 3):
                    nc.vector.tensor_tensor(group(xn, g), bs(bank(4 + g)), group(xn if n == 2 else mid, g), ALU.add).then_inc(s.dve_done, 1)
                    dve.wait_ge(s.dve_done, 1)
                    dve.sem_inc(s.dve_done, -1)
                else:
                    nc.vector.tensor_tensor(xd, bs(bank(4 + g)), xd, ALU.add).then_inc(s.dve_done, 1)
                    dve.wait_ge(s.dve_done, 1)
                    dve.sem_inc(s.dve_done, -1)
            dve.sem_inc(s.stage_pe, 1)

        dve.sem_inc(s.o_free, 1)
        dve.sem_inc(s.side_free, 2)
        dve.wait_ge(s.x_loaded, 16)
        dve.wait_ge(loaded["const"], 16)
        dve.wait_ge(loaded["sa0"], 16)
        for i, v in enumerate((1e-5, 1e-6)):
            nc.vector.memset(eps[:, i:i + 1], v).then_inc(s.dve_done, 1)
            dve.wait_ge(s.dve_done, 1)
            dve.sem_inc(s.dve_done, -1)
        nc.vector.memset(mrows[:, :], 0.0).then_inc(s.dve_done, 1)
        dve.wait_ge(s.dve_done, 1)
        dve.sem_inc(s.dve_done, -1)
        for i in range(2):
            nc.vector.memset(ctxT[i][C:QR, :], 1.0).then_inc(s.dve_done, 1)
            dve.wait_ge(s.dve_done, 1)
            dve.sem_inc(s.dve_done, -1)
            nc.vector.memset(ctxk[i][:, :, C:C + 1], 1.0).then_inc(s.dve_done, 1)
            dve.wait_ge(s.dve_done, 1)
            dve.sem_inc(s.dve_done, -1)
        nc.vector.tensor_copy(ident_bf[:, :], W("const", "ident")).then_inc(s.dve_done, 1)
        dve.wait_ge(s.dve_done, 1)
        dve.sem_inc(s.dve_done, -1)
        nc.vector.memset(ones_bf[:, :], 1.0).then_inc(s.dve_done, 1)
        dve.wait_ge(s.dve_done, 1)
        dve.sem_inc(s.dve_done, -1)
        dve.sem_inc(s.film_free, 2)
        nc.vector.tensor_copy(causal_bf[:, :], W("const", "causal")).then_inc(s.dve_done, 1)
        dve.wait_ge(s.dve_done, 1)
        dve.sem_inc(s.dve_done, -1)
        dve.sem_inc(s.start_act, 1)
        dve.sem_inc(s.w_cross_free, 1)
        dve.sem_inc(ctx_free[0], 1)
        dve.sem_inc(ctx_free[1], 1)
        dve.sem_inc(s.stage_pe, 1)
        stages(layernorm, self_attention, cross_attention, feed_forward, film_block)
        dve.sem_inc(s.x_final, 1)

    @block.tensor
    def _(pe):
        mm = nc.tensor.matmul
        ident = W("const", "ident")

        def layernorm(src, eps=0, affine=None, add=False):
            pe.wait_ge(s.stage_pe, 1)
            pe.sem_inc(s.stage_pe, -1)
            for g in range(NG):
                mm(bank(g), W("const", "mean"), group(src, g), start=True, stop=True).then_inc(s.mean, 1)
            for g in range(NG):
                pe.wait_ge(s.squared, 1)
                pe.sem_inc(s.squared, -1)
                for j in range(GB):
                    ins = mm(bank(4 + g, 1, S, j), squares[:, GB * g + j, :], W("const", "mean")[:, 0:1], start=True, stop=True)
                ins.then_inc(s.variance, 1)
            for g in range(NG):
                pe.wait_ge(s.inverse_ready, 1)
                pe.sem_inc(s.inverse_ready, -1)
                mm(bank(g), W("const", "ones")[0:S, :], group(deviation, g)[0:S], start=True, stop=True).then_inc(s.inverse_spread, 1)

        def self_attention(n):
            cfg = SELF[SA[n]]
            nsm, vw, wst = cfg["nsm"], cfg["vw"], SA[n]
            pe.wait_ge(s.stage_pe, 1)
            pe.sem_inc(s.stage_pe, -1)
            if cfg.get("quant"):
                pe.wait_ge(s.magnitudes, 1)
                pe.sem_inc(s.magnitudes, -1)
                mm(ps[:, 0, 0:3], W("const", "ones"), col[:, 0:3], start=True, stop=True).then_inc(s.totals, 1)
            pe.wait_ge(s.stage_pe, 1)
            pe.sem_inc(s.stage_pe, -1)
            wqk, wv, wo = W(wst, "wqk"), W(wst, "wv"), W(wst, "wo")
            N = GB * nsm * 2

            def scores(k):
                b, sm, half = k // (2 * nsm), k // 2 % nsm, k % 2
                for c in range(2):
                    if cfg["causal"]:
                        mm(bank(2 * (k % 2) + c, GT, S), ident_bf[0:S, 0:S], causal_bf[:, :], start=True, stop=False)
                    h = HEADS * sm + 8 * half + 4 * c
                    last = mm(bank(2 * (k % 2) + c, GT, S), qk[:, 2 * sm, b * S:b * S + S], km[:, h:h + 4, b * S:b * S + S],
                              start=not cfg["causal"], stop=True)
                last.then_inc(s.scores, 1)

            def turn(k):
                pe.wait_ge(s.probs_ready, 1)
                pe.sem_inc(s.probs_ready, -1)
                for c in range(2):
                    for j in range(4):
                        at = c * GT + j * S
                        last = nc.tensor.transpose(bank(4 + c, S, S, j * S), probs[:, k % 2, at:at + S], ident[0:S, 0:S])
                    last.then_inc(s.turned, 1)

            def values(k):
                b, half = k // (2 * nsm), k % 2
                if half == 0:
                    pe.wait_ge(s.o_free, 1)
                    pe.sem_inc(s.o_free, -1)
                for c in range(2):
                    pe.wait_ge(s.probsT_ready, 1)
                    pe.sem_inc(s.probsT_ready, -1)
                    for j in range(4):
                        h = 8 * half + 4 * c + j
                        last = mm(bank(7, vw + 1, S, h * (vw + 1)), probsT[:, k % 2, c * GT + j * S:c * GT + j * S + S],
                                  vaug[:, b, h * (vw + 1):(h + 1) * (vw + 1)], start=True, stop=True)
                if half == 1:
                    last.then_inc(s.o_full, 1)

            with pe.Fori(0, NG) as g:
                pe.wait_ge(s.xg_ready, 1)
                pe.sem_inc(s.xg_ready, -1)
                for m in range(2 * nsm):
                    pe.wait_ge(proj_bank_free[m % 2], 1)
                    pe.sem_inc(proj_bank_free[m % 2], -1)
                    mm(bank(6 - m % 2), wqk[:, m * 128:m * 128 + 128], xg[:, :], start=True, stop=True).then_inc(s.proj_full, 1)
                    if cfg.get("unit"):
                        if m == 0:
                            pe.wait_ge(s.o_free, 1)
                            pe.sem_inc(s.o_free, -1)
                        pe.wait_ge(s.head_sq, 1)
                        pe.sem_inc(s.head_sq, -1)
                        mm(bank(7), W("const", "head_rows"), group(squares, 0), start=True, stop=True).then_inc(s.head_norm, 1)
                        pe.wait_ge(s.qk_ready, 1)
                        pe.sem_inc(s.qk_ready, -1)
                        if m == 1:
                            pe.sem_inc(s.o_free, 1)
                for b in range(GB):
                    pe.wait_ge(proj_bank_free[b % 2], 1)
                    pe.sem_inc(proj_bank_free[b % 2], -1)
                    vc = wv.shape[1]
                    if cfg["bias"]:
                        mm(bank(6 - b % 2, vc, S), W("const", "ones")[0:1, 0:S], W(wst, "bv"), start=True, stop=False)
                    mm(bank(6 - b % 2, vc, S), xg[:, b * S:b * S + S], wv, start=not cfg["bias"], stop=True).then_inc(s.proj_full, 1)
                for b in range(GB):
                    pe.wait_ge(s.v_ready, 1)
                    pe.sem_inc(s.v_ready, -1)
                pe.wait_ge(s.km_act, nsm)
                pe.sem_inc(s.km_act, -nsm)
                pe.wait_ge(s.km_dve, nsm)
                pe.sem_inc(s.km_dve, -nsm)
                pe.wait_ge(s.km_pool, nsm)
                pe.sem_inc(s.km_pool, -nsm)
                scores(0)
                scores(1)
                for k in range(N + 1):
                    if k > 0:
                        values(k - 1)
                    if k < N:
                        turn(k)
                    if k + 2 < N:
                        scores(k + 2)
                pe.wait_ge(s.y_ready, 1)
                pe.sem_inc(s.y_ready, -1)
                for c in range(vw // 8):
                    pe.wait_ge(s.proj_free, 1)
                    pe.sem_inc(s.proj_free, -1)
                    for b in range(GB):
                        last = nc.tensor.transpose(bank(6, S, 128, b * S), y_tok[:, b, 128 * c:128 * c + 128], ident[0:S, 0:S])
                    last.then_inc(s.y_turned, 1)
                pe.wait_ge(s.o_free, 1)
                pe.sem_inc(s.o_free, -1)
                for c in range(vw // 8):
                    pe.wait_ge(s.y_feat_ready, 1)
                    pe.sem_inc(s.y_feat_ready, -1)
                    last = mm(bank(7), wo[:, 128 * c:128 * c + 128], y_feat[:, c, :], start=c == 0, stop=c == vw // 8 - 1)
                last.then_inc(s.out_full, 1)

        def cross_attention(n):
            cfg = CROSS[CA[n]]
            H, hd, wst = cfg["H"], cfg["hd"], CA[n]
            nU, w = -(-H // 4), min(H, 4)
            parts = where[wst]
            pe.wait_ge(s.stage_pe, 1)
            pe.sem_inc(s.stage_pe, -1)
            pe.wait_ge(s.stage_pe, 1)
            pe.sem_inc(s.stage_pe, -1)
            folds = [0]

            def fold(cols, rows, lhsT, rhs):
                pe.wait_ge(s.side_free, 1)
                pe.sem_inc(s.side_free, -1)
                mm(bank(6 + folds[0] % 2, cols, rows), lhsT, rhs, start=True, stop=True).then_inc(s.side_full, 1)
                folds[0] += 1

            for h in range(H):
                wk = W(wst, "wk")[:, h * QR:h * QR + QR]
                wq = W(wst, "wq")[:, h * 128:h * 128 + 128]
                fold(QR, 128, wq, wk)
                if "bq" in parts:
                    fold(1, QR, wk, W(wst, "bq")[:, h:h + 1])
                if "wo" in parts:
                    fold(128, C + 1, W(wst, "wv")[:, h * 97:h * 97 + 97], W(wst, "wo")[:, h * 128:h * 128 + 128])
            pe.wait_ge(s.stage_pe, 1)
            pe.sem_inc(s.stage_pe, -1)
            count = [0]

            def side(kind, arg, b, par):
                if kind in ("recips", "q_round", "q_low"):
                    return
                if (kind, arg) == ("maxima", 1):
                    return
                k = 6 + count[0] % 2
                count[0] += 1
                if kind == "maxima":
                    pe.wait_ge(s.maxima_ready, 1)
                    pe.sem_inc(s.maxima_ready, -1)
                if kind == "project":
                    pe.wait_ge(s.u_ready, nU)
                    pe.sem_inc(s.u_ready, -nU)
                if kind == "chunk" and arg == (0, 0):
                    pe.wait_ge(s.ctx_bf, 1)
                    pe.sem_inc(s.ctx_bf, -1)
                if kind == "chunk" and arg[0] % 4 == 0 and arg[1] == 0:
                    pe.wait_ge(s.q_bf, 1)
                    pe.sem_inc(s.q_bf, -1)
                pe.wait_ge(s.side_free, 1)
                pe.sem_inc(s.side_free, -1)
                if kind == "spread" and H > 1:
                    if arg == 0:
                        pe.wait_ge(s.rexp_ready, 1)
                        pe.sem_inc(s.rexp_ready, -1)
                    ins = mm(bank(k, w * S, C + 1), W("const", "ones")[0:H, 0:C + 1], rexp[:, 4 * arg:4 * arg + w, :], start=True, stop=True)
                elif kind == "spread":
                    g = arg
                    ins = mm(bank(k, w * S, C + 1), W("const", "row96"), u_raw[:, 4 * g:4 * g + w, :], start=True, stop=True)
                elif kind == "project":
                    for h in range(H):
                        ins = mm(bank(k, S), vfold[:, h * 128:h * 128 + 128], u_rec[:, h, :], start=h == 0, stop=h == H - 1)
                elif kind == "query":
                    for j in range(w):
                        h = 4 * arg + j
                        ins = mm(bank(k, S, QR, j * S), wfold[:, h * QR:h * QR + QR], xn[:, bass.ds(b + 1, 1), :], start=True, stop=True)
                elif kind == "chunk":
                    h, c = arg
                    a, z = CHUNKS[c]
                    ins = mm(bank(k, z - a, S), qa_bf[:, h, :], ctxT_bf[:, a:z], start=True, stop=True)
                else:
                    ins = nc.tensor.transpose(bank(k, S, C + HEADS), mrows[:, :], ident[0:S, 0:S])
                ins.then_inc(s.side_full, 1)

            def batch(b, par, prep, tail, main=True, first=False):
                us = units(H) if main else []
                at = side_places(H, prep, tail, main)

                def scoresT(u, par=par):
                    if u == 0:
                        pe.wait_ge(s.qa_ready, 1)
                        pe.sem_inc(s.qa_ready, -1)
                        if H > 1:
                            pe.wait_ge(s.ctx_split, 1)
                            pe.sem_inc(s.ctx_split, -1)
                    for t, pc, h0, nh, g in us[u]:
                        r = key_rows_of(t)
                        if H > 1:
                            o, keys = bank(u % 2, nh * S, r, pc), slice(128 * t, 128 * t + r)
                            hi, q = ctxT_hi[par][:, keys], qa_hi[par][:, h0:h0 + nh, :]
                            mm(o, hi, q, start=True, stop=False)
                            mm(o, hi, qa_lo[par][:, h0:h0 + nh, :], start=False, stop=False)
                            ins = mm(o, ctxT_lo[par][:, keys], q, start=False, stop=True)
                            continue
                        ins = mm(bank(u % 2, nh * S, r, pc), ctxT[par][:, 128 * t:128 * t + r], qa[par][:, 0, :],
                                 start=True, stop=True)
                    ins.then_inc(s.scoresT, 1)

                def values(u):
                    if H == 1:
                        pe.wait_ge(s.pexp_ready, 1)
                        pe.sem_inc(s.pexp_ready, -1)
                    for t, pc, h0, nh, g in us[u]:
                        r = key_rows_of(t)
                        if t == 0 and not first:
                            pe.wait_ge(s.u_raw_free if H > 1 else s.u_raw_ready, 1)
                            pe.sem_inc(s.u_raw_free if H > 1 else s.u_raw_ready, -1)
                        o = bank(2 + g, nh * S, C + 1)
                        if H > 1:
                            pe.wait_ge(s.pexp_hi_there, 1)
                            pe.sem_inc(s.pexp_hi_there, -1)
                            hi = pexp_hi[u % 3][0:r, :]
                            mm(o, ctxk_hi[par][0:r, t, :], hi, start=t == 0, stop=False, skip_group_check=True)
                            mm(o, ctxk_lo[par][0:r, t, :], hi, start=False, stop=False, skip_group_check=True)
                            continue
                        ins = mm(o, ctxk[par][0:r, t, :], pexp[u % 3][0:r, pc:pc + nh * S],
                                 start=t == 0, stop=t == KT - 1, skip_group_check=True)
                        if t == KT - 1:
                            ins.then_inc(s.u_full, 1)

                def values_lo(u):
                    pe.wait_ge(s.pexp_lo_ready, 1)
                    pe.sem_inc(s.pexp_lo_ready, -1)
                    t, pc, h0, nh, g = us[u][0]
                    r = key_rows_of(t)
                    ins = mm(bank(2 + g, nh * S, C + 1), ctxk_hi[par][0:r, t, :], pexp_lo[u % 3][0:r, :],
                             start=False, stop=t == KT - 1, skip_group_check=True)
                    if t == KT - 1:
                        ins.then_inc(s.u_full, 1)

                if main:
                    if first or H == 1:
                        scoresT(0)
                        scoresT(1)
                else:
                    if not prep:
                        pe.wait_ge(s.u_raw_free if H > 1 else s.u_raw_ready, nU)
                        pe.sem_inc(s.u_raw_free if H > 1 else s.u_raw_ready, -nU)
                for u in range(len(us)):
                    values(u)
                    if u + 2 < len(us):
                        scoresT(u + 2)
                    elif H > 1 and prep:
                        scoresT(u + 2 - len(us), 1 - par)
                    if H > 1:
                        values_lo(u)
                    for it in at.get(u, []):
                        side(*it, b, par)
                for p in sorted(at):
                    if p >= len(us):
                        for it in at[p]:
                            side(*it, b, par)

            batch(-1, 1, True, False, main=False)
            batch(0, 0, True, False, first=True)
            with pe.Fori(0, B // 2 - 1) as i:
                batch(2 * i + 1, 1, True, True)
                batch(2 * i + 2, 0, True, True)
            batch(B - 1, 1, False, True)
            batch(B, 0, False, True, main=False)

        def film_block(layernorm, feed_forward):
            layernorm(x)
            pe.wait_ge(s.stage_pe, 1)
            pe.sem_inc(s.stage_pe, -1)
            pe.wait_ge(s.stage_pe, 1)
            pe.sem_inc(s.stage_pe, -1)
            for h in range(TH):
                pe.wait_ge(s.side_free, 1)
                pe.sem_inc(s.side_free, -1)
                mm(bank(6 + h % 2, C), W("tk", "wq")[:, h * 128:h * 128 + 128], W("tk", "wk")[:, h * C:h * C + C],
                   start=True, stop=True).then_inc(s.side_full, 1)
            pe.wait_ge(s.stage_pe, 1)
            pe.sem_inc(s.stage_pe, -1)

            def queries(b):
                pe.wait_ge(s.proj_free, 1)
                pe.sem_inc(s.proj_free, -1)
                for h in range(TH):
                    ins = mm(bank(6, S, C, h * S), wf4[:, h * C:h * C + C], xn[:, bass.ds(b, 1), :], start=True, stop=True)
                ins.then_inc(s.proj_full, 1)
                pe.wait_ge(s.qv_ready, 1)
                pe.sem_inc(s.qv_ready, -1)
                pe.wait_ge(s.mask_ready, 1)
                pe.sem_inc(s.mask_ready, -1)

            def scores(h, par):
                pe.wait_ge(s.row_scores_free, 1)
                pe.sem_inc(s.row_scores_free, -1)
                for c, (a, z) in enumerate(CHUNKS):
                    to = bank(3 * (h % 2) + c, z - a, S)
                    mm(to, ones_bf[:, 0:S], mask_bf[par][:, a:z], start=True, stop=False)
                    ins = mm(to, qv[:, h, :], ctxT[par][0:C, a:z], start=False, stop=True)
                ins.then_inc(s.row_scores, 1)

            def mean(par):
                pe.wait_ge(s.kept_ready, TH)
                pe.sem_inc(s.kept_ready, -TH)
                for u in range(KT // 4):
                    pe.wait_ge(s.proj_free, 1)
                    pe.sem_inc(s.proj_free, -1)
                    for t in range(4 * u, 4 * u + 4):
                        r = key_rows_of(t)
                        for h in range(TH):
                            ins = mm(bank(6, S, r, t % 4 * S), kept[:, h, 128 * t:128 * t + r], turn_scale[:, h, :],
                                     start=h == 0, stop=h == TH - 1)
                    ins.then_inc(s.proj_full, 1)
                pe.wait_ge(s.mean_ready, KT // 4)
                pe.sem_inc(s.mean_ready, -(KT // 4))
                pe.wait_ge(s.proj_free, 1)
                pe.sem_inc(s.proj_free, -1)
                for t in range(KT):
                    r = key_rows_of(t)
                    ins = mm(bank(6, S, C), ctxk[par][0:r, t, 0:C], meanT[0:r, t, :], start=t == 0, stop=t == KT - 1)
                ins.then_inc(s.proj_full, 1)
                pe.wait_ge(s.uv_ready, 1)
                pe.sem_inc(s.uv_ready, -1)
                pe.wait_ge(s.proj_free, 1)
                pe.sem_inc(s.proj_free, -1)
                mm(bank(6, S), W("tk", "wv"), uv, start=True, stop=True).then_inc(s.proj_full, 1)

            def batch(b, par, last=False):
                scores(2, par)
                scores(3, par)
                if not last:
                    queries(b + 1)
                    scores(0, 1 - par)
                    scores(1, 1 - par)
                mean(par)
            queries(0)
            scores(0, 0)
            scores(1, 0)
            batch(0, 0)
            with pe.Fori(0, B // 2 - 1) as i:
                batch(2 * i + 1, 1)
                batch(2 * i + 2, 0)
            batch(B - 1, 1, last=True)
            layernorm(mid)
            pe.wait_ge(s.stage_pe, 1)
            pe.sem_inc(s.stage_pe, -1)
            modulate("film_in")
            modulate("film_out")
            layernorm(mid)
            feed_forward(3)
            layernorm(xn)

        def modulate(name):
            for g in range(NG):
                pe.wait_ge(s.film_free, 1)
                pe.sem_inc(s.film_free, -1)
                for c in range(2):
                    ins = mm(bank(2 * (g % 2) + c), W("tk", name)[:, 128 * c:128 * c + 128], group(ct, g), start=True, stop=True)
                ins.then_inc(s.film_full, 1)

        def feed_forward(n):
            cfg = FEED[FF[n]]
            w = FF[n]
            pe.wait_ge(s.stage_pe, 1)
            pe.sem_inc(s.stage_pe, -1)
            pe.wait_ge(s.stage_pe, 1)
            pe.sem_inc(s.stage_pe, -1)
            if cfg["gate"]:
                E = cfg["E"]
                for b in range(B):
                    to = bank(0, E, S, b * E)
                    if "gate_b" in where[w]:
                        mm(to, W("const", "ones")[0:1, 0:S], W(w, "gate_b"), start=True, stop=False)
                    ins = mm(to, xn[:, b, :], W(w, "gate"), start="gate_b" not in where[w], stop=True)
                ins.then_inc(s.logits_ready, 1)
                pe.wait_ge(s.weights_ready, 1)
                pe.sem_inc(s.weights_ready, -1)
                for b in range(B):
                    ins = nc.tensor.transpose(bank(b // GB, S, E, b % GB * S), weight[:, b, 0:E], ident[0:S, 0:S])
                    if b % GB == GB - 1:
                        ins.then_inc(s.gates_turned, 1)
                pe.wait_ge(s.gates_there, 1)
                pe.sem_inc(s.gates_there, -1)
            for g in range(NG):
                if n == 1:
                    mm(bank(4 + g), W(w, "b2"), gateT[0:16, g * GT:g * GT + GT], start=True, stop=False)
                    mm(bank(4 + g), W(w, "sb2"), W("const", "ones_row"), start=False, stop=False)
                elif "b2" in where[w]:
                    mm(bank(4 + g), W(w, "b2"), W("const", "ones_row"), start=True, stop=False)
                else:
                    mm(bank(4 + g), W("const", "zeros")[0:1, :], W("const", "ones_row"), start=True, stop=False)

            def up(c, g, k):
                if g == 0:
                    pe.wait_ge(chunk_loaded[c], 16)
                    pe.sem_inc(chunk_loaded[c], -16)
                ins = mm(bank(k), chunk[c][:, 0:128], group(xn, g), start=True, stop=True)
                if cfg["up2"]:
                    ins = mm(bank(2 + k), chunk[c][:, 128:256], group(xn, g), start=True, stop=True)
                ins.then_inc(s.up_done, 1)

            def down(c, g, k, last):
                pe.wait_ge(s.h_ready, 1)
                pe.sem_inc(s.h_ready, -1)
                ins = mm(bank(4 + g), chunk[c][:, 256:384], h_all[k], start=False, stop=last)
                if g == NG - 1:
                    ins.then_inc(chunk_free[c], 1)
                if last and g < NG - 1:
                    ins.then_inc(s.down_done, 1)
                if last and g == NG - 1:
                    nc.tensor.drain().then_inc(s.down_done, 1)

            def block(chunks, more):
                us = [(c, g) for c in chunks for g in range(NG)]
                for u, (c, g) in enumerate(us):
                    down(c, g, u % 2, not more and c == chunks[-1])
                    if u + 2 < len(us):
                        up(*us[u + 2], u % 2)
                    elif more:
                        up(0, u + 2 - len(us), u % 2)
            up(0, 0, 0)
            up(0, 1, 1)
            if cfg["loop"]:
                with pe.Fori(0, cfg["loop"]) as i:
                    block(range(4), True)
            block(range(cfg["last"]), False)

        pe.wait_ge(loaded["const"], 16)
        for c in range(4):
            pe.sem_inc(chunk_free[c], 1)
        stages(layernorm, self_attention, cross_attention, feed_forward, film_block)
        pe.wait_ge(s.stage_pe, 1)
        pe.sem_inc(s.stage_pe, -1)

    ctx.close()


def kernel(**inputs):
    import concourse.bacc as bacc
    from concourse.bass_utils import run_bass_kernel_spmd

    p = {k: np.asarray(v) for k, v in inputs.items()}
    arrays, where = {}, {}
    parts = {"const": constants(), "sa0": self_parts(0, p), "ca0": cross_parts(0, p), "sa1": self_parts(1, p),
             "ca1": cross_parts(1, p), "sa2": self_parts(2, p), "ca2": cross_parts(2, p), "sa3": self_parts(3, p),
             "tk": film_parts(p)}
    for n, name in zip((0, 1, 2, "g", 3), FEED):
        arrays[name + "_chunks"], parts[name] = feed_parts(n, p)
    for name, value in parts.items():
        arrays[name], where[name] = pack(value)
    arrays["x"] = np.ascontiguousarray(p["x"].transpose(2, 0, 1))
    arrays["text_mask"] = np.ascontiguousarray(p["mask_BxS_bf1"]).view(np.uint8).reshape(1, -1)
    arrays["ctx_mask"] = np.ascontiguousarray(p["mask_BxS2_bf1"]).view(np.uint8)
    arrays["ctx"] = np.ascontiguousarray(p["ctx_768"])
    arrays["ctxT"] = np.ascontiguousarray(p["ctx_768"].transpose(0, 2, 1))
    nc = bacc.Bacc("TRN2", target_bir_lowering=False, num_devices=1)
    dram = {k: nc.dram_tensor("in_" + k, a.shape, mybir.dt.from_np(a.dtype), kind="ExternalInput").ap() for k, a in arrays.items()}
    out = nc.dram_tensor("out", (D, B, S), F32, kind="ExternalOutput").ap()
    build(nc, dram, where, out)
    r = run_bass_kernel_spmd(nc, [{"in_" + k: a for k, a in arrays.items()}], core_ids=[0])
    return np.ascontiguousarray(r.results[0]["out"].transpose(1, 2, 0))
```
